# Optimizing a Trainium2 kernel written in Bass

```python
import numpy as np
import jax
import jax.numpy as jnp

def _softmax(x, axis=-1):
    return jax.nn.softmax(x, axis=axis)
def _gelu(x):
    return jax.nn.gelu(x, approximate=True)
def _silu(x):
    return jax.nn.silu(x)
def _sigmoid(x):
    return jax.nn.sigmoid(x)
def _layernorm(x, axis=-1, eps=1e-5):
    m = jnp.mean(x, axis=axis, keepdims=True)
    v = jnp.var(x, axis=axis, keepdims=True)
    return (x - m) / jnp.sqrt(v + eps)
def _scatter_add(tgt, idx, src, axis=0):
    return tgt.at[idx].add(src)
def _segment_sum(src, seg, n):
    return jax.ops.segment_sum(src, seg, n)

kernel_name = 'mk_conv_attn_hybrid_d2_conv_nchw384_987a26'

def setup_inputs(seed: int = 0):
    np.random.seed(seed)
    _w = jnp.asarray
    def _rec_inputs():
        import jax
        import jax.numpy as jnp
        _gk = jax.random.key(seed)
        x = -0.001003 + 1 * jax.random.normal(jax.random.fold_in(_gk, 1), (4, 384, 32, 32), jnp.float32)
        return x
    x = _rec_inputs()
    def _L0_conv_setup():
        import jax, jax.numpy as jnp
        import numpy as np
        HEADS = 8
        MAXD = 7
        SPAN = 2 * MAXD + 1
        L = SPAN * SPAN

        def _rel_idx(h, w):
            yy, xx = jnp.meshgrid(jnp.arange(h), jnp.arange(w), indexing='ij')
            y = yy.reshape(-1)
            x = xx.reshape(-1)
            dy = jnp.clip(y[:, None] - y[None, :], -MAXD, MAXD)
            dx = jnp.clip(x[:, None] - x[None, :], -MAXD, MAXD)
            return ((dy + MAXD) * SPAN + (dx + MAXD)).astype(jnp.int32)
        key = jax.random.key(seed)
        ks = jax.random.split(key, 7)
        B, C, H, W = (4, 384, 32, 32)
        hd = C // HEADS
        s = 0.02
        return {'x': jax.random.normal(ks[0], (B, C, H, W), jnp.float32), 'w_qkv': jax.random.normal(ks[1], (C, 3 * C), jnp.float32) * s, 'w_proj': jax.random.normal(ks[2], (C, C), jnp.float32) * s, 'b_proj': jax.random.normal(ks[3], (C,), jnp.float32) * s, 'table_q': jax.random.normal(ks[4], (HEADS, L, hd), jnp.float32) * s, 'table_k': jax.random.normal(ks[5], (HEADS, L, hd), jnp.float32) * s, 'table_v': jax.random.normal(ks[6], (HEADS, L, hd), jnp.float32) * s}
    _L0_conv_all = _L0_conv_setup()
    _L0_conv_in = {k: v for k, v in _L0_conv_all.items() if k in ('w_qkv', 'w_proj', 'b_proj', 'table_q', 'table_k', 'table_v', )}
    del _L0_conv_all

    def _L1_attn_setup():
        import jax, jax.numpy as jnp
        import numpy as np
        HEADS = 8
        WINDOW = 64
        BLOCK = 256
        key = jax.random.key(seed)
        ks = jax.random.split(key, 6)
        C = 384
        inp = {'x': jax.random.normal(ks[0], (256, 256, C), jnp.float32), 'mem': jax.random.normal(ks[1], (64, C), jnp.float32), 'qkv_w': jax.random.normal(ks[2], (C, 3 * C), jnp.float32) * 0.02, 'qkv_b': jax.random.normal(ks[3], (3 * C,), jnp.float32) * 0.02, 'proj_w': jax.random.normal(ks[4], (C, C), jnp.float32) * 0.02, 'proj_b': jax.random.normal(ks[5], (C,), jnp.float32) * 0.02}
        return inp
    _L1_attn_all = _L1_attn_setup()
    _L1_attn_in = {k: v for k, v in _L1_attn_all.items() if k in ('mem', 'qkv_w', 'qkv_b', 'proj_w', 'proj_b', )}
    del _L1_attn_all

    def _L1_ffn_setup():
        import jax, jax.numpy as jnp
        import numpy as np
        NUM_EXPERTS = 4
        TOP_K = 2
        DIM = 384
        HID = 4 * DIM
        key = jax.random.key(seed)
        ks = jax.random.split(key, 5)
        B, S = (16, 2048)
        scale_in = 1.0 / np.sqrt(DIM)
        scale_hid = 1.0 / np.sqrt(HID)
        return {'x': jax.random.normal(ks[0], (B, S, DIM), dtype=jnp.float32), 'gate_w': jax.random.normal(ks[1], (DIM, NUM_EXPERTS), dtype=jnp.float32) * scale_in, 'gate_b': jnp.zeros((NUM_EXPERTS,), dtype=jnp.float32), 'w1': jax.random.normal(ks[2], (NUM_EXPERTS, DIM, HID), dtype=jnp.float32) * scale_in, 'b1': jnp.zeros((NUM_EXPERTS, HID), dtype=jnp.float32), 'w2': jax.random.normal(ks[3], (NUM_EXPERTS, HID, DIM), dtype=jnp.float32) * scale_hid, 'b2': jnp.zeros((NUM_EXPERTS, DIM), dtype=jnp.float32)}
    _L1_ffn_all = _L1_ffn_setup()
    _L1_ffn_in = {k: v for k, v in _L1_ffn_all.items() if k in ('gate_w', 'gate_b', 'w1', 'b1', 'w2', 'b2', )}
    del _L1_ffn_all

    return {
        "x": x,
        "L0_conv_w_qkv": _L0_conv_in["w_qkv"],
        "L0_conv_w_proj": _L0_conv_in["w_proj"],
        "L0_conv_b_proj": _L0_conv_in["b_proj"],
        "L0_conv_table_q": _L0_conv_in["table_q"],
        "L0_conv_table_k": _L0_conv_in["table_k"],
        "L0_conv_table_v": _L0_conv_in["table_v"],
        "L1_attn_mem": _L1_attn_in["mem"],
        "L1_attn_qkv_w": _L1_attn_in["qkv_w"],
        "L1_attn_qkv_b": _L1_attn_in["qkv_b"],
        "L1_attn_proj_w": _L1_attn_in["proj_w"],
        "L1_attn_proj_b": _L1_attn_in["proj_b"],
        "L1_ffn_gate_w": _L1_ffn_in["gate_w"],
        "L1_ffn_gate_b": _L1_ffn_in["gate_b"],
        "L1_ffn_w1": _L1_ffn_in["w1"],
        "L1_ffn_b1": _L1_ffn_in["b1"],
        "L1_ffn_w2": _L1_ffn_in["w2"],
        "L1_ffn_b2": _L1_ffn_in["b2"],
    }

def reference(x, L0_conv_w_qkv, L0_conv_w_proj, L0_conv_b_proj, L0_conv_table_q, L0_conv_table_k, L0_conv_table_v, L1_attn_mem, L1_attn_qkv_w, L1_attn_qkv_b, L1_attn_proj_w, L1_attn_proj_b, L1_ffn_gate_w, L1_ffn_gate_b, L1_ffn_w1, L1_ffn_b1, L1_ffn_w2, L1_ffn_b2):
    import jax
    import jax.numpy as jnp
    def _L0_conv_ref(x, w_qkv, w_proj, b_proj, table_q, table_k, table_v):
        import jax, jax.numpy as jnp
        import numpy as np
        HEADS = 8
        MAXD = 7
        SPAN = 2 * MAXD + 1
        L = SPAN * SPAN

        def _rel_idx(h, w):
            yy, xx = jnp.meshgrid(jnp.arange(h), jnp.arange(w), indexing='ij')
            y = yy.reshape(-1)
            x = xx.reshape(-1)
            dy = jnp.clip(y[:, None] - y[None, :], -MAXD, MAXD)
            dx = jnp.clip(x[:, None] - x[None, :], -MAXD, MAXD)
            return ((dy + MAXD) * SPAN + (dx + MAXD)).astype(jnp.int32)
        b, c, h, w = x.shape
        n = h * w
        hd = c // HEADS
        scale = hd ** (-0.5)
        idx = _rel_idx(h, w)
        xt = x.reshape(b, c, n).transpose(0, 2, 1)
        qkv = (xt @ w_qkv).reshape(b, n, 3, HEADS, hd).transpose(2, 0, 3, 1, 4)
        q = qkv[0] * scale
        k = qkv[1]
        v = qkv[2]
        attn = jnp.einsum('bhid,bhjd->bhij', q, k)
        sk = jnp.einsum('bhid,hLd->bhiL', q, table_k)
        attn = attn + jnp.take_along_axis(sk, idx[None, None], axis=-1)
        sq = jnp.einsum('bhjd,hLd->bhjL', k * scale, table_q)
        attn = attn + jnp.take_along_axis(sq, idx[None, None], axis=-1).transpose(0, 1, 3, 2)
        attn = jax.nn.softmax(attn, axis=-1)
        out = jnp.einsum('bhij,bhjd->bhid', attn, v)
        wsum = jnp.zeros((b, HEADS, n, L), attn.dtype)
        wsum = wsum.at[:, :, jnp.arange(n)[:, None], idx].add(attn)
        out = out + jnp.einsum('bhiL,hLd->bhid', wsum, table_v)
        out = out.transpose(0, 2, 1, 3).reshape(b, n, c)
        out = out @ w_proj + b_proj
        return out.transpose(0, 2, 1).reshape(b, c, h, w)

    def _L1_attn_ref(x, mem, qkv_w, qkv_b, proj_w, proj_b):
        import jax, jax.numpy as jnp
        import numpy as np
        HEADS = 8
        WINDOW = 64
        BLOCK = 256
        B, T, C = x.shape
        H = HEADS
        hd = C // H
        scale = hd ** (-0.5)
        qkv = x @ qkv_w + qkv_b
        q, k, v = jnp.split(qkv, 3, axis=-1)
        M = mem.shape[0]
        m = jnp.broadcast_to(mem[None], (B, M, C))
        k = jnp.concatenate([m, k], axis=1)
        v = jnp.concatenate([m, v], axis=1)

        def heads(t):
            return t.reshape(B, -1, H, hd).transpose(0, 2, 1, 3)
        q, k, v = (heads(q), heads(k), heads(v))
        att = jnp.einsum('bhqd,bhkd->bhqk', q, k) * scale
        i = jnp.arange(T)[:, None]
        j = jnp.arange(T)[None, :]
        band = (j <= i) & (jnp.abs(i - j) <= WINDOW)
        full_mask = jnp.concatenate([jnp.ones((T, M), bool), band], axis=1)
        att = jnp.where(full_mask[None, None], att, -jnp.inf)
        p = jax.nn.softmax(att, axis=-1)
        y = jnp.einsum('bhqk,bhkd->bhqd', p, v)
        y = y.transpose(0, 2, 1, 3).reshape(B, T, C)
        return y @ proj_w + proj_b

    def _L1_ffn_ref(x, gate_w, gate_b, w1, b1, w2, b2):
        import jax, jax.numpy as jnp
        import numpy as np
        NUM_EXPERTS = 4
        TOP_K = 2
        DIM = 384
        HID = 4 * DIM
        scores = jnp.einsum('bsd,de->bse', x, gate_w) + gate_b
        probs = jax.nn.softmax(scores, axis=-1)
        topk_vals, topk_idx = jax.lax.top_k(probs, TOP_K)
        mask = jnp.sum(jax.nn.one_hot(topk_idx, NUM_EXPERTS, dtype=probs.dtype), axis=-2)
        masked = probs * mask
        masked = masked / (jnp.sum(masked, axis=-1, keepdims=True) + 1e-09)
        h = jax.nn.gelu(jnp.einsum('bsd,edh->ebsh', x, w1) + b1[:, None, None, :], approximate=False)
        y = jnp.einsum('ebsh,ehd->ebsd', h, w2) + b2[:, None, None, :]
        out = jnp.einsum('bse,ebsd->bsd', masked, y)
        return out

    def _gn(v, G=32, eps=1e-5):
        B_, C_, H_, W_ = v.shape
        g = v.reshape(B_, G, C_ // G, H_, W_)
        m = jnp.mean(g, axis=(2, 3, 4), keepdims=True)
        s = jnp.var(g, axis=(2, 3, 4), keepdims=True)
        return ((g - m) / jnp.sqrt(s + eps)).reshape(v.shape)

    def _ln_c(v, eps=1e-6):
        m = jnp.mean(v, axis=1, keepdims=True)
        s = jnp.var(v, axis=1, keepdims=True)
        return (v - m) / jnp.sqrt(s + eps)

    def _ln_t(v, eps=1e-5):
        m = jnp.mean(v, axis=-1, keepdims=True)
        s = jnp.var(v, axis=-1, keepdims=True)
        return (v - m) / jnp.sqrt(s + eps)

    def _to_tokens(v):
        B_, C_, H_, W_ = v.shape
        return v.reshape(B_, C_, H_ * W_).transpose(0, 2, 1)
    def _from_tokens(t, like):
        B_, C_, H_, W_ = like.shape
        return t.transpose(0, 2, 1).reshape(B_, C_, H_, W_)

    x = x + _L0_conv_ref(_gn(x), L0_conv_w_qkv, L0_conv_w_proj, L0_conv_b_proj, L0_conv_table_q, L0_conv_table_k, L0_conv_table_v)
    t = _to_tokens(x)
    t = t + _L1_attn_ref(_ln_t(t), L1_attn_mem, L1_attn_qkv_w, L1_attn_qkv_b, L1_attn_proj_w, L1_attn_proj_b)
    t = t + _L1_ffn_ref(_ln_t(t), L1_ffn_gate_w, L1_ffn_gate_b, L1_ffn_w1, L1_ffn_b1, L1_ffn_w2, L1_ffn_b2)
    x = _from_tokens(t, x)
    return x


_drawn_inputs = setup_inputs


def setup_inputs(seed=0):
    import zlib

    import numpy as np

    out = dict(_drawn_inputs(seed))
    spreads = {'L1_ffn_gate_b': (0.0, 0.1), 'L1_ffn_b1': (0.0, 0.1), 'L1_ffn_b2': (0.0, 0.1)}
    factors = {'L0_conv_w_qkv': 3.034,
     'L0_conv_w_proj': 4.326,
     'L0_conv_table_q': 8.0,
     'L0_conv_table_k': 8.0,
     'L0_conv_table_v': 7.528,
     'L1_attn_qkv_b': 8.0}
    for name, (base, spread) in spreads.items():
        noise = np.random.default_rng([zlib.crc32(name.encode()), seed]).standard_normal(out[name].shape)
        drawn = base * np.exp(spread * noise) if base else spread * noise
        out[name] = jnp.asarray(drawn.astype(out[name].dtype))
    for name, factor in factors.items():
        out[name] = (out[name] * factor).astype(out[name].dtype)
    return out
```

```python
from contextlib import ExitStack

import concourse.bass as bass
from concourse import mybir

F32 = mybir.dt.float32
ACT = mybir.ActivationFunctionType
ALU = mybir.AluOpType
AX_X = mybir.AxisListType.X

P = 128
B, C, HH, WW = 4, 384, 32, 32
N = HH * WW
T = B * N
CT = C // P
HEADS = 8
HD = C // HEADS
SPAN = 15
MAXD = 7
EXT = 2 * WW - 1
KP = 96
SCALE = float(HD) ** -0.5
BIG = 3.0e38
CH_ROWS = [4, 4, 4, 3]
NCH = len(CH_ROWS)
GROUP = 12
ROWF = WW
MEM = 64
WIN = 64
EXPERTS = 4
HID = 4 * C
HT = HID // P
MASKED = -1.0e30


class Scope:

    def __init__(self, nc):
        self.nc, self.ctx, self.sems = nc, ExitStack(), []

    def __enter__(self):
        return self

    def __exit__(self, *a):
        self.ctx.close()

    def sb(self, name, shape, dt=F32):
        return self.ctx.enter_context(self.nc.sbuf_tensor(name, shape, dt))

    def ps(self, name, shape, dt=F32):
        return self.ctx.enter_context(self.nc.psum_tensor(name, shape, dt))

    def sem(self, name):
        s = self.ctx.enter_context(self.nc.semaphore(name))
        self.sems.append(s)
        return s

    def clear(self):
        for s in self.sems:
            self.nc.gpsimd.sem_clear(s)
        self.nc.all_engine_barrier()


def norm_qkv(nc, x, w_qkv, tv, mhalf, qs, ks, vs, tve):
    with Scope(nc) as s:
        xc = s.sb("xc", [P, CT, B, N])
        w = s.sb("w0", [P, CT, 3 * C])
        grp = s.sb("grp", [P, P])
        stats = s.sb("stats", [P, CT, B, 2, 6])
        mv = s.sb("mv", [P, CT, B, 2])
        mean = s.sb("mean", [P, B])
        dev = s.sb("dev", [P, CT, B])
        var = s.sb("var", [P, CT, B])
        rstd = s.sb("rstd", [P, B])
        st = s.sb("st", [KP, 2, T])
        vst = s.sb("vst", [P, 2, 8, C])
        pg = s.ps("pg", [P, 2, 512])
        pq = s.ps("pq", [P, 4, 512])
        x_in = [s.sem(f"x_in{b}") for b in range(B)]
        w_in = s.sem("w_in")
        grp_step = s.sem("grp_step")
        stat_step = s.sem("stat_step")
        sums = s.sem("sums")
        normed = s.sem("normed")
        prod = s.sem("prod")
        copied_act = s.sem("copied_act")
        copied_dve = s.sem("copied_dve")
        stored = [s.sem(f"stored{i}") for i in range(2)]
        vstored = [s.sem(f"vstored{i}") for i in range(2)]
        ext_out = s.sem("ext_out")
        powed = s.sem("powed0")
        NB = T // 512
        PIECES = [(part, m) for part in range(2) for m in range(4)]
        NQK = len(PIECES) * NB
        NV = T // P

        with nc.Block() as block:
            @block.sync
            def _(sp):
                for b in range(B):
                    sp.dma_start(xc[:, :, b, :], x[b].rearrange("(p t) n -> p t n", t=CT)).then_inc(x_in[b], 16)
                sp.dma_start(w[:], w_qkv.rearrange("(p t) n -> p t n", t=CT)).then_inc(w_in, 16)
                lo = WW - 1 - MAXD
                for h in range(HEADS):
                    sp.dma_start(tve[h, :, lo:lo + SPAN, :], tv[h]).then_inc(ext_out, 16)
                    sp.dma_start(tve[h, :, 0:lo, :], tv[h, :, 0:1, :].broadcast_to([SPAN, lo, HD])).then_inc(ext_out, 16)
                    sp.dma_start(tve[h, :, lo + SPAN:EXT, :],
                                 tv[h, :, SPAN - 1:SPAN, :].broadcast_to([SPAN, EXT - lo - SPAN, HD])).then_inc(ext_out, 16)
                for i, (part, m) in enumerate(PIECES):
                    sp.wait_ge(copied_act, (i + 1) * NB // 2)
                    sp.wait_ge(copied_dve, (i + 1) * NB // 2)
                    dst = (qs if part == 0 else ks).rearrange("h d n -> (h d) n")
                    sp.dma_start(dst[m * KP:(m + 1) * KP, :], st[:, i % 2, :]).then_inc(stored[i % 2], 16)
                for i in range(NV // 8):
                    sp.wait_ge(copied_act, NQK // 2 + (i + 1) * 4)
                    sp.wait_ge(copied_dve, NQK // 2 + (i + 1) * 4)
                    sp.dma_start(vs[:, i * 8:(i + 1) * 8, :], vst[:, i % 2]).then_inc(vstored[i % 2], 16)
                for i in range(2):
                    sp.wait_ge(stored[i], 16 * len(PIECES) // 2)
                    sp.wait_ge(vstored[i], 16 * NV // 16)
                sp.wait_ge(ext_out, 16 * 3 * HEADS)

            @block.gpsimd
            def _(pool):
                pool.memset(grp[:], 1.0 / GROUP).then_inc(grp_step, 1)
                g3 = grp[:].rearrange("p (g r) -> p g r", r=4)
                pool.wait_ge(grp_step, 1)
                pool.affine_select(out=g3, in_=g3, compare_op=ALU.is_ge, fill=0.0, base=0,
                                   pattern=[[-4, 32], [0, 4]], channel_multiplier=1).then_inc(grp_step, 1)
                pool.wait_ge(grp_step, 2)
                pool.affine_select(out=g3, in_=g3, compare_op=ALU.is_ge, fill=0.0, base=3,
                                   pattern=[[4, 32], [0, 4]], channel_multiplier=-1).then_inc(grp_step, 1)
                pool.wait_ge(stat_step, 3 * CT * B + 5)
                pool.tensor_tensor(rstd[:], rstd[:], mhalf[:, 0:B], ALU.pow).then_inc(powed, 1)

            @block.vector
            def _(dve):
                n = 0
                for b in range(B):
                    dve.wait_ge(x_in[b], 16)
                    for t in range(CT):
                        for k in range(2):
                            dve.bn_stats(stats[:, t, b, k, :], xc[:, t, b, k * 512:(k + 1) * 512]).then_inc(stat_step, 1)
                            n += 1
                for b in range(B):
                    for t in range(CT):
                        dve.wait_ge(stat_step, 2 * CT * B)
                        dve.bn_aggr(mv[:, t, b, :], stats[:, t, b].rearrange("p k s -> p (k s)")).then_inc(stat_step, 1)
                        n += 1
                dve.wait_ge(sums, 1)
                dve.tensor_copy(mean[:], pg[:, 0, 0:B]).then_inc(stat_step, 1)
                n += 1
                dve.wait_ge(stat_step, n)
                dve.tensor_tensor(dev[:], mv[:, :, :, 0], mean[:].rearrange("p (o b) -> p o b", o=1).broadcast_to([P, CT, B]),
                                  ALU.subtract).then_inc(stat_step, 1)
                n += 1
                dve.wait_ge(stat_step, n)
                dve.tensor_tensor(dev[:], dev[:], dev[:], ALU.mult).then_inc(stat_step, 1)
                n += 1
                dve.wait_ge(stat_step, n)
                dve.tensor_tensor(var[:], mv[:, :, :, 1], dev[:], ALU.add).then_inc(stat_step, 1)
                n += 1
                dve.wait_ge(sums, 2)
                dve.tensor_scalar(rstd[:], pg[:, 1, 0:B], 1e-5, None, ALU.add).then_inc(stat_step, 1)
                dve.wait_ge(powed, 1)
                for b in range(B):
                    for t in range(CT):
                        dve.tensor_scalar(xc[:, t, b, :], xc[:, t, b, :], mean[:, b:b + 1], rstd[:, b:b + 1],
                                          ALU.subtract, ALU.mult).then_inc(normed, 1)
                for i, (part, m) in enumerate(PIECES):
                    for nb in range(1, NB, 2):
                        j = i * NB + nb
                        dve.wait_ge(prod, j + 1)
                        if i >= 2:
                            dve.wait_ge(stored[i % 2], 16 * (i // 2))
                        dve.tensor_scalar(st[:, i % 2, nb * 512:(nb + 1) * 512], pq[0:KP, j % 4, :],
                                          SCALE if part == 0 else 1.0, None, ALU.mult).then_inc(copied_dve, 1)
                for i in range(1, NV, 2):
                    dve.wait_ge(prod, NQK + i + 1)
                    if i >= 16:
                        dve.wait_ge(vstored[i // 8 % 2], 16 * (i // 16))
                    dve.tensor_copy(vst[:, i // 8 % 2, i % 8, :], pq[:, (NQK + i) % 4, 0:C]).then_inc(copied_dve, 1)

            @block.scalar
            def _(act):
                for i, (part, m) in enumerate(PIECES):
                    for nb in range(0, NB, 2):
                        j = i * NB + nb
                        act.wait_ge(prod, j + 1)
                        if i >= 2:
                            act.wait_ge(stored[i % 2], 16 * (i // 2))
                        act.activation(st[:, i % 2, nb * 512:(nb + 1) * 512], pq[0:KP, j % 4, :], ACT.Copy,
                                       scale=SCALE if part == 0 else 1.0).then_inc(copied_act, 1)
                for i in range(0, NV, 2):
                    act.wait_ge(prod, NQK + i + 1)
                    if i >= 16:
                        act.wait_ge(vstored[i // 8 % 2], 16 * (i // 16))
                    act.activation(vst[:, i // 8 % 2, i % 8, :], pq[:, (NQK + i) % 4, 0:C], ACT.Copy).then_inc(copied_act, 1)

            @block.tensor
            def _(pe):
                pe.wait_ge(grp_step, 3)
                pe.wait_ge(stat_step, 3 * CT * B)
                for t in range(CT):
                    mm = pe.matmul(pg[:, 0, 0:B], grp[:], mv[:, t, :, 0], start=(t == 0), stop=(t == CT - 1))
                mm.then_inc(sums, 1)
                pe.wait_ge(stat_step, 3 * CT * B + 4)
                for t in range(CT):
                    mm = pe.matmul(pg[:, 1, 0:B], grp[:], var[:, t, :], start=(t == 0), stop=(t == CT - 1))
                mm.then_inc(sums, 1)
                pe.wait_ge(w_in, 16)

                def free(j):
                    if j >= 4:
                        pe.wait_ge(copied_dve if j % 2 else copied_act, (j - 4) // 2 + 1)

                for i, (part, m) in enumerate(PIECES):
                    for nb in range(NB):
                        j = i * NB + nb
                        pe.wait_ge(normed, min(CT * (nb // 2 + 1), CT * B))
                        free(j)
                        for t in range(CT):
                            mm = pe.matmul(pq[0:KP, j % 4, :], w[:, t, part * C + m * KP:part * C + (m + 1) * KP],
                                           xc[:, t, nb // 2, nb % 2 * 512:nb % 2 * 512 + 512],
                                           start=(t == 0), stop=(t == CT - 1))
                        mm.then_inc(prod, 1)
                for i in range(NV):
                    free(NQK + i)
                    for t in range(CT):
                        mm = pe.matmul(pq[:, (NQK + i) % 4, 0:C], xc[:, t, i // 8, i % 8 * P:(i % 8 + 1) * P],
                                       w[:, t, 2 * C:3 * C], start=(t == 0), stop=(t == CT - 1))
                    mm.then_inc(prod, 1)
        s.clear()


def bias_tables(nc, tkq, qs, ks, us, ws):
    with Scope(nc) as s:
        qk = s.sb("qk", [KP, 2, B, HH, WW])
        tab = s.sb("tab", [HD, 2, SPAN, SPAN])
        ext = s.sb("ext", [HD, 2, SPAN, EXT])
        win = s.sb("win", [KP, 2, WW, P])
        st = [s.sb(f"bst{i}", [P, B * HH, WW]) for i in range(4)]
        windows = s.sem("windows")
        pb = s.ps("pb", [P, 4, 4, P])
        zeroed = s.sem("zeroed")
        qk_in = s.sem("qk_in")
        tab_in = s.sem("tab_in")
        extended = s.sem("extended")
        prod = s.sem("bprod")
        copied_act = s.sem("bcopied_act")
        copied_dve = s.sem("bcopied_dve")
        out = [s.sem(f"bout{i}") for i in range(4)]

        with nc.Block() as block:
            @block.vector
            def _(dve):
                dve.memset(qk[:].rearrange("p a b y x -> p (a b y x)"), 0.0)
                dve.memset(win[:].rearrange("p a x e -> p (a x e)"), 0.0)

        lo = WW - 1 - MAXD
        UNITS = [(which, c) for c in range(NCH) for which in range(2)]

        def evac(eng, odd):
            for u, (which, c) in enumerate(UNITS):
                n = CH_ROWS[c] * 32
                for q in range(odd, 8, 2):
                    eng.wait_ge(prod, u * 8 + q + 1)
                    if u >= 4:
                        eng.wait_ge(out[u % 4], 16 * (1 if which == 0 else CH_ROWS[c - 2]))
                    dst = st[u % 4][0:n, :, q * 4:(q + 1) * 4].rearrange("p t x -> p x t")
                    src = pb[0:n, (u * 8 + q) % 4]
                    if odd:
                        eng.tensor_copy(dst, src).then_inc(copied_dve, 1)
                    else:
                        eng.activation(dst, src, ACT.Copy).then_inc(copied_act, 1)

        with nc.Fori(0, HEADS) as h:
            with nc.Block() as block:
                @block.sync
                def _(sp):
                    sp.dma_start(tab[:], tkq[bass.ds(h, 1)].rearrange("h d a r e -> (h d) a r e")).then_inc(tab_in, 16)
                    for which, src in ((0, qs), (1, ks)):
                        sp.dma_start(qk[0:HD, which].rearrange("d b y x -> d (b y x)"),
                                     src[bass.ds(h, 1)].rearrange("h d n -> (h d) n")).then_inc(qk_in, 16)
                    for u, (which, c) in enumerate(UNITS):
                        rows = CH_ROWS[c]
                        sp.wait_ge(copied_act, 4 * (u + 1))
                        sp.wait_ge(copied_dve, 4 * (u + 1))
                        if which == 0:
                            sp.dma_start(us[bass.ds(h, 1), :, 0:rows * 32, c, :].rearrange("h g p f -> p (h g) f"),
                                         st[u % 4][0:rows * 32].rearrange("p (g f) x -> p g (f x)", g=8)).then_inc(out[u % 4], 16)
                        else:
                            for r in range(rows):
                                sp.dma_start(ws[bass.ds(h, 1), :, :, c * 4 + r, :].rearrange("h b x f -> x (h b) f"),
                                             st[u % 4][r * 32:(r + 1) * 32].rearrange("p (b y) x -> p b (y x)", b=B)).then_inc(out[u % 4], 16)
                    sp.wait_ge(out[0], 32)
                    sp.wait_ge(out[2], 32)
                    sp.wait_ge(out[1], 16 * 8)
                    sp.wait_ge(out[3], 16 * 7)

                @block.vector
                def _(dve):
                    dve.wait_ge(tab_in, 16)
                    for a, fac in ((0, 1.0), (1, SCALE)):
                        dve.tensor_scalar(ext[0:HD, a, :, lo:lo + SPAN], tab[:, a], fac, None, ALU.mult).then_inc(extended, 1)
                        dve.tensor_scalar(ext[0:HD, a, :, 0:lo], tab[:, a, :, 0:1].broadcast_to([HD, SPAN, lo]),
                                          fac, None, ALU.mult).then_inc(extended, 1)
                        dve.tensor_scalar(ext[0:HD, a, :, lo + SPAN:EXT],
                                          tab[:, a, :, SPAN - 1:SPAN].broadcast_to([HD, SPAN, EXT - lo - SPAN]),
                                          fac, None, ALU.mult).then_inc(extended, 1)
                    evac(dve, 1)

                @block.gpsimd
                def _(pool):
                    pool.wait_ge(extended, 6)
                    for u, (which, c) in enumerate(UNITS):
                        if u >= 2:
                            pool.wait_ge(prod, (u - 1) * 8)
                        rows = CH_ROWS[c]
                        src = ext[:, which, c * 4:c * 4 + rows, 0:WW]
                        src = bass.AP(tensor=src.tensor, offset=src.offset,
                                      ap=[list(src.ap[0]), [1, WW], [EXT, rows], [1, WW]])
                        dst = win[0:HD, u % 2, :, 0:rows * WW].rearrange("d x (r e) -> d x r e", r=rows)
                        pool.tensor_copy(dst, src).then_inc(windows, 1)

                @block.scalar
                def _(act):
                    evac(act, 0)

                @block.tensor
                def _(pe):
                    pe.wait_ge(qk_in, 32)
                    for u, (which, c) in enumerate(UNITS):
                        n = CH_ROWS[c] * 32
                        pe.wait_ge(windows, u + 1)
                        for q in range(8):
                            j = u * 8 + q
                            if j >= 4:
                                pe.wait_ge(copied_dve if j % 2 else copied_act, (j - 4) // 2 + 1)
                            for i in range(4):
                                x = q * 4 + i
                                mov = qk[:, which, :, :, x]
                                if which == 0:
                                    mov = mov.rearrange("d b y -> d y b")
                                mm = pe.matmul(pb[0:n, j % 4, i, :], win[:, u % 2, WW - 1 - x, 0:n], mov, start=True, stop=True)
                            mm.then_inc(prod, 1)
            s.clear()


def attention(nc, ident, qs, ks, vs, us, ws, tve, os_):
    GR = 4
    NG = HH // GR
    HALF = HH // 2
    PADR = MAXD
    with Scope(nc) as s:
        kk = s.sb("kk", [KP, B, N])
        qg = s.sb("qg", [KP, 2, B, GR * WW])
        ug = s.sb("ug", [P, 2, NCH, GR * P])
        wt = s.sb("wt", [P, SPAN * HH, WW])
        vh = s.sb("vh", [P, T // P, HD])
        tvx = s.sb("tvx", [P, NCH, WW, HD])
        pr = s.sb("pr", [P, 2, HH + 2 * PADR, WW])
        edge_lo = s.sb("edge_lo", [P, 2, 4, WW])
        edge_hi = s.sb("edge_hi", [P, 2, 3, WW])
        pt = s.sb("pt", [P, 8, GR, P])
        rt = s.sb("rt", [P, NCH, HALF, P])
        oh = s.sb("oh", [HD, B, HALF, WW])
        strip_lo = s.sb("strip_lo", [P, HH - 4, WW])
        strip_hi = s.sb("strip_hi", [P, HH - 5, WW])
        nmax = s.sb("nmax", [P, 2, 3])
        rsum = s.sb("rsum", [P, 2])
        rinv = s.sb("rinv", [P, 2])
        ps = s.ps("ps_s", [P, 2, 2, 512])
        ptp = s.ps("ptp", [P, 2, 4, P])
        rtp = s.ps("rtp", [P, 4, P])
        po = s.ps("po", [P, 512])

        strips = s.sem("strips")
        pads = s.sem("pads")
        k_in, v_in, tv_in, w_in = s.sem("k_in"), s.sem("v_in"), s.sem("tv_in"), s.sem("w_in2")
        grp_in = [s.sem(f"grp_in{i}") for i in range(2)]
        scored = s.sem("scored")
        biased = s.sem("biased")
        bias_step = s.sem("bias_step")
        exped = s.sem("exped")
        norm_step = s.sem("norm_step")
        normed = s.sem("normed2")
        turned = s.sem("turned")
        turned_rel = s.sem("turned_rel")
        pt_copied = s.sem("pt_copied")
        rt_copied = s.sem("rt_copied")
        vprod = s.sem("vprod")
        o_step = s.sem("o_step")
        o_out = s.sem("o_out")

        with nc.Block() as block:
            @block.vector
            def _(dve):
                dve.memset(kk[:].rearrange("p b n -> p (b n)"), 0.0)
                dve.memset(qg[:].rearrange("p a b n -> p (a b n)"), 0.0)
                dve.memset(pr[:].rearrange("p a y x -> p (a y x)"), 0.0)
                for i in range(HH - 4):
                    k = max(0, i - (HH - 8))
                    dve.tensor_copy(strip_lo[:, i, :], ident[:, k * 32:(k + 1) * 32])
                for i in range(HH - 5):
                    k = min(i, 2)
                    dve.tensor_copy(strip_hi[:, i, :], ident[:, k * 32:(k + 1) * 32])

        def spans(y):
            out = []
            if y - MAXD >= 0:
                out.append((0, y - MAXD + 1, None, 0))
            a, b = max(0, y - MAXD + 1), min(HH, y + MAXD)
            out.append((a, b, a - y + MAXD, 1))
            if y + MAXD < HH:
                out.append((y + MAXD, HH, None, SPAN - 1))
            return out

        NSP = [len(spans(y)) for y in range(HH)]

        with nc.Fori(0, HEADS) as h:
            with nc.Block() as block:
                @block.sync
                def _(sp):
                    def group(g):
                        if g >= 2:
                            sp.wait_ge(scored, GR * (g - 1))
                        sp.dma_start(qg[0:HD, g % 2], qs[bass.ds(h, 1)].rearrange("h d (b n) -> (h d) b n", b=B)[
                            :, :, g * GR * WW:(g + 1) * GR * WW]).then_inc(grp_in[g % 2], 16)
                        sp.dma_start(ug[:, g % 2, 0:3], us[bass.ds(h, 1), g, :, 0:3, :].rearrange("h p c f -> (h p) c f")
                                     ).then_inc(grp_in[g % 2], 16)
                        sp.dma_start(ug[0:96, g % 2, 3], us[bass.ds(h, 1), g, 0:96, 3, :].rearrange("h p f -> (h p) f")
                                     ).then_inc(grp_in[g % 2], 16)

                    sp.dma_start(kk[0:HD].rearrange("d b n -> d (b n)"),
                                 ks[bass.ds(h, 1)].rearrange("h d n -> (h d) n")).then_inc(k_in, 16)
                    group(0)
                    sp.dma_start(wt[:].rearrange("p r x -> p (r x)"),
                                 ws[bass.ds(h, 1)].rearrange("h b x a f -> (h b x) (a f)")).then_inc(w_in, 16)
                    group(1)
                    sp.dma_start(vh[:], vs[:, :, bass.ds(h * HD, HD)]).then_inc(v_in, 16)
                    for c in range(NCH):
                        for r in range(CH_ROWS[c]):
                            src = tve[bass.ds(h, 1), c * 4 + r].rearrange("h e d -> (h e) d")
                            sp.dma_start(tvx[r * 32:(r + 1) * 32, c], skewed(src)).then_inc(tv_in, 16)
                    def store(half):
                        sp.wait_ge(o_step, (half + 1) * 8)
                        sp.dma_start(os_[bass.ds(h * HD, HD)].rearrange("c (b n) -> c b n", b=B)[
                            :, :, half * HALF * WW:(half + 1) * HALF * WW],
                            oh[:].rearrange("d b y x -> d b (y x)")).then_inc(o_out, 16)

                    for g in range(2, NG):
                        if g == HALF // GR + 2:
                            store(0)
                        group(g)
                    store(1)
                    sp.wait_ge(o_out, 32)

                @block.tensor
                def _(pe):
                    def scores(y):
                        g = y // GR
                        if y % GR == 0:
                            pe.wait_ge(grp_in[g % 2], 48 * (g // 2 + 1))
                        if y >= 2:
                            pe.wait_ge(biased, y - 1)
                        for half in range(2):
                            for b in range(B):
                                pe.matmul(ps[b * 32:(b + 1) * 32, y % 2, half, :],
                                          qg[:, g % 2, b, y % GR * WW:(y % GR + 1) * WW],
                                          kk[:, b, half * 512:(half + 1) * 512],
                                          start=True, stop=False, skip_group_check=True)
                        for c, (a, b, strip, off, n) in enumerate([
                                (0, y - 3, strip_lo, HH - 4 - (y - 3), P),
                                (y - 3, y + 1, None, 0, P),
                                (y + 1, y + 5, None, 0, P),
                                (y + 5, HH, strip_hi, 0, 96)]):
                            lo, hi = max(a, 0), min(b, HH)
                            for p0, p1 in ((lo, min(hi, 16)), (max(lo, 16), hi)):
                                if p0 >= p1:
                                    continue
                                if strip is None:
                                    mov = ident[0:n, (p0 - a) * 32:(p1 - a) * 32]
                                else:
                                    mov = strip[0:n, off + p0 - a:off + p1 - a, :]
                                mm = pe.matmul(ps[:, y % 2, p0 // 16, p0 % 16 * 32:(p0 % 16 + p1 - p0) * 32],
                                               ug[0:n, g % 2, c, y % GR * P:(y % GR + 1) * P], mov,
                                               start=False, stop=True, skip_group_check=True)
                        mm.then_inc(scored, 1)

                    def turn(y):
                        pe.wait_ge(normed, y + 1)
                        for i in range(2):
                            if y >= 1:
                                pe.wait_ge(pt_copied, 2 * y - 1 + i)
                            for k in range(4):
                                r0 = PADR + (i * 4 + k) * 4
                                mm = pe.matmul(ptp[:, i, k, :], pr[:, y % 2, r0:r0 + 4, :], ident[:], start=True,
                                               stop=True, is_transpose=True)
                            mm.then_inc(turned, 1)
                        if y >= 1:
                            pe.wait_ge(rt_copied, y)
                        for c, rows in enumerate((edge_lo[:, y % 2], pr[:, y % 2, y + 4:y + 8, :],
                                                  pr[:, y % 2, y + 8:y + 12, :], edge_hi[:, y % 2])):
                            n = CH_ROWS[c] * 32
                            mm = pe.matmul(rtp[0:n, c, :], rows, ident[:], start=True, stop=True, is_transpose=True)
                        mm.then_inc(turned_rel, 1)

                    def free(n):
                        if n >= 1:
                            pe.wait_ge(o_step, n)

                    def values(g, n):
                        pe.wait_ge(pt_copied, 2 * GR * (g + 1))
                        if g == 0:
                            pe.wait_ge(v_in, 16)
                        free(n)
                        for b in range(B):
                            for k in range(8):
                                mm = pe.matmul(po[0:HD, b * P:(b + 1) * P], vh[:, b * 8 + k, :],
                                               pt[:, k, :, b * 32:(b + 1) * 32], start=(k == 0), stop=(k == 7))
                        mm.then_inc(vprod, 1)

                    def table_values(half, n):
                        pe.wait_ge(rt_copied, HALF * (half + 1))
                        if half == 0:
                            pe.wait_ge(tv_in, 16 * SPAN)
                        for q in range(4):
                            free(n + q)
                            for i in range(8):
                                x = q * 8 + i
                                for c in range(NCH):
                                    rows = CH_ROWS[c] * 32
                                    mov = rt[0:rows, c].rearrange("p y (b x) -> p y b x", b=B)[:, :, :, x]
                                    mm = pe.matmul(po[0:HD, i * 64:(i + 1) * 64], tvx[0:rows, c, WW - 1 - x, :], mov,
                                                   start=(c == 0), stop=(c == NCH - 1))
                            mm.then_inc(vprod, 1)

                    pe.wait_ge(k_in, 16)
                    n = 0
                    for y in range(HH + 1):
                        if y < HH:
                            scores(y)
                        t = y - 1
                        if t > 0 and t % GR == 0:
                            values(t // GR - 1, n)
                            n += 1
                        if t == HALF:
                            table_values(0, n)
                            n += 4
                        if t >= 0:
                            turn(t)
                    values(NG - 1, n)
                    table_values(1, n + 1)

                @block.vector
                def _(dve):
                    def bias(y):
                        dve.wait_ge(scored, y + 1)
                        if y >= 2:
                            dve.wait_ge(turned_rel, y - 1)
                        for i, (a, b, r, row) in enumerate(spans(y)):
                            if r is None:
                                tabl = wt[:, row * HH + a:row * HH + b, :]
                            else:
                                r0 = r * HH + a
                                tabl = wt[:, r0:r0 + (b - a - 1) * (HH + 1) + 1:HH + 1, :]
                            if i:
                                dve.wait_ge(bias_step, sum(k - 1 for k in NSP[:y]) + i)
                            ins = dve.tensor_tensor_reduce(
                                pr[:, y % 2, PADR + a:PADR + b, :],
                                ps[:, y % 2].rearrange("p a f -> p (a f)")[:, a * 32:b * 32].rearrange("p (y x) -> p y x", x=WW),
                                tabl, -1.0, nmax[:, y % 2, i - 1:i] if i else BIG, ALU.add, ALU.min,
                                nmax[:, y % 2, i:i + 1])
                            ins.then_inc(biased if i == NSP[y] - 1 else bias_step, 1)

                    def normalise(y):
                        dve.wait_ge(exped, y + 1)
                        dve.reciprocal(rinv[:, y % 2:y % 2 + 1], rsum[:, y % 2:y % 2 + 1]).then_inc(norm_step, 1)
                        dve.wait_ge(norm_step, 2 * y + 1)
                        dve.tensor_scalar(pr[:, y % 2, PADR:PADR + HH, :], pr[:, y % 2, PADR:PADR + HH, :],
                                          rinv[:, y % 2:y % 2 + 1], None, ALU.mult).then_inc(norm_step, 1)
                        dve.wait_ge(norm_step, 2 * y + 2)
                        dve.tensor_reduce(edge_lo[:, y % 2, 0, :], pr[:, y % 2, 0:y + 1, :].rearrange("p y x -> p x y"),
                                          AX_X, ALU.add)
                        dve.tensor_copy(edge_lo[:, y % 2, 1:4, :], pr[:, y % 2, y + 1:y + 4, :])
                        dve.tensor_reduce(edge_hi[:, y % 2, 2, :],
                                          pr[:, y % 2, y + 2 * PADR:HH + 2 * PADR, :].rearrange("p y x -> p x y"),
                                          AX_X, ALU.add)
                        dve.tensor_copy(edge_hi[:, y % 2, 0:2, :], pr[:, y % 2, y + 12:y + 14, :]).then_inc(normed, 1)

                    def out_values(g, n):
                        dve.wait_ge(vprod, n + 1)
                        if g == NG // 2:
                            dve.wait_ge(o_out, 16)
                        y0 = g * GR % HALF
                        dve.tensor_copy(oh[:, :, y0:y0 + GR, :], po[0:HD].rearrange("d (b y x) -> d b y x", b=B, y=GR)
                                        ).then_inc(o_step, 1)

                    def out_table(n):
                        for q in range(4):
                            dve.wait_ge(vprod, n + q + 1)
                            dve.wait_ge(o_step, n + q)
                            o = oh[:, :, :, q * 8:(q + 1) * 8].rearrange("d b y x -> d x y b")
                            dve.tensor_tensor(o, po[0:HD].rearrange("d (x y b) -> d x y b", x=8, b=B), o,
                                              ALU.add).then_inc(o_step, 1)

                    dve.wait_ge(w_in, 16)
                    n = 0
                    for y in range(HH + 1):
                        if y < HH:
                            bias(y)
                        t = y - 1
                        if t > 0 and t % GR == 0:
                            out_values(t // GR - 1, n)
                            n += 1
                        if t == HALF:
                            out_table(n)
                            n += 4
                        if t >= 0:
                            normalise(t)
                    out_values(NG - 1, n)
                    out_table(n + 1)

                @block.scalar
                def _(act):
                    for y in range(HH + 1):
                        if y < HH:
                            act.wait_ge(biased, y + 1)
                            if y >= 2:
                                act.wait_ge(norm_step, 2 * (y - 2) + 1)
                            act.activation(pr[:, y % 2, PADR:PADR + HH, :], pr[:, y % 2, PADR:PADR + HH, :], ACT.Exp,
                                           bias=nmax[:, y % 2, NSP[y] - 1:NSP[y]], scale=-1.0,
                                           accum_out=rsum[:, y % 2:y % 2 + 1]).then_inc(exped, 1)
                        t = y - 1
                        if t < 0:
                            continue
                        for i in range(2):
                            act.wait_ge(turned, 2 * t + i + 1)
                            act.activation(pt[:, i * 4:(i + 1) * 4, t % GR, :], ptp[:, i], ACT.Copy).then_inc(pt_copied, 1)
                        act.wait_ge(turned_rel, t + 1)
                        act.activation(rt[:, 0:3, t % HALF, :], rtp[:, 0:3], ACT.Copy)
                        act.activation(rt[0:96, 3, t % HALF, :], rtp[0:96, 3], ACT.Copy).then_inc(rt_copied, 1)
            s.clear()


def skewed(src):
    row = list(src.ap[-2])[0]
    return bass.AP(tensor=src.tensor, offset=src.offset, ap=[[row, WW], [row, WW], [1, HD]])


def layer_norm(dve, step, n, powed, m, x, bst, bmv, rstd, xn):
    dve.bn_stats(bst, x).then_inc(step, 1)
    dve.wait_ge(step, n + 1)
    dve.bn_aggr(bmv, bst).then_inc(step, 1)
    dve.wait_ge(step, n + 2)
    dve.tensor_scalar(rstd, bmv[:, 1:2], 1e-5, None, ALU.add).then_inc(step, 1)
    dve.wait_ge(powed, m + 1)
    dve.tensor_scalar(xn, x, bmv[:, 0:1], rstd, ALU.subtract, ALU.mult).then_inc(step, 1)


def window(nc, xt, w_proj0, b_proj0, mem_t, mem, qkv_w, qkv_b, qkb, proj_w, proj_b, ident, mhalf, os_, x2):
    NT = N // P
    KEYS = MEM + WIN + P
    with Scope(nc) as s:
        wp0 = s.sb("wp0", [P, CT, C])
        wqk = s.sb("wqk", [P, CT, 2, HEADS, 64])
        wv = s.sb("wv", [P, CT, C])
        wp1 = s.sb("wp1", [P, CT, C])
        brow = s.sb("brow", [P, 3, C])
        bqk = s.sb("bqk", [HD, 2, HEADS])
        mask = s.sb("mask", [P, 2, KEYS])
        oin = s.sb("oin", [P, 2, CT, P])
        xin = s.sb("xin", [P, 2, C])
        x1 = s.sb("x1", [P, NT, C])
        xn = s.sb("xn", [P, 2, C])
        xnt = s.sb("xnt", [P, CT, N])
        bst = s.sb("bst", [P, 6])
        rstd = s.sb("rstdw", [P, 1])
        powed = s.sem("powedw")
        bmv = s.sb("bmv", [P, 2])
        qt = s.sb("qt", [KP, HEADS, N])
        kb = s.sb("kb", [KP, NT, HEADS, KEYS])
        vv = s.sb("vv", [P, NT, C])
        vp = s.sb("vp", [P, NT, C])
        pr = s.sb("pw", [P, 2, 4, KEYS])
        nmax = s.sb("nmaxw", [P, 2, 4])
        rsum = s.sb("rsumw", [P, 2, HEADS])
        rinv = s.sb("rinvw", [P, 2, HEADS])
        pt = s.sb("ptw", [P, 2, 4, P])
        yn = s.sb("yn", [P, C])
        yt = s.sb("yt", [P, CT, P])
        xo = s.sb("xo", [P, 2, C])
        pm = s.ps("pm", [P, 2, 512])
        pqk = s.ps("pqk", [P, 2, 512])
        psc = s.ps("psc", [P, 2, 2, KEYS])
        ptr = s.ps("ptr", [P, 2, 4, P])

        wl = s.sem("wl")
        zer = s.sem("zer")
        msk = s.sem("msk")
        bq_scaled = s.sem("bq_scaled")
        tile_in = [s.sem(f"tile_in{i}") for i in range(2)]
        m_done = s.sem("m_done")
        f_step = s.sem("f_step")
        xn_turned = s.sem("xn_turned")
        xnt_copied = s.sem("xnt_copied")
        qk_done = s.sem("qk_done")
        qk_act = s.sem("qk_act")
        qk_dve = s.sem("qk_dve")
        v_added = s.sem("v_added")
        s_done = s.sem("s_done")
        masked = s.sem("masked")
        exped = s.sem("exped_w")
        p_turned = s.sem("p_turned")
        p_copied = s.sem("p_copied")
        y_step = s.sem("y_step")
        y_copied = s.sem("y_copied")
        x2_added = s.sem("x2_added")
        x2_step = s.sem("x2_step")
        x2_out = [s.sem(f"x2_out{i}") for i in range(2)]

        with nc.Block() as block:
            @block.vector
            def _(dve):
                dve.memset(wqk[:].rearrange("p t a h e -> p (t a h e)"), 0.0).then_inc(zer, 1)
                dve.memset(kb[:].rearrange("p t h k -> p (t h k)"), 0.0).then_inc(zer, 1)
                dve.memset(vp[:].rearrange("p t c -> p (t c)"), 0.0).then_inc(zer, 1)
                dve.memset(qt[:].rearrange("p h n -> p (h n)"), 0.0)
                dve.wait_ge(wl, 16 * 20)
                dve.tensor_scalar(bqk[:, 0], bqk[:, 0], SCALE, None, ALU.mult)

            @block.gpsimd
            def _(pool):
                pool.memset(mask[:].rearrange("p a k -> p (a k)"), 0.0).then_inc(msk, 1)
                pool.wait_ge(msk, 1)
                pool.affine_select(out=mask[:, 0, MEM:MEM + WIN], in_=mask[:, 0, MEM:MEM + WIN], compare_op=ALU.is_ge,
                                   fill=MASKED, base=0, pattern=[[1, WIN]], channel_multiplier=-1)
                pool.memset(mask[:, 1, MEM:MEM + WIN], MASKED)
                for a in range(2):
                    m = mask[:, a, MEM + WIN:KEYS]
                    pool.affine_select(out=m, in_=m, compare_op=ALU.is_ge, fill=MASKED, base=0,
                                       pattern=[[-1, P]], channel_multiplier=1).then_inc(msk, 1)
                    pool.wait_ge(msk, 2 + 2 * a)
                    pool.affine_select(out=m, in_=m, compare_op=ALU.is_ge, fill=MASKED, base=WIN,
                                       pattern=[[1, P]], channel_multiplier=-1).then_inc(msk, 1)

            @block.sync
            def _(sp):
                def load(dst, src):
                    sp.dma_start(dst, src).then_inc(wl, 16)

                load(wp0[:], w_proj0.rearrange("(t p) n -> p t n", p=P))
                load(wv[:], qkv_w[:, 2 * C:3 * C].rearrange("(t p) n -> p t n", p=P))
                load(wp1[:], proj_w.rearrange("(t p) n -> p t n", p=P))
                load(brow[:, 0], b_proj0.rearrange("(o n) -> o n", o=1).broadcast_to([P, C]))
                load(brow[:, 1], qkv_b[2 * C:3 * C].rearrange("(o n) -> o n", o=1).broadcast_to([P, C]))
                load(brow[:, 2], proj_b.rearrange("(o n) -> o n", o=1).broadcast_to([P, C]))
                load(bqk[:], qkb)
                sp.wait_ge(zer, 1)
                for t in range(CT):
                    for a in range(2):
                        load(wqk[:, t, a, :, 0:HD], qkv_w[t * P:(t + 1) * P, a * C:(a + 1) * C].rearrange("p (h d) -> p h d", d=HD))
                sp.wait_ge(zer, 3)
                for t in range(4):
                    load(kb[0:HD, 2 * t:2 * t + 1, :, 0:MEM].rearrange("d o h k -> d (o h) k"), mem_t)
                for t in range(2):
                    load(vp[0:MEM, 4 * t], mem)
                load(vp[0:MEM, 2], mem)
                sp.wait_ge(wl, 16 * 20)

        with nc.Block() as block:
            @block.scalar
            def _(act):
                for t in range(4):
                    act.activation(kb[0:HD, 2 * t + 1, :, 0:MEM], kb[0:HD, 2 * t, :, 0:MEM], ACT.Copy)
                for t, u in ((1, 0), (3, 2), (5, 4)):
                    act.activation(vp[0:MEM, t], vp[0:MEM, u], ACT.Copy)

            @block.vector
            def _(dve):
                for t, u in ((6, 4), (7, 4)):
                    dve.tensor_copy(vp[0:MEM, t], vp[0:MEM, u])

        def turn_xn(pe, t):
            pe.wait_ge(f_step, 6 * (t + 1))
            if t >= 2:
                pe.wait_ge(xnt_copied, t - 1)
            for c in range(CT):
                mm = pe.matmul(ptr[:, t % 2, c, :], xn[:, t % 2, c * P:(c + 1) * P], ident[:], start=True, stop=True,
                               is_transpose=True)
            mm.then_inc(xn_turned, 1)

        def probs(pe, u):
            t, q = divmod(u, 2)
            for k in range(4):
                h = q * 4 + k
                pe.wait_ge(exped, 4 * u + k + 1)
                j = 4 * u + k
                if k % 2 == 0 and j >= 4:
                    pe.wait_ge(p_copied, (j - 4) // 2 + 1)
                for c in range(2):
                    mm = pe.matmul(ptr[:, k // 2, k % 2 * 2 + c, :], pr[:, u % 2, k, c * P:(c + 1) * P], ident[:],
                                   start=True, stop=True, is_transpose=True)
                if k % 2 == 1:
                    mm.then_inc(p_turned, 1)
            for i in range(2):
                pe.wait_ge(p_copied, 2 * u + i + 1)
                if q == 0 and i == 0 and t >= 1:
                    pe.wait_ge(y_step, t)
                for k in (2 * i, 2 * i + 1):
                    h = q * 4 + k
                    for c in range(2):
                        mm = pe.matmul(pm[:, 0, h * HD:(h + 1) * HD], pt[:, i, k % 2 * 2 + c, :],
                                       (vp if c == 0 else vv)[:, t, h * HD:(h + 1) * HD], start=(c == 0), stop=(c == 1),
                                       skip_group_check=True)
            mm.then_inc(m_done, 1)
            if q == 1:
                pe.wait_ge(y_step, t + 1)
                pe.wait_ge(p_copied, 2 * u + 2)
                for c in range(CT):
                    mm = pe.matmul(ptr[:, 0, c, :], yn[:, c * P:(c + 1) * P], ident[:], start=True, stop=True,
                                   is_transpose=True)
                mm.then_inc(p_turned, 1)
                pe.wait_ge(y_copied, t + 1)
                if t >= 1:
                    pe.wait_ge(x2_added, t)
                for c in range(CT):
                    mm = pe.matmul(pm[:, 1, 0:C], yt[:, c], wp1[:, c], start=(c == 0), stop=(c == CT - 1))
                mm.then_inc(m_done, 1)

        with nc.Fori(0, B) as b:
            with nc.Block() as block:
                @block.sync
                def _(sp):
                    for t in range(NT):
                        if t >= 2:
                            sp.wait_ge(m_done, t - 1)
                            sp.wait_ge(f_step, 6 * (t - 2) + 1)
                        tok = bass.ds(b * N + t * P, P)
                        sp.dma_start(oin[:, t % 2], os_.rearrange("(c p) n -> p c n", p=P)[:, :, tok]).then_inc(tile_in[t % 2], 16)
                        sp.dma_start(xin[:, t % 2], xt[tok, :]).then_inc(tile_in[t % 2], 16)
                    for t in range(NT):
                        sp.wait_ge(x2_added, t + 1)
                        sp.dma_start(x2[bass.ds(b * N + t * P, P), :], xo[:, t % 2]).then_inc(x2_out[t % 2], 16)
                    for i in range(2):
                        sp.wait_ge(x2_out[i], 16 * NT // 2)

                @block.gpsimd
                def _(pool):
                    for t in range(NT):
                        pool.wait_ge(f_step, 6 * t + 5)
                        pool.tensor_tensor(rstd[:], rstd[:], mhalf[:, 0:1], ALU.pow).then_inc(powed, 1)

                @block.tensor
                def _(pe):
                    for t in range(NT):
                        pe.wait_ge(tile_in[t % 2], 32 * (t // 2 + 1))
                        if t >= 2:
                            pe.wait_ge(f_step, 6 * (t - 2) + 1)
                        for c in range(CT):
                            mm = pe.matmul(pm[:, t % 2, 0:C], oin[:, t % 2, c], wp0[:, c], start=(c == 0), stop=(c == CT - 1))
                        mm.then_inc(m_done, 1)
                        if t >= 1:
                            turn_xn(pe, t - 1)
                    turn_xn(pe, NT - 1)
                    pe.wait_ge(xnt_copied, NT)
                    for t in range(NT):
                        if t >= 2:
                            pe.wait_ge(v_added, t - 1)
                        else:
                            pe.wait_ge(f_step, 6 * NT)
                        for c in range(CT):
                            mm = pe.matmul(pm[:, t % 2, 0:C], xnt[:, c, t * P:(t + 1) * P], wv[:, c], start=(c == 0), stop=(c == CT - 1))
                        mm.then_inc(m_done, 1)
                    j = 0
                    for a in range(2):
                        for hp in range(HEADS // 2):
                            for half in range(2):
                                if j >= 2:
                                    pe.wait_ge(qk_act, j - 1)
                                    pe.wait_ge(qk_dve, j - 1)
                                for c in range(CT):
                                    mm = pe.matmul(pqk[:, j % 2, :], wqk[:, c, a, 2 * hp:2 * hp + 2].rearrange("p h e -> p (h e)"),
                                                   xnt[:, c, half * 512:(half + 1) * 512], start=(c == 0), stop=(c == CT - 1))
                                mm.then_inc(qk_done, 1)
                                j += 1
                    pe.wait_ge(qk_act, 16)
                    pe.wait_ge(qk_dve, 16)
                    pe.wait_ge(v_added, NT)
                    U = 2 * NT
                    for u in range(U + 1):
                        if u < U:
                            t, q = divmod(u, 2)
                            for k in range(4):
                                if u >= 1 and k % 2 == 0:
                                    pe.wait_ge(masked, 4 * (u - 1) + k + 2)
                                h = q * 4 + k
                                mm = pe.matmul(psc[:, k // 2, k % 2, :], qt[:, h, t * P:(t + 1) * P], kb[:, t, h, :],
                                               start=True, stop=True)
                                if k % 2 == 1:
                                    mm.then_inc(s_done, 1)
                        if u >= 1:
                            probs(pe, u - 1)

                @block.vector
                def _(dve):
                    n = 0
                    for t in range(NT):
                        dve.wait_ge(m_done, t + 1)
                        dve.wait_ge(tile_in[t % 2], 32 * (t // 2 + 1))
                        dve.tensor_tensor(x1[:, t], pm[:, t % 2, 0:C], xin[:, t % 2], ALU.add).then_inc(f_step, 1)
                        dve.wait_ge(f_step, n + 1)
                        dve.tensor_tensor(x1[:, t], x1[:, t], brow[:, 0], ALU.add).then_inc(f_step, 1)
                        dve.wait_ge(f_step, n + 2)
                        if t >= 2:
                            dve.wait_ge(xn_turned, t - 1)
                        layer_norm(dve, f_step, n + 2, powed, t, x1[:, t], bst[:], bmv[:], rstd[:], xn[:, t % 2])
                        n += 6
                    for t in range(NT):
                        dve.wait_ge(m_done, NT + t + 1)
                        if t + 1 < NT:
                            dve.tensor_tensor(vp[WIN:P, t + 1], pm[WIN:P, t % 2, 0:C], brow[WIN:P, 1], ALU.add)
                        dve.tensor_tensor(vv[:, t], pm[:, t % 2, 0:C], brow[:, 1], ALU.add).then_inc(v_added, 1)
                    j = 0
                    for a in range(2):
                        for hp in range(HEADS // 2):
                            for half in range(2):
                                dve.wait_ge(qk_done, j + 1)
                                src = pqk[64:64 + HD, j % 2, :]
                                h = 2 * hp + 1
                                if a == 0:
                                    dve.tensor_scalar(qt[0:HD, h, half * 512:(half + 1) * 512], src, SCALE, bqk[:, 0, h:h + 1],
                                                      ALU.mult, ALU.add).then_inc(qk_dve, 1)
                                else:
                                    s4 = src.rearrange("d (t k) -> d t k", k=P)
                                    m = 4 if half == 0 else 3
                                    dve.tensor_scalar(kb[0:HD, half * 4 + 1:half * 4 + 1 + m, h, MEM:MEM + WIN], s4[:, 0:m, WIN:P],
                                                      bqk[:, 1, h:h + 1], None, ALU.add)
                                    dve.tensor_scalar(kb[0:HD, half * 4:half * 4 + 4, h, MEM + WIN:KEYS], s4,
                                                      bqk[:, 1, h:h + 1], None, ALU.add).then_inc(qk_dve, 1)
                                j += 1

                    def finish(t):
                        dve.wait_ge(m_done, 2 * NT + 3 * t + 2)
                        dve.wait_ge(exped, 8 * (t + 1))
                        dve.reciprocal(rinv[:, t % 2], rsum[:, t % 2]).then_inc(x2_step, 1)
                        dve.wait_ge(x2_step, 2 * t + 1)
                        if t >= 1:
                            dve.wait_ge(y_copied, t)
                        dve.tensor_tensor(yn[:].rearrange("p (h d) -> p h d", d=HD), pm[:, 0, 0:C].rearrange("p (h d) -> p h d", d=HD),
                                          rinv[:, t % 2].rearrange("p (h o) -> p h o", o=1).broadcast_to([P, HEADS, HD]),
                                          ALU.mult).then_inc(y_step, 1)
                        dve.wait_ge(m_done, 2 * NT + 3 * t + 3)
                        if t >= 2:
                            dve.wait_ge(x2_out[t % 2], 16 * (t // 2))
                        dve.tensor_tensor(xo[:, t % 2], pm[:, 1, 0:C], x1[:, t], ALU.add).then_inc(x2_step, 1)
                        dve.wait_ge(x2_step, 2 * t + 2)
                        dve.tensor_tensor(xo[:, t % 2], xo[:, t % 2], brow[:, 2], ALU.add).then_inc(x2_added, 1)

                    for u in range(2 * NT + 1):
                        if u < 2 * NT:
                            t, q = divmod(u, 2)
                            for k in range(4):
                                dve.wait_ge(s_done, 2 * u + k // 2 + 1)
                                if u >= 2 and k % 2 == 0:
                                    dve.wait_ge(p_turned, 2 * (u - 2) + k // 2 + 1 + (u - 2) // 2)
                                dve.tensor_tensor_reduce(pr[:, u % 2, k, :], psc[:, k // 2, k % 2, :], mask[:, 1 if t == 0 else 0],
                                                         -1.0, BIG, ALU.add, ALU.min, nmax[:, u % 2, k:k + 1]).then_inc(masked, 1)
                        if u >= 1 and (u - 1) % 2 == 1:
                            finish((u - 1) // 2)

                @block.scalar
                def _(act):
                    for t in range(NT):
                        act.wait_ge(xn_turned, t + 1)
                        act.activation(xnt[:, :, t * P:(t + 1) * P], ptr[:, t % 2, 0:CT, :], ACT.Copy).then_inc(xnt_copied, 1)
                    j = 0
                    for a in range(2):
                        for hp in range(HEADS // 2):
                            for half in range(2):
                                act.wait_ge(qk_done, j + 1)
                                src = pqk[0:HD, j % 2, :]
                                h = 2 * hp
                                if a == 0:
                                    act.activation(qt[0:HD, h, half * 512:(half + 1) * 512], src, ACT.Identity, scale=SCALE,
                                                   bias=bqk[:, 0, h:h + 1]).then_inc(qk_act, 1)
                                else:
                                    s4 = src.rearrange("d (t k) -> d t k", k=P)
                                    m = 4 if half == 0 else 3
                                    act.activation(kb[0:HD, half * 4 + 1:half * 4 + 1 + m, h, MEM:MEM + WIN], s4[:, 0:m, WIN:P],
                                                   ACT.Identity, bias=bqk[:, 1, h:h + 1])
                                    act.activation(kb[0:HD, half * 4:half * 4 + 4, h, MEM + WIN:KEYS], s4, ACT.Identity,
                                                   bias=bqk[:, 1, h:h + 1]).then_inc(qk_act, 1)
                                j += 1

                    def copies(u):
                        t, q = divmod(u, 2)
                        for i in range(2):
                            act.wait_ge(p_turned, 2 * u + u // 2 + i + 1)
                            act.activation(pt[:, i], ptr[:, i], ACT.Copy).then_inc(p_copied, 1)
                        if q == 1:
                            act.wait_ge(p_turned, 2 * u + u // 2 + 3)
                            act.activation(yt[:], ptr[:, 0, 0:CT], ACT.Copy).then_inc(y_copied, 1)

                    for u in range(2 * NT + 1):
                        if u < 2 * NT:
                            t, q = divmod(u, 2)
                            for k in range(4):
                                act.wait_ge(masked, 4 * u + k + 1)
                                if t >= 2 and k == 0:
                                    act.wait_ge(x2_step, 2 * (t - 2) + 1)
                                act.activation(pr[:, u % 2, k, :], pr[:, u % 2, k, :], ACT.Exp, bias=nmax[:, u % 2, k:k + 1],
                                               scale=-1.0, accum_out=rsum[:, t % 2, q * 4 + k:q * 4 + k + 1]).then_inc(exped, 1)
                        if u >= 1:
                            copies(u - 1)
            s.clear()


def experts(nc, x2, gate_w, gate_b, w1, b1, w2, b2, ident, mhalf, out):
    TB = 512
    TT = TB // P
    with Scope(nc) as s:
        w1s = s.sb("w1s", [P, EXPERTS, CT, HID])
        w2s = s.sb("w2s", [P, EXPERTS, HT, C])
        gw = s.sb("gw", [P, CT, EXPERTS])
        gb = s.sb("gb", [P, EXPERTS])
        b1s = s.sb("b1s", [P, EXPERTS, HT])
        b2s = s.sb("b2s", [EXPERTS, C])
        tri = s.sb("tri", [P, EXPERTS, EXPERTS])
        xr = s.sb("xr", [P, TT, C])
        xn = s.sb("xne", [P, C])
        xnt = s.sb("xnte", [P, CT, TB])
        bst = s.sb("bste", [P, 6])
        rstd = s.sb("rstde", [P, 1])
        powed = s.sem("powede")
        bmv = s.sb("bmve", [P, 2])
        g = s.sb("g", [P, TT, EXPERTS])
        red = s.sb("red", [P, TT])
        lt = s.sb("lt", [P, TT, EXPERTS, EXPERTS])
        eq = s.sb("eq", [P, TT, EXPERTS, EXPERTS])
        gt = s.sb("gt", [EXPERTS, TT, P])
        ht = s.sb("ht", [P, HT, TB])
        pu = s.ps("pu", [P, 3, 512])
        pd = s.ps("pd", [P, 3, 512])
        ptr = s.ps("ptre", [P, 4, P])
        pgt = s.ps("pgt", [P, 512])
        wl = s.sem("wle")
        tri_step = s.sem("tri_step")
        x_in = s.sem("x_in_e")
        ln = s.sem("ln")
        turned = s.sem("turned_e")
        copied = s.sem("copied_e")
        g_done = s.sem("g_done")
        g_step = s.sem("g_step")
        g_exp = s.sem("g_exp")
        gr_step = s.sem("gr_step")
        gt_done = s.sem("gt_done")
        gt_copied = s.sem("gt_copied")
        up = s.sem("up")
        gelu = s.sem("gelu")
        down = s.sem("down")
        summed = s.sem("summed")
        o_out = s.sem("o_out_e")

        with nc.Block() as block:
            @block.sync
            def _(sp):
                sp.dma_start(gw[:], gate_w.rearrange("(t p) n -> p t n", p=P)).then_inc(wl, 16)
                sp.dma_start(gb[:], gate_b.rearrange("(o n) -> o n", o=1).broadcast_to([P, EXPERTS])).then_inc(wl, 16)
                sp.dma_start(b1s[:], b1).then_inc(wl, 16)
                sp.dma_start(b2s[:], b2).then_inc(wl, 16)
                for e in range(EXPERTS):
                    sp.dma_start(w1s[:, e], w1[e].rearrange("(t p) n -> p t n", p=P)).then_inc(wl, 16)
                    sp.dma_start(w2s[:, e], w2[e].rearrange("(t p) n -> p t n", p=P)).then_inc(wl, 16)
                sp.wait_ge(wl, 16 * (4 + 2 * EXPERTS))

            @block.gpsimd
            def _(pool):
                pool.memset(tri[:].rearrange("p j e -> p (j e)"), 1.0).then_inc(tri_step, 1)
                pool.wait_ge(tri_step, 1)
                pool.affine_select(out=tri[:], in_=tri[:], compare_op=ALU.is_gt, fill=0.0, base=0,
                                   pattern=[[-1, EXPERTS], [1, EXPERTS]], channel_multiplier=0)

        with nc.Fori(0, T // TB) as blk:
            with nc.Block() as block:
                @block.sync
                def _(sp):
                    sp.dma_start(xr[:], x2[bass.ds(blk * TB, TB), :].rearrange("(t p) c -> p t c", p=P)).then_inc(x_in, 16)
                    sp.wait_ge(summed, TT * (1 + EXPERTS))
                    sp.dma_start(out[bass.ds(blk * TB, TB), :].rearrange("(t p) c -> p t c", p=P), xr[:]).then_inc(o_out, 16)
                    sp.wait_ge(o_out, 16)

                @block.gpsimd
                def _(pool):
                    for t in range(TT):
                        pool.wait_ge(ln, 4 * t + 3)
                        pool.tensor_tensor(rstd[:], rstd[:], mhalf[:, 0:1], ALU.pow).then_inc(powed, 1)

                @block.tensor
                def _(pe):
                    for t in range(TT):
                        pe.wait_ge(ln, 4 * (t + 1))
                        if t >= 1:
                            pe.wait_ge(copied, t)
                        for c in range(CT):
                            mm = pe.matmul(ptr[:, c, :], xn[:, c * P:(c + 1) * P], ident[:], start=True, stop=True,
                                           is_transpose=True)
                        mm.then_inc(turned, 1)
                    pe.wait_ge(copied, TT)
                    for t in range(TT):
                        for c in range(CT):
                            mm = pe.matmul(pgt[:, t * EXPERTS:(t + 1) * EXPERTS], xnt[:, c, t * P:(t + 1) * P], gw[:, c],
                                           start=(c == 0), stop=(c == CT - 1), skip_group_check=True)
                    mm.then_inc(g_done, 1)
                    j = d = 0
                    for e in range(EXPERTS):
                        for m in range(HT):
                            if j >= 3:
                                pe.wait_ge(gelu, j - 2)
                            for c in range(CT):
                                mm = pe.matmul(pu[:, j % 3, :], w1s[:, e, c, m * P:(m + 1) * P], xnt[:, c, :],
                                               start=(c == 0), stop=(c == CT - 1))
                            mm.then_inc(up, 1)
                            j += 1
                        if e == 0:
                            pe.wait_ge(g_step, 13)
                            for t in range(TT):
                                mm = pe.matmul(ptr[0:EXPERTS, t, :], g[:, t, :], ident[:], start=True, stop=True,
                                               is_transpose=True)
                            mm.then_inc(gt_done, 1)
                            pe.wait_ge(gt_copied, 1)
                            for t in range(TT):
                                if d >= 3:
                                    pe.wait_ge(summed, d - 2)
                                pe.matmul(pd[:, d % 3, 0:C], gt[:, t, :], b2s[:], start=True, stop=True).then_inc(down, 1)
                                d += 1
                        for t in range(TT):
                            pe.wait_ge(summed, d - 2)
                            for m in range(HT):
                                if t == 0:
                                    pe.wait_ge(gelu, e * HT + m + 1)
                                mm = pe.matmul(pd[:, d % 3, 0:C], ht[:, m, t * P:(t + 1) * P], w2s[:, e, m],
                                               start=(m == 0), stop=(m == HT - 1))
                            mm.then_inc(down, 1)
                            d += 1

                @block.scalar
                def _(act):
                    for t in range(TT):
                        act.wait_ge(turned, t + 1)
                        act.activation(xnt[:, :, t * P:(t + 1) * P], ptr[:, 0:CT, :], ACT.Copy).then_inc(copied, 1)
                    act.wait_ge(g_step, 3)
                    act.activation(g[:], g[:], ACT.Exp).then_inc(g_exp, 1)
                    j = 0
                    for e in range(EXPERTS):
                        for m in range(HT):
                            act.wait_ge(up, j + 1)
                            if e >= 1:
                                act.wait_ge(down, TT * (e + 1))
                            act.activation(ht[:, m, :], pu[:, j % 3, :], ACT.Gelu, bias=b1s[:, e, m:m + 1]).then_inc(gelu, 1)
                            j += 1
                        if e == 0:
                            act.wait_ge(gt_done, 1)
                            act.activation(gt[:], ptr[0:EXPERTS], ACT.Copy).then_inc(gt_copied, 1)

                @block.vector
                def _(dve):
                    dve.wait_ge(x_in, 16)
                    for t in range(TT):
                        if t >= 1:
                            dve.wait_ge(turned, t)
                        dve.wait_ge(ln, 4 * t)
                        layer_norm(dve, ln, 4 * t, powed, t, xr[:, t], bst[:], bmv[:], rstd[:], xn[:])
                    n = [0]

                    def step(ins):
                        ins.then_inc(g_step, 1)
                        n[0] += 1
                        dve.wait_ge(g_step, n[0])

                    def over(a, e):
                        return a.rearrange("p (t o) -> p t o", o=1).broadcast_to([P, TT, e])

                    dve.wait_ge(g_done, 1)
                    scores = pgt[:, 0:TT * EXPERTS].rearrange("p (t e) -> p t e", e=EXPERTS)
                    step(dve.tensor_tensor(g[:], scores, gb[:].rearrange("p (o e) -> p o e", o=1).broadcast_to([P, TT, EXPERTS]),
                                           ALU.add))
                    step(dve.tensor_reduce(red[:], g[:], AX_X, ALU.max))
                    step(dve.tensor_tensor(g[:], g[:], over(red[:], EXPERTS), ALU.subtract))
                    dve.wait_ge(g_exp, 1)
                    step(dve.tensor_reduce(red[:], g[:], AX_X, ALU.add))
                    step(dve.reciprocal(red[:], red[:]))
                    step(dve.tensor_tensor(g[:], g[:], over(red[:], EXPERTS), ALU.mult))
                    for_e = g[:].rearrange("p t (o e) -> p t o e", o=1).broadcast_to([P, TT, EXPERTS, EXPERTS])
                    for_j = g[:].rearrange("p t (j o) -> p t j o", o=1).broadcast_to([P, TT, EXPERTS, EXPERTS])
                    dve.tensor_tensor(lt[:], for_e, for_j, ALU.is_lt)
                    step(dve.tensor_tensor(eq[:], for_e, for_j, ALU.is_equal))
                    step(dve.tensor_tensor(eq[:], eq[:], tri[:].rearrange("p (o j) e -> p o j e", o=1).broadcast_to(
                        [P, TT, EXPERTS, EXPERTS]), ALU.mult))
                    step(dve.tensor_tensor(lt[:], lt[:], eq[:], ALU.add))
                    step(dve.tensor_reduce(eq[:, :, 0, :], lt[:].rearrange("p t j e -> p t e j"), AX_X, ALU.add))
                    step(dve.scalar_tensor_tensor(out=g[:], in0=eq[:, :, 0, :], scalar=1.5, in1=g[:], op0=ALU.is_lt, op1=ALU.mult))
                    step(dve.tensor_reduce(red[:], g[:], AX_X, ALU.add))
                    dve.tensor_scalar(red[:], red[:], 1e-9, None, ALU.add).then_inc(gr_step, 1)
                    dve.wait_ge(gr_step, 1)
                    dve.reciprocal(red[:], red[:]).then_inc(gr_step, 1)
                    dve.wait_ge(gr_step, 2)
                    step(dve.tensor_tensor(g[:], g[:], over(red[:], EXPERTS), ALU.mult))
                    d = 0
                    for t in range(TT):
                        dve.wait_ge(down, d + 1)
                        dve.tensor_tensor(xr[:, t], pd[:, d % 3, 0:C], xr[:, t], ALU.add).then_inc(summed, 1)
                        d += 1
                    for e in range(EXPERTS):
                        for t in range(TT):
                            dve.wait_ge(down, d + 1)
                            dve.wait_ge(summed, d - TT + 1)
                            dve.scalar_tensor_tensor(out=xr[:, t], in0=pd[:, d % 3, 0:C], scalar=g[:, t, e:e + 1], in1=xr[:, t],
                                                     op0=ALU.mult, op1=ALU.add).then_inc(summed, 1)
                            d += 1
            s.clear()


def build(nc, a):
    def dram(name, shape):
        return nc.dram_tensor(name, shape, F32, kind="Internal").ap()

    qs, ks = dram("qs", (HEADS, HD, T)), dram("ks", (HEADS, HD, T))
    vs = dram("vs", (P, T // P, C))
    tve = dram("tve", (HEADS, SPAN, EXT, HD))
    us = dram("us", (HEADS, 8, P, NCH, 512))
    ws = dram("ws", (HEADS, B, WW, SPAN, N))
    os_ = dram("os_", (C, T))
    x2 = dram("x2", (T, C))
    with Scope(nc) as s:
        ident = s.sb("ident", [P, P])
        mhalf = s.sb("mhalf", [P, B])
        ident_step = s.sem("ident_step")
        with nc.Block() as block:
            @block.gpsimd
            def _(pool):
                pool.memset(mhalf[:], -0.5)
                pool.memset(ident[:], 1.0).then_inc(ident_step, 1)
                pool.wait_ge(ident_step, 1)
                pool.affine_select(out=ident[:], in_=ident[:], compare_op=ALU.is_equal, fill=0.0, base=0,
                                   pattern=[[-1, P]], channel_multiplier=1)
        norm_qkv(nc, a["x"], a["w_qkv"], a["tv"], mhalf, qs, ks, vs, tve)
        bias_tables(nc, a["tkq"], qs, ks, us, ws)
        attention(nc, ident, qs, ks, vs, us, ws, tve, os_)
        window(nc, a["xt"], a["w_proj"], a["b_proj"], a["mem_t"], a["mem"], a["qkv_w"], a["qkv_b"], a["qkb"],
               a["proj_w"], a["proj_b"], ident, mhalf, os_, x2)
        experts(nc, x2, a["gate_w"], a["gate_b"], a["w1"], a["b1"], a["w2"], a["b2"], ident, mhalf, a["out"])


def kernel(**inputs):
    import numpy as np
    import concourse.bacc as bacc
    from concourse.bass_utils import run_bass_kernel_spmd

    i = {k: np.asarray(v) for k, v in inputs.items()}
    x = i["x"].reshape(B, C, N)
    tk = i["L0_conv_table_k"].reshape(HEADS, SPAN, SPAN, HD)[:, ::-1, ::-1].transpose(0, 3, 1, 2)
    tq = i["L0_conv_table_q"].reshape(HEADS, SPAN, SPAN, HD)[:, :, ::-1].transpose(0, 3, 1, 2)
    arrays = {
        "x": x,
        "xt": x.transpose(0, 2, 1).reshape(T, C),
        "w_qkv": i["L0_conv_w_qkv"], "w_proj": i["L0_conv_w_proj"], "b_proj": i["L0_conv_b_proj"],
        "tkq": np.stack([tk, tq], axis=2),
        "tv": i["L0_conv_table_v"].reshape(HEADS, SPAN, SPAN, HD)[:, ::-1, ::-1],
        "mem": i["L1_attn_mem"],
        "mem_t": i["L1_attn_mem"].reshape(MEM, HEADS, HD).transpose(2, 1, 0),
        "qkv_w": i["L1_attn_qkv_w"], "qkv_b": i["L1_attn_qkv_b"],
        "qkb": i["L1_attn_qkv_b"][:2 * C].reshape(2, HEADS, HD).transpose(2, 0, 1),
        "proj_w": i["L1_attn_proj_w"], "proj_b": i["L1_attn_proj_b"],
        "gate_w": i["L1_ffn_gate_w"], "gate_b": i["L1_ffn_gate_b"],
        "w1": i["L1_ffn_w1"], "b1": i["L1_ffn_b1"].reshape(EXPERTS, HT, P).transpose(2, 0, 1),
        "w2": i["L1_ffn_w2"], "b2": i["L1_ffn_b2"],
    }
    nc = bacc.Bacc("TRN2", target_bir_lowering=False, num_devices=1)
    given, a = {}, {}
    for name, v in arrays.items():
        given[f"in_{name}"] = np.ascontiguousarray(v)
        a[name] = nc.dram_tensor(f"in_{name}", v.shape, F32, kind="ExternalInput").ap()
    a["out"] = nc.dram_tensor("out_tokens", (T, C), F32, kind="ExternalOutput").ap()
    build(nc, a)
    r = run_bass_kernel_spmd(nc, [given], core_ids=[0])
    y = r.results[0]["out_tokens"]
    return y.reshape(B, N, C).transpose(0, 2, 1).reshape(B, C, HH, WW)
```

```python
from contextlib import ExitStack

import concourse.bass as bass
from concourse import mybir

F32 = mybir.dt.float32
F32R = mybir.dt.float32r
ACT = mybir.ActivationFunctionType
ALU = mybir.AluOpType
AX_X = mybir.AxisListType.X

P = 128
B, C, HH, WW = 4, 384, 32, 32
N = HH * WW
T = B * N
CT = C // P
HEADS = 8
HD = C // HEADS
SPAN = 15
MAXD = 7
EXT = 2 * WW - 1
KP = 96
SCALE = float(HD) ** -0.5
BIG = 3.0e38
CH_ROWS = [4, 4, 4, 3]
NCH = len(CH_ROWS)
GROUP = 12
ROWF = WW
MEM = 64
WIN = 64
EXPERTS = 4
HID = 4 * C
HT = HID // P
MASKED = -1.0e30


class Scope:

    def __init__(self, nc):
        self.nc, self.ctx, self.sems = nc, ExitStack(), []

    def __enter__(self):
        return self

    def __exit__(self, *a):
        self.ctx.close()

    def sb(self, name, shape, dt=F32):
        return self.ctx.enter_context(self.nc.sbuf_tensor(name, shape, dt))

    def ps(self, name, shape, dt=F32):
        return self.ctx.enter_context(self.nc.psum_tensor(name, shape, dt))

    def sem(self, name):
        s = self.ctx.enter_context(self.nc.semaphore(name))
        self.sems.append(s)
        return s

    def clear(self):
        for s in self.sems:
            self.nc.gpsimd.sem_clear(s)
        self.nc.all_engine_barrier()


def norm_qkv(nc, x, w_qkv, tv, mhalf, qs, ks, vs, tve):
    with Scope(nc) as s:
        xc = s.sb("xc", [P, CT, B, N])
        w = s.sb("w0", [P, CT, 3 * C])
        grp = s.sb("grp", [P, P])
        stats = s.sb("stats", [P, CT, B, 2, 6])
        mv = s.sb("mv", [P, CT, B, 2])
        mean = s.sb("mean", [P, B])
        dev = s.sb("dev", [P, CT, B])
        var = s.sb("var", [P, CT, B])
        rstd = s.sb("rstd", [P, B])
        st = s.sb("st", [KP, 2, T])
        vst = s.sb("vst", [P, 2, 8, C])
        pg = s.ps("pg", [P, 2, 512])
        pq = s.ps("pq", [P, 4, 512])
        x_in = [s.sem(f"x_in{b}") for b in range(B)]
        w_in = s.sem("w_in")
        grp_step = s.sem("grp_step")
        stat_step = s.sem("stat_step")
        sums = s.sem("sums")
        normed = s.sem("normed")
        prod = s.sem("prod")
        copied_act = s.sem("copied_act")
        copied_dve = s.sem("copied_dve")
        stored = [s.sem(f"stored{i}") for i in range(2)]
        vstored = [s.sem(f"vstored{i}") for i in range(2)]
        ext_out = s.sem("ext_out")
        powed = s.sem("powed0")
        NB = T // 512
        PIECES = [(part, m) for part in range(2) for m in range(4)]
        NQK = len(PIECES) * NB
        NV = T // P

        with nc.Block() as block:
            @block.sync
            def _(sp):
                for b in range(B):
                    sp.dma_start(xc[:, :, b, :], x[b].rearrange("(p t) n -> p t n", t=CT)).then_inc(x_in[b], 16)
                sp.dma_start(w[:], w_qkv.rearrange("(p t) n -> p t n", t=CT)).then_inc(w_in, 16)
                lo = WW - 1 - MAXD
                for h in range(HEADS):
                    sp.dma_start(tve[h, :, lo:lo + SPAN, :], tv[h]).then_inc(ext_out, 16)
                    sp.dma_start(tve[h, :, 0:lo, :], tv[h, :, 0:1, :].broadcast_to([SPAN, lo, HD])).then_inc(ext_out, 16)
                    sp.dma_start(tve[h, :, lo + SPAN:EXT, :],
                                 tv[h, :, SPAN - 1:SPAN, :].broadcast_to([SPAN, EXT - lo - SPAN, HD])).then_inc(ext_out, 16)
                for i, (part, m) in enumerate(PIECES):
                    sp.wait_ge(copied_act, (i + 1) * NB // 2)
                    sp.wait_ge(copied_dve, (i + 1) * NB // 2)
                    dst = (qs if part == 0 else ks).rearrange("h d n -> (h d) n")
                    sp.dma_start(dst[m * KP:(m + 1) * KP, :], st[:, i % 2, :]).then_inc(stored[i % 2], 16)
                for i in range(NV // 8):
                    sp.wait_ge(copied_act, NQK // 2 + (i + 1) * 4)
                    sp.wait_ge(copied_dve, NQK // 2 + (i + 1) * 4)
                    sp.dma_start(vs[:, i * 8:(i + 1) * 8, :], vst[:, i % 2]).then_inc(vstored[i % 2], 16)
                for i in range(2):
                    sp.wait_ge(stored[i], 16 * len(PIECES) // 2)
                    sp.wait_ge(vstored[i], 16 * NV // 16)
                sp.wait_ge(ext_out, 16 * 3 * HEADS)

            @block.gpsimd
            def _(pool):
                pool.memset(grp[:], 1.0 / GROUP).then_inc(grp_step, 1)
                g3 = grp[:].rearrange("p (g r) -> p g r", r=4)
                pool.wait_ge(grp_step, 1)
                pool.affine_select(out=g3, in_=g3, compare_op=ALU.is_ge, fill=0.0, base=0,
                                   pattern=[[-4, 32], [0, 4]], channel_multiplier=1).then_inc(grp_step, 1)
                pool.wait_ge(grp_step, 2)
                pool.affine_select(out=g3, in_=g3, compare_op=ALU.is_ge, fill=0.0, base=3,
                                   pattern=[[4, 32], [0, 4]], channel_multiplier=-1).then_inc(grp_step, 1)
                pool.wait_ge(stat_step, 3 * CT * B + 5)
                pool.tensor_tensor(rstd[:], rstd[:], mhalf[:, 0:B], ALU.pow).then_inc(powed, 1)

            @block.vector
            def _(dve):
                n = 0
                for b in range(B):
                    dve.wait_ge(x_in[b], 16)
                    for t in range(CT):
                        for k in range(2):
                            dve.bn_stats(stats[:, t, b, k, :], xc[:, t, b, k * 512:(k + 1) * 512]).then_inc(stat_step, 1)
                            n += 1
                for b in range(B):
                    for t in range(CT):
                        dve.wait_ge(stat_step, 2 * CT * B)
                        dve.bn_aggr(mv[:, t, b, :], stats[:, t, b].rearrange("p k s -> p (k s)")).then_inc(stat_step, 1)
                        n += 1
                dve.wait_ge(sums, 1)
                dve.tensor_copy(mean[:], pg[:, 0, 0:B]).then_inc(stat_step, 1)
                n += 1
                dve.wait_ge(stat_step, n)
                dve.tensor_tensor(dev[:], mv[:, :, :, 0], mean[:].rearrange("p (o b) -> p o b", o=1).broadcast_to([P, CT, B]),
                                  ALU.subtract).then_inc(stat_step, 1)
                n += 1
                dve.wait_ge(stat_step, n)
                dve.tensor_tensor(dev[:], dev[:], dev[:], ALU.mult).then_inc(stat_step, 1)
                n += 1
                dve.wait_ge(stat_step, n)
                dve.tensor_tensor(var[:], mv[:, :, :, 1], dev[:], ALU.add).then_inc(stat_step, 1)
                n += 1
                dve.wait_ge(sums, 2)
                dve.tensor_scalar(rstd[:], pg[:, 1, 0:B], 1e-5, None, ALU.add).then_inc(stat_step, 1)
                dve.wait_ge(powed, 1)
                for b in range(B):
                    for t in range(CT):
                        dve.tensor_scalar(xc[:, t, b, :], xc[:, t, b, :], mean[:, b:b + 1], rstd[:, b:b + 1],
                                          ALU.subtract, ALU.mult).then_inc(normed, 1)
                for i, (part, m) in enumerate(PIECES):
                    for nb in range(1, NB, 2):
                        j = i * NB + nb
                        dve.wait_ge(prod, j + 1)
                        if i >= 2:
                            dve.wait_ge(stored[i % 2], 16 * (i // 2))
                        dve.tensor_scalar(st[:, i % 2, nb * 512:(nb + 1) * 512], pq[0:KP, j % 4, :],
                                          SCALE if part == 0 else 1.0, None, ALU.mult).then_inc(copied_dve, 1)
                for i in range(1, NV, 2):
                    dve.wait_ge(prod, NQK + i + 1)
                    if i >= 16:
                        dve.wait_ge(vstored[i // 8 % 2], 16 * (i // 16))
                    dve.tensor_copy(vst[:, i // 8 % 2, i % 8, :], pq[:, (NQK + i) % 4, 0:C]).then_inc(copied_dve, 1)

            @block.scalar
            def _(act):
                for i, (part, m) in enumerate(PIECES):
                    for nb in range(0, NB, 2):
                        j = i * NB + nb
                        act.wait_ge(prod, j + 1)
                        if i >= 2:
                            act.wait_ge(stored[i % 2], 16 * (i // 2))
                        act.activation(st[:, i % 2, nb * 512:(nb + 1) * 512], pq[0:KP, j % 4, :], ACT.Copy,
                                       scale=SCALE if part == 0 else 1.0).then_inc(copied_act, 1)
                for i in range(0, NV, 2):
                    act.wait_ge(prod, NQK + i + 1)
                    if i >= 16:
                        act.wait_ge(vstored[i // 8 % 2], 16 * (i // 16))
                    act.activation(vst[:, i // 8 % 2, i % 8, :], pq[:, (NQK + i) % 4, 0:C], ACT.Copy).then_inc(copied_act, 1)

            @block.tensor
            def _(pe):
                pe.wait_ge(grp_step, 3)
                pe.wait_ge(stat_step, 3 * CT * B)
                for t in range(CT):
                    mm = pe.matmul(pg[:, 0, 0:B], grp[:], mv[:, t, :, 0], start=(t == 0), stop=(t == CT - 1))
                mm.then_inc(sums, 1)
                pe.wait_ge(stat_step, 3 * CT * B + 4)
                for t in range(CT):
                    mm = pe.matmul(pg[:, 1, 0:B], grp[:], var[:, t, :], start=(t == 0), stop=(t == CT - 1))
                mm.then_inc(sums, 1)
                pe.wait_ge(w_in, 16)

                def free(j):
                    if j >= 4:
                        pe.wait_ge(copied_dve if j % 2 else copied_act, (j - 4) // 2 + 1)

                for i, (part, m) in enumerate(PIECES):
                    for nb in range(NB):
                        j = i * NB + nb
                        pe.wait_ge(normed, min(CT * (nb // 2 + 1), CT * B))
                        free(j)
                        for t in range(CT):
                            mm = pe.matmul(pq[0:KP, j % 4, :], w[:, t, part * C + m * KP:part * C + (m + 1) * KP],
                                           xc[:, t, nb // 2, nb % 2 * 512:nb % 2 * 512 + 512],
                                           start=(t == 0), stop=(t == CT - 1))
                        mm.then_inc(prod, 1)
                for i in range(NV):
                    free(NQK + i)
                    for t in range(CT):
                        mm = pe.matmul(pq[:, (NQK + i) % 4, 0:C], xc[:, t, i // 8, i % 8 * P:(i % 8 + 1) * P],
                                       w[:, t, 2 * C:3 * C], start=(t == 0), stop=(t == CT - 1))
                    mm.then_inc(prod, 1)
        s.clear()


def bias_tables(nc, tkq, qs, ks, us, ws):
    with Scope(nc) as s:
        qk = s.sb("qk", [KP, 2, B, HH, WW])
        tab = s.sb("tab", [HD, 2, SPAN, SPAN])
        ext = s.sb("ext", [HD, 2, SPAN, EXT])
        win = s.sb("win", [KP, 2, WW, P])
        st = [s.sb(f"bst{i}", [P, B * HH, WW]) for i in range(4)]
        win_dve = s.sem("win_dve")
        win_act = s.sem("win_act")
        pb = s.ps("pb", [P, 4, 4, P])
        zeroed = s.sem("zeroed")
        qk_in = s.sem("qk_in")
        tab_in = s.sem("tab_in")
        extended = s.sem("extended")
        prod = s.sem("bprod")
        copied_act = s.sem("bcopied_act")
        copied_dve = s.sem("bcopied_dve")
        out = [s.sem(f"bout{i}") for i in range(4)]

        with nc.Block() as block:
            @block.vector
            def _(dve):
                dve.memset(qk[:].rearrange("p a b y x -> p (a b y x)"), 0.0)
                dve.memset(win[:].rearrange("p a x e -> p (a x e)"), 0.0)

        lo = WW - 1 - MAXD
        UNITS = [(which, c) for c in range(NCH) for which in range(2)]

        def window_of(u):
            which, c = UNITS[u]
            rows = CH_ROWS[c]
            src = ext[:, which, c * 4:c * 4 + rows, 0:WW]
            src = bass.AP(tensor=src.tensor, offset=src.offset, ap=[list(src.ap[0]), [1, WW], [EXT, rows], [1, WW]])
            return win[0:HD, u % 2, :, 0:rows * WW].rearrange("d x (r e) -> d x r e", r=rows), src

        def windows(eng, u, part):
            if u >= 2:
                eng.wait_ge(prod, (u - 1) * 8)
            dst, src = window_of(u)
            if part == "dve":
                eng.tensor_copy(dst[:, 0:DVE_COLS], src[:, 0:DVE_COLS]).then_inc(win_dve, 1)
            else:
                eng.activation(dst[:, DVE_COLS:WW], src[:, DVE_COLS:WW], ACT.Copy).then_inc(win_act, 1)

        DVE_COLS = 20

        def evac(eng, odd):
            for u, (which, c) in enumerate(UNITS):
                if u == 0:
                    windows(eng, 0, "dve" if odd else "act")
                if u + 1 < len(UNITS):
                    windows(eng, u + 1, "dve" if odd else "act")
                n = CH_ROWS[c] * 32
                for q in range(odd, 8, 2):
                    eng.wait_ge(prod, u * 8 + q + 1)
                    if u >= 4:
                        eng.wait_ge(out[u % 4], 16 * (1 if which == 0 else CH_ROWS[c - 2]))
                    dst = st[u % 4][0:n, :, q * 4:(q + 1) * 4].rearrange("p t x -> p x t")
                    src = pb[0:n, (u * 8 + q) % 4]
                    if odd:
                        eng.tensor_copy(dst, src).then_inc(copied_dve, 1)
                    else:
                        eng.activation(dst, src, ACT.Copy).then_inc(copied_act, 1)

        with nc.Fori(0, HEADS) as h:
            with nc.Block() as block:
                @block.sync
                def _(sp):
                    sp.dma_start(tab[:], tkq[bass.ds(h, 1)].rearrange("h d a r e -> (h d) a r e")).then_inc(tab_in, 16)
                    for which, src in ((0, qs), (1, ks)):
                        sp.dma_start(qk[0:HD, which].rearrange("d b y x -> d (b y x)"),
                                     src[bass.ds(h, 1)].rearrange("h d n -> (h d) n")).then_inc(qk_in, 16)
                    for u, (which, c) in enumerate(UNITS):
                        rows = CH_ROWS[c]
                        sp.wait_ge(copied_act, 4 * (u + 1))
                        sp.wait_ge(copied_dve, 4 * (u + 1))
                        if which == 0:
                            sp.dma_start(us[bass.ds(h, 1), :, 0:rows * 32, c, :].rearrange("h g p f -> p (h g) f"),
                                         st[u % 4][0:rows * 32].rearrange("p (g f) x -> p g (f x)", g=8)).then_inc(out[u % 4], 16)
                        else:
                            for r in range(rows):
                                sp.dma_start(ws[bass.ds(h, 1), :, :, c * 4 + r, :].rearrange("h b x f -> x (h b) f"),
                                             st[u % 4][r * 32:(r + 1) * 32].rearrange("p (b y) x -> p b (y x)", b=B)).then_inc(out[u % 4], 16)
                    sp.wait_ge(out[0], 32)
                    sp.wait_ge(out[2], 32)
                    sp.wait_ge(out[1], 16 * 8)
                    sp.wait_ge(out[3], 16 * 7)

                @block.vector
                def _(dve):
                    dve.wait_ge(tab_in, 16)
                    for a, fac in ((0, 1.0), (1, SCALE)):
                        dve.tensor_scalar(ext[0:HD, a, :, lo:lo + SPAN], tab[:, a], fac, None, ALU.mult).then_inc(extended, 1)
                        dve.tensor_scalar(ext[0:HD, a, :, 0:lo], tab[:, a, :, 0:1].broadcast_to([HD, SPAN, lo]),
                                          fac, None, ALU.mult).then_inc(extended, 1)
                        dve.tensor_scalar(ext[0:HD, a, :, lo + SPAN:EXT],
                                          tab[:, a, :, SPAN - 1:SPAN].broadcast_to([HD, SPAN, EXT - lo - SPAN]),
                                          fac, None, ALU.mult).then_inc(extended, 1)
                    dve.wait_ge(extended, 6)
                    evac(dve, 1)

                @block.scalar
                def _(act):
                    act.wait_ge(extended, 6)
                    evac(act, 0)

                @block.tensor
                def _(pe):
                    pe.wait_ge(qk_in, 32)
                    for u, (which, c) in enumerate(UNITS):
                        n = CH_ROWS[c] * 32
                        pe.wait_ge(win_dve, u + 1)
                        pe.wait_ge(win_act, u + 1)
                        for q in range(8):
                            j = u * 8 + q
                            if j >= 4:
                                pe.wait_ge(copied_dve if j % 2 else copied_act, (j - 4) // 2 + 1)
                            for i in range(4):
                                x = q * 4 + i
                                mov = qk[:, which, :, :, x]
                                if which == 0:
                                    mov = mov.rearrange("d b y -> d y b")
                                mm = pe.matmul(pb[0:n, j % 4, i, :], win[:, u % 2, WW - 1 - x, 0:n], mov, start=True, stop=True)
                            mm.then_inc(prod, 1)
            s.clear()


def attention(nc, ident, qs, ks, vs, us, ws, tve, os_):
    GR = 4
    NG = HH // GR
    HALF = HH // 2
    PADR = MAXD
    PRB = 3
    with Scope(nc) as s:
        kk = s.sb("kk", [KP, B, N])
        qg = s.sb("qg", [KP, 2, B, GR * WW])
        ug = s.sb("ug", [P, 2, NCH, GR * P])
        wt = s.sb("wt", [P, SPAN * HH, WW])
        vh = s.sb("vh", [P, T // P, HD])
        tvx = s.sb("tvx", [P, NCH, WW, HD])
        pr = s.sb("pr", [P, PRB * (HH + PADR) + PADR, WW])
        edge_lo = s.sb("edge_lo", [P, 2, 4, WW])
        edge_hi = s.sb("edge_hi", [P, 2, 3, WW])
        pt = s.sb("pt", [P, 8, GR, P])
        rt = s.sb("rt", [P, NCH, HALF, P])
        oh = s.sb("oh", [HD, B, HALF, WW])
        strip_lo = s.sb("strip_lo", [P, HH - 4, WW])
        strip_hi = s.sb("strip_hi", [P, HH - 5, WW])
        nmax = s.sb("nmax", [P, 2, 3])
        rsum = s.sb("rsum", [P, 2])
        rinv = s.sb("rinv", [P, 2])
        ps = s.ps("ps_s", [P, 2, 2, 512])
        ptp = s.ps("ptp", [P, 2, 4, P])
        rtp = s.ps("rtp", [P, 4, P])
        po = s.ps("po", [P, 512])

        strips = s.sem("strips")
        pads = s.sem("pads")
        v_in, tv_in = s.sem("v_in"), s.sem("tv_in")
        EARLY = [((1, SPAN), (0, 8), 14), ((1, SPAN), (8, 16), 22), ((SPAN - 1, SPAN), (16, HH), 25)]
        LATE = [((0, 1), (0, HH), MAXD), ((1, SPAN - 1), (16, 24), 10), ((1, SPAN - 1), (24, HH), 18)]
        late_in = [s.sem(f"late_in{i}") for i in range(len(LATE))]
        next_in = s.sem("next_in")
        grp_in = [s.sem(f"grp_in{i}") for i in range(2)]
        scored = s.sem("scored")
        biased = s.sem("biased")
        bias_step = s.sem("bias_step")
        exped = s.sem("exped")
        norm_step = s.sem("norm_step")
        normed = s.sem("normed2")
        turned = s.sem("turned")
        turned_rel = s.sem("turned_rel")
        pt_copied = s.sem("pt_copied")
        rt_copied = s.sem("rt_copied")
        vprod = s.sem("vprod")
        o_step = s.sem("o_step")
        o_out = s.sem("o_out")

        with nc.Block() as block:
            @block.vector
            def _(dve):
                dve.memset(kk[:].rearrange("p b n -> p (b n)"), 0.0)
                dve.memset(qg[:].rearrange("p a b n -> p (a b n)"), 0.0)
                dve.memset(pr[:].rearrange("p y x -> p (y x)"), 0.0)
                for i in range(HH - 4):
                    k = max(0, i - (HH - 8))
                    dve.tensor_copy(strip_lo[:, i, :], ident[:, k * 32:(k + 1) * 32])
                for i in range(HH - 5):
                    k = min(i, 2)
                    dve.tensor_copy(strip_hi[:, i, :], ident[:, k * 32:(k + 1) * 32])

        def rows_of(y, a, b):
            r = y % PRB * (HH + PADR)
            return pr[:, r + a:r + b, :]

        def spans(y):
            out = []
            if y - MAXD >= 0:
                out.append((0, y - MAXD + 1, None, 0))
            a, b = max(0, y - MAXD + 1), min(HH, y + MAXD)
            out.append((a, b, a - y + MAXD, 1))
            if y + MAXD < HH:
                out.append((y + MAXD, HH, None, SPAN - 1))
            return out

        NSP = [len(spans(y)) for y in range(HH)]

        def load_table(sp, h, part, done):
            (a0, a1), (y0, y1), _ = part
            dst = wt[:].rearrange("p (a y) x -> p a (y x)", a=SPAN)[:, a0:a1, y0 * WW:y1 * WW]
            sp.dma_start(dst, ws[bass.ds(h, 1)].rearrange("h b x a f -> (h b x) a f")[:, a0:a1, y0 * WW:y1 * WW]
                         ).then_inc(done, 16)

        def load_keys(sp, h, done):
            sp.dma_start(kk[0:HD].rearrange("d b n -> d (b n)"),
                         ks[bass.ds(h, 1)].rearrange("h d n -> (h d) n")).then_inc(done, 16)

        def load_group(sp, h, g, done):
            sp.dma_start(qg[0:HD, g % 2], qs[bass.ds(h, 1)].rearrange("h d (b n) -> (h d) b n", b=B)[
                :, :, g * GR * WW:(g + 1) * GR * WW]).then_inc(done, 16)
            sp.dma_start(ug[:, g % 2, 0:3], us[bass.ds(h, 1), g, :, 0:3, :].rearrange("h p c f -> (h p) c f")).then_inc(done, 16)
            sp.dma_start(ug[0:96, g % 2, 3], us[bass.ds(h, 1), g, 0:96, 3, :].rearrange("h p f -> (h p) f")).then_inc(done, 16)

        NEXT_DMAS = len(EARLY) + 4
        with nc.Block() as block:
            @block.sync
            def _(sp):
                load_keys(sp, 0, next_in)
                load_group(sp, 0, 0, next_in)
                for part in EARLY:
                    load_table(sp, 0, part, next_in)
                sp.wait_ge(next_in, 16 * NEXT_DMAS)
        s.clear()

        def head(h, last):
            with nc.Block() as block:
                @block.sync
                def _(sp):
                    load_table(sp, h, LATE[0], late_in[0])
                    load_group(sp, h, 1, grp_in[1])
                    sp.dma_start(vh[:], vs[:, :, bass.ds(h * HD, HD)]).then_inc(v_in, 16)
                    load_table(sp, h, LATE[1], late_in[1])
                    load_table(sp, h, LATE[2], late_in[2])
                    for c in range(NCH):
                        for r in range(CH_ROWS[c]):
                            src = tve[bass.ds(h, 1), c * 4 + r].rearrange("h e d -> (h e) d")
                            sp.dma_start(tvx[r * 32:(r + 1) * 32, c], skewed(src)).then_inc(tv_in, 16)

                    def store(half):
                        sp.wait_ge(o_step, (half + 1) * (NG // 2 + 2))
                        sp.dma_start(os_[bass.ds(h * HD, HD)].rearrange("c (b n) -> c b n", b=B)[
                            :, :, half * HALF * WW:(half + 1) * HALF * WW],
                            oh[:].rearrange("d b y x -> d b (y x)")).then_inc(o_out, 16)

                    def early(i):
                        if not last:
                            sp.wait_ge(biased, EARLY[i][2] + 1)
                            load_table(sp, h + 1, EARLY[i], next_in)

                    for g in range(2, NG):
                        if g == 5:
                            early(0)
                        if g == HALF // GR + 2:
                            store(0)
                        if g == NG - 1:
                            early(1)
                        sp.wait_ge(scored, GR * (g - 1))
                        load_group(sp, h, g, grp_in[g % 2])
                    early(2)
                    if not last:
                        sp.wait_ge(scored, GR * (NG - 1))
                        load_group(sp, h + 1, 0, next_in)
                        sp.wait_ge(scored, HH)
                        load_keys(sp, h + 1, next_in)
                    store(1)
                    sp.wait_ge(o_out, 32)
                    if not last:
                        sp.wait_ge(next_in, 16 * NEXT_DMAS)

                @block.tensor
                def _(pe):
                    def scores(y):
                        g = y // GR
                        if y % GR == 0 and g >= 1:
                            pe.wait_ge(grp_in[g % 2], 48 * ((g + 1) // 2))
                        if y >= 2:
                            pe.wait_ge(biased, y - 1)
                        for half in range(2):
                            for b in range(B):
                                pe.matmul(ps[b * 32:(b + 1) * 32, y % 2, half, :],
                                          qg[:, g % 2, b, y % GR * WW:(y % GR + 1) * WW],
                                          kk[:, b, half * 512:(half + 1) * 512],
                                          start=True, stop=False, skip_group_check=True)
                        for c, (a, b, strip, off, n) in enumerate([
                                (0, y - 3, strip_lo, HH - 4 - (y - 3), P),
                                (y - 3, y + 1, None, 0, P),
                                (y + 1, y + 5, None, 0, P),
                                (y + 5, HH, strip_hi, 0, 96)]):
                            lo, hi = max(a, 0), min(b, HH)
                            for p0, p1 in ((lo, min(hi, 16)), (max(lo, 16), hi)):
                                if p0 >= p1:
                                    continue
                                if strip is None:
                                    mov = ident[0:n, (p0 - a) * 32:(p1 - a) * 32]
                                else:
                                    mov = strip[0:n, off + p0 - a:off + p1 - a, :]
                                mm = pe.matmul(ps[:, y % 2, p0 // 16, p0 % 16 * 32:(p0 % 16 + p1 - p0) * 32],
                                               ug[0:n, g % 2, c, y % GR * P:(y % GR + 1) * P], mov,
                                               start=False, stop=True, skip_group_check=True)
                        mm.then_inc(scored, 1)

                    def turn(y):
                        pe.wait_ge(normed, y + 1)
                        for i in range(2):
                            if y >= 1:
                                pe.wait_ge(pt_copied, 2 * y - 1 + i)
                            for k in range(4):
                                r0 = PADR + (i * 4 + k) * 4
                                mm = pe.matmul(ptp[:, i, k, :], rows_of(y, r0, r0 + 4), ident[:], start=True,
                                               stop=True, is_transpose=True)
                            mm.then_inc(turned, 1)
                        if y >= 1:
                            pe.wait_ge(rt_copied, y)
                        for c, rows in enumerate((edge_lo[:, y % 2], rows_of(y, y + 4, y + 8),
                                                  rows_of(y, y + 8, y + 12), edge_hi[:, y % 2])):
                            n = CH_ROWS[c] * 32
                            mm = pe.matmul(rtp[0:n, c, :], rows, ident[:], start=True, stop=True, is_transpose=True)
                        mm.then_inc(turned_rel, 1)

                    def free(n):
                        if n >= 1:
                            pe.wait_ge(o_step, n)

                    def values(g, n):
                        pe.wait_ge(pt_copied, 2 * GR * (g + 1))
                        if g == 0:
                            pe.wait_ge(v_in, 16)
                        free(n)
                        for pair in range(B // 2):
                            for k in range(8):
                                for odd in range(2):
                                    b = 2 * pair + odd
                                    mm = pe.matmul(po[odd * 64:odd * 64 + HD, pair * P:(pair + 1) * P], vh[:, b * 8 + k, :],
                                                   pt[:, k, :, b * 32:(b + 1) * 32], start=(k == 0), stop=(k == 7))
                        mm.then_inc(vprod, 1)

                    def table_values(half, n):
                        pe.wait_ge(rt_copied, HALF * (half + 1))
                        if half == 0:
                            pe.wait_ge(tv_in, 16 * SPAN)
                        for q in range(2):
                            free(n + q)
                            for i in range(8):
                                for c in range(NCH):
                                    rows = CH_ROWS[c] * 32
                                    for odd in range(2):
                                        x = q * 16 + 2 * i + odd
                                        mov = rt[0:rows, c].rearrange("p y (b x) -> p y b x", b=B)[:, :, :, x]
                                        mm = pe.matmul(po[odd * 64:odd * 64 + HD, i * 64:(i + 1) * 64],
                                                       tvx[0:rows, c, WW - 1 - x, :], mov,
                                                       start=(c == 0), stop=(c == NCH - 1))
                            mm.then_inc(vprod, 1)

                    n = 0
                    for y in range(HH + 2):
                        if y < HH:
                            scores(y)
                        t = y - 2
                        if t > 0 and t % GR == 0:
                            values(t // GR - 1, n)
                            n += 1
                        if t == HALF:
                            table_values(0, n)
                            n += 2
                        if t >= 0:
                            turn(t)
                    values(NG - 1, n)
                    table_values(1, n + 1)

                @block.vector
                def _(dve):
                    def bias(y):
                        dve.wait_ge(scored, y + 1)
                        if y >= PRB:
                            dve.wait_ge(turned_rel, y - PRB + 1)
                        for i, (_, _, tile) in enumerate(LATE):
                            if y == tile:
                                dve.wait_ge(late_in[i], 16)
                        for i, (a, b, r, row) in enumerate(spans(y)):
                            if r is None:
                                tabl = wt[:, row * HH + a:row * HH + b, :]
                            else:
                                r0 = r * HH + a
                                tabl = wt[:, r0:r0 + (b - a - 1) * (HH + 1) + 1:HH + 1, :]
                            if i:
                                dve.wait_ge(bias_step, sum(k - 1 for k in NSP[:y]) + i)
                            ins = dve.tensor_tensor_reduce(
                                rows_of(y, PADR + a, PADR + b),
                                ps[:, y % 2].rearrange("p a f -> p (a f)")[:, a * 32:b * 32].rearrange("p (y x) -> p y x", x=WW),
                                tabl, -1.0, nmax[:, y % 2, i - 1:i] if i else BIG, ALU.add, ALU.min,
                                nmax[:, y % 2, i:i + 1])
                            ins.then_inc(biased if i == NSP[y] - 1 else bias_step, 1)

                    def normalise(y):
                        dve.wait_ge(exped, y + 1)
                        dve.reciprocal(rinv[:, y % 2:y % 2 + 1], rsum[:, y % 2:y % 2 + 1]).then_inc(norm_step, 1)
                        dve.wait_ge(norm_step, 2 * y + 1)
                        dve.tensor_scalar(rows_of(y, PADR, PADR + HH), rows_of(y, PADR, PADR + HH),
                                          rinv[:, y % 2:y % 2 + 1], None, ALU.mult).then_inc(norm_step, 1)
                        dve.wait_ge(norm_step, 2 * y + 2)
                        if y >= 2:
                            dve.wait_ge(turned_rel, y - 1)
                        dve.tensor_reduce(edge_lo[:, y % 2, 0, :], rows_of(y, 0, y + 1).rearrange("p y x -> p x y"),
                                          AX_X, ALU.add)
                        dve.tensor_copy(edge_lo[:, y % 2, 1:4, :], rows_of(y, y + 1, y + 4))
                        dve.tensor_reduce(edge_hi[:, y % 2, 2, :],
                                          rows_of(y, y + 2 * PADR, HH + 2 * PADR).rearrange("p y x -> p x y"),
                                          AX_X, ALU.add)
                        dve.tensor_copy(edge_hi[:, y % 2, 0:2, :], rows_of(y, y + 12, y + 14)).then_inc(normed, 1)

                    def out_values(g, n):
                        dve.wait_ge(vprod, n + 1)
                        if g == NG // 2:
                            dve.wait_ge(o_out, 16)
                        y0 = g * GR % HALF
                        for odd in range(2):
                            ins = dve.tensor_copy(oh[:, odd:B:2, y0:y0 + GR, :],
                                                  po[odd * 64:odd * 64 + HD, 0:2 * P].rearrange("d (b y x) -> d b y x", b=2, y=GR))
                        ins.then_inc(o_step, 1)

                    def out_table(n):
                        for q in range(2):
                            dve.wait_ge(vprod, n + q + 1)
                            dve.wait_ge(o_step, n + q)
                            for odd in range(2):
                                o = oh[:, :, :, q * 16 + odd:(q + 1) * 16:2].rearrange("d b y x -> d x y b")
                                ins = dve.tensor_tensor(o, po[odd * 64:odd * 64 + HD].rearrange("d (x y b) -> d x y b", x=8, b=B), o,
                                                        ALU.add)
                            ins.then_inc(o_step, 1)

                    n = 0
                    for y in range(HH + 2):
                        t = y - 2
                        if t > 0 and t % GR == 0:
                            out_values(t // GR - 1, n)
                            n += 1
                        if t == HALF:
                            out_table(n)
                            n += 2
                        if y < HH:
                            bias(y)
                        if 1 <= y <= HH:
                            normalise(y - 1)
                    out_values(NG - 1, n)
                    out_table(n + 1)

                @block.scalar
                def _(act):
                    for y in range(HH + 1):
                        if y < HH:
                            act.wait_ge(biased, y + 1)
                            if y >= 2:
                                act.wait_ge(norm_step, 2 * (y - 2) + 1)
                            act.activation(rows_of(y, PADR, PADR + HH), rows_of(y, PADR, PADR + HH), ACT.Exp,
                                           bias=nmax[:, y % 2, NSP[y] - 1:NSP[y]], scale=-1.0,
                                           accum_out=rsum[:, y % 2:y % 2 + 1]).then_inc(exped, 1)
                        t = y - 1
                        if t < 0:
                            continue
                        for i in range(2):
                            act.wait_ge(turned, 2 * t + i + 1)
                            act.activation(pt[:, i * 4:(i + 1) * 4, t % GR, :], ptp[:, i], ACT.Copy).then_inc(pt_copied, 1)
                        act.wait_ge(turned_rel, t + 1)
                        act.activation(rt[:, 0:3, t % HALF, :], rtp[:, 0:3], ACT.Copy)
                        act.activation(rt[0:96, 3, t % HALF, :], rtp[0:96, 3], ACT.Copy).then_inc(rt_copied, 1)
            s.clear()

        with nc.Fori(0, HEADS - 1) as h:
            head(h, False)
        head(HEADS - 1, True)


def skewed(src):
    row = list(src.ap[-2])[0]
    return bass.AP(tensor=src.tensor, offset=src.offset, ap=[[row, WW], [row, WW], [1, HD]])


def layer_norm(dve, step, n, powed, m, x, bst, bmv, rstd, xn):
    dve.bn_stats(bst, x).then_inc(step, 1)
    dve.wait_ge(step, n + 1)
    dve.bn_aggr(bmv, bst).then_inc(step, 1)
    dve.wait_ge(step, n + 2)
    dve.tensor_scalar(rstd, bmv[:, 1:2], 1e-5, None, ALU.add).then_inc(step, 1)
    dve.wait_ge(powed, m + 1)
    dve.tensor_scalar(xn, x, bmv[:, 0:1], rstd, ALU.subtract, ALU.mult).then_inc(step, 1)


def window(nc, xt, w_proj0, b_proj0, mem_t, mem, qkv_w, qkv_b, qkb, proj_w, proj_b, ident, mhalf, os_, x2):
    NT = N // P
    KEYS = MEM + WIN + P
    with Scope(nc) as s:
        wp0 = s.sb("wp0", [P, CT, C])
        wqk = s.sb("wqk", [P, CT, 2, HEADS, 64])
        wv = s.sb("wv", [P, CT, C])
        wp1 = s.sb("wp1", [P, CT, C])
        brow = s.sb("brow", [P, 3, C])
        bqk = s.sb("bqk", [HD, 2, HEADS])
        mask = s.sb("mask", [P, 2, KEYS])
        oin = s.sb("oin", [P, 2, CT, P])
        xin = s.sb("xin", [P, 2, C])
        x1 = s.sb("x1", [P, NT, C])
        xn = s.sb("xn", [P, 2, C])
        xnt = s.sb("xnt", [P, CT, N])
        bst = s.sb("bst", [P, 6])
        rstd = s.sb("rstdw", [P, 1])
        powed = s.sem("powedw")
        bmv = s.sb("bmv", [P, 2])
        qt = s.sb("qt", [KP, HEADS, N])
        kb = s.sb("kb", [KP, NT, HEADS, KEYS])
        vv = s.sb("vv", [P, NT, C])
        vp = s.sb("vp", [P, NT, C])
        pr = s.sb("pw", [P, 2, 4, KEYS])
        nmax = s.sb("nmaxw", [P, 2, 4])
        rsum = s.sb("rsumw", [P, 3, HEADS])
        rinv = s.sb("rinvw", [P, 2, HEADS])
        pt = s.sb("ptw", [P, 2, 4, P])
        yn = s.sb("yn", [P, C])
        yt = s.sb("yt", [P, CT, P])
        xo = s.sb("xo", [P, 2, C])
        pm = s.ps("pm", [P, 2, 512])
        pqk = s.ps("pqk", [P, 2, 512])
        psc = s.ps("psc", [P, 2, 2, KEYS])
        ptr = s.ps("ptr", [P, 2, 4, P])

        wl = s.sem("wl")
        zer = s.sem("zer")
        msk = s.sem("msk")
        bq_scaled = s.sem("bq_scaled")
        tile_in = [s.sem(f"tile_in{i}") for i in range(2)]
        xb_added = s.sem("xb_added")
        proj0 = s.sem("proj0")
        v_done = s.sem("v_done")
        y_done = s.sem("y_done")
        y_turned = s.sem("y_turned")
        proj1 = s.sem("proj1")
        f_step = s.sem("f_step")
        xn_turned = s.sem("xn_turned")
        xnt_copied = s.sem("xnt_copied")
        qk_done = s.sem("qk_done")
        qk_act = s.sem("qk_act")
        qk_dve = s.sem("qk_dve")
        v_added = s.sem("v_added")
        s_done = s.sem("s_done")
        masked = s.sem("masked")
        exped = s.sem("exped_w")
        p_turned = s.sem("p_turned")
        p_copied = s.sem("p_copied")
        y_step = s.sem("y_step")
        y_copied = s.sem("y_copied")
        x2_added = s.sem("x2_added")
        x2_step = s.sem("x2_step")
        x2_half = s.sem("x2_half")
        x2_out = [s.sem(f"x2_out{i}") for i in range(2)]

        with nc.Block() as block:
            @block.vector
            def _(dve):
                dve.memset(wqk[:].rearrange("p t a h e -> p (t a h e)"), 0.0).then_inc(zer, 1)
                dve.memset(kb[:].rearrange("p t h k -> p (t h k)"), 0.0).then_inc(zer, 1)
                dve.memset(vp[:].rearrange("p t c -> p (t c)"), 0.0).then_inc(zer, 1)
                dve.memset(qt[:].rearrange("p h n -> p (h n)"), 0.0)
                dve.wait_ge(wl, 16 * 20)
                dve.tensor_scalar(bqk[:, 0], bqk[:, 0], SCALE, None, ALU.mult)

            @block.gpsimd
            def _(pool):
                pool.memset(mask[:].rearrange("p a k -> p (a k)"), 0.0).then_inc(msk, 1)
                pool.wait_ge(msk, 1)
                pool.affine_select(out=mask[:, 0, MEM:MEM + WIN], in_=mask[:, 0, MEM:MEM + WIN], compare_op=ALU.is_ge,
                                   fill=MASKED, base=0, pattern=[[1, WIN]], channel_multiplier=-1)
                pool.memset(mask[:, 1, MEM:MEM + WIN], MASKED)
                for a in range(2):
                    m = mask[:, a, MEM + WIN:KEYS]
                    pool.affine_select(out=m, in_=m, compare_op=ALU.is_ge, fill=MASKED, base=0,
                                       pattern=[[-1, P]], channel_multiplier=1).then_inc(msk, 1)
                    pool.wait_ge(msk, 2 + 2 * a)
                    pool.affine_select(out=m, in_=m, compare_op=ALU.is_ge, fill=MASKED, base=WIN,
                                       pattern=[[1, P]], channel_multiplier=-1).then_inc(msk, 1)

            @block.sync
            def _(sp):
                def load(dst, src):
                    sp.dma_start(dst, src).then_inc(wl, 16)

                load(wp0[:], w_proj0.rearrange("(t p) n -> p t n", p=P))
                load(wv[:], qkv_w[:, 2 * C:3 * C].rearrange("(t p) n -> p t n", p=P))
                load(wp1[:], proj_w.rearrange("(t p) n -> p t n", p=P))
                load(brow[:, 0], b_proj0.rearrange("(o n) -> o n", o=1).broadcast_to([P, C]))
                load(brow[:, 1], qkv_b[2 * C:3 * C].rearrange("(o n) -> o n", o=1).broadcast_to([P, C]))
                load(brow[:, 2], proj_b.rearrange("(o n) -> o n", o=1).broadcast_to([P, C]))
                load(bqk[:], qkb)
                sp.wait_ge(zer, 1)
                for t in range(CT):
                    for a in range(2):
                        load(wqk[:, t, a, :, 0:HD], qkv_w[t * P:(t + 1) * P, a * C:(a + 1) * C].rearrange("p (h d) -> p h d", d=HD))
                sp.wait_ge(zer, 3)
                for t in range(4):
                    load(kb[0:HD, 2 * t:2 * t + 1, :, 0:MEM].rearrange("d o h k -> d (o h) k"), mem_t)
                for t in range(2):
                    load(vp[0:MEM, 4 * t], mem)
                load(vp[0:MEM, 2], mem)
                sp.wait_ge(wl, 16 * 20)

        with nc.Block() as block:
            @block.scalar
            def _(act):
                for t in range(4):
                    act.activation(kb[0:HD, 2 * t + 1, :, 0:MEM], kb[0:HD, 2 * t, :, 0:MEM], ACT.Copy)
                for t, u in ((1, 0), (3, 2), (5, 4)):
                    act.activation(vp[0:MEM, t], vp[0:MEM, u], ACT.Copy)

            @block.vector
            def _(dve):
                for t, u in ((6, 4), (7, 4)):
                    dve.tensor_copy(vp[0:MEM, t], vp[0:MEM, u])

        def turn_xn(pe, t):
            pe.wait_ge(f_step, 5 * (t + 1))
            if t >= 2:
                pe.wait_ge(xnt_copied, t - 1)
            for c in range(CT):
                mm = pe.matmul(ptr[:, t % 2, c, :], xn[:, t % 2, c * P:(c + 1) * P], ident[:], start=True, stop=True,
                               is_transpose=True)
            mm.then_inc(xn_turned, 1)

        def values_in(pe, t):
            pe.wait_ge(xnt_copied, t + 1)
            if t >= 2:
                pe.wait_ge(v_added, t - 1)
            for c in range(CT):
                mm = pe.matmul(pqk[:, t % 2, 0:C], xnt[:, c, t * P:(t + 1) * P], wv[:, c], start=(c == 0), stop=(c == CT - 1))
            mm.then_inc(v_done, 1)

        U = 2 * NT

        def scores(pe, u):
            t, q = divmod(u, 2)
            for k in range(4):
                if u >= 1 and k % 2 == 0:
                    pe.wait_ge(masked, 4 * (u - 1) + k + 2)
                h = q * 4 + k
                mm = pe.matmul(psc[:, k // 2, k % 2, :], qt[:, h, t * P:(t + 1) * P], kb[:, t, h, :],
                               start=True, stop=True)
                if k % 2 == 1:
                    mm.then_inc(s_done, 1)

        def turn_probs(pe, u):
            for k in range(4):
                pe.wait_ge(exped, 4 * u + k + 1)
                if k % 2 == 0 and u >= 1:
                    pe.wait_ge(p_copied, 2 * (u - 1) + k // 2 + 1)
                for c in range(2):
                    mm = pe.matmul(ptr[:, k // 2, k % 2 * 2 + c, :], pr[:, u % 2, k, c * P:(c + 1) * P], ident[:],
                                   start=True, stop=True, is_transpose=True)
                if k % 2 == 1:
                    mm.then_inc(p_turned, 1)

        def value_sums(pe, u):
            t, q = divmod(u, 2)
            if q == 0 and t >= 1:
                pe.wait_ge(y_step, t)
            for i in range(2):
                pe.wait_ge(p_copied, 2 * u + i + 1)
                for k in (2 * i, 2 * i + 1):
                    h = q * 4 + k
                    for c in range(2):
                        mm = pe.matmul(pm[:, 0, h * HD:(h + 1) * HD], pt[:, i, k % 2 * 2 + c, :],
                                       (vp if c == 0 else vv)[:, t, h * HD:(h + 1) * HD], start=(c == 0), stop=(c == 1),
                                       skip_group_check=True)
                mm.then_inc(y_done, 1)

        def turn_y(pe, t):
            pe.wait_ge(y_step, t + 1)
            if t >= 1:
                pe.wait_ge(y_copied, t)
            for c in range(CT):
                mm = pe.matmul(pqk[:, 0, c * P:(c + 1) * P], yn[:, c * P:(c + 1) * P], ident[:], start=True, stop=True,
                               is_transpose=True)
            mm.then_inc(y_turned, 1)

        def project(pe, t):
            pe.wait_ge(y_copied, t + 1)
            if t >= 1:
                pe.wait_ge(x2_added, t)
            for c in range(CT):
                mm = pe.matmul(pm[:, 1, 0:C], yt[:, c], wp1[:, c], start=(c == 0), stop=(c == CT - 1))
            mm.then_inc(proj1, 1)

        with nc.Fori(0, B) as b:
            with nc.Block() as block:
                @block.sync
                def _(sp):
                    for t in range(NT):
                        if t >= 2:
                            sp.wait_ge(proj0, t - 1)
                            sp.wait_ge(f_step, 5 * (t - 2) + 1)
                        tok = bass.ds(b * N + t * P, P)
                        sp.dma_start(oin[:, t % 2], os_.rearrange("(c p) n -> p c n", p=P)[:, :, tok]).then_inc(tile_in[t % 2], 16)
                        sp.dma_start(xin[:, t % 2], xt[tok, :]).then_inc(tile_in[t % 2], 16)
                    for t in range(NT):
                        sp.wait_ge(x2_added, t + 1)
                        sp.dma_start(x2[bass.ds(b * N + t * P, P), :], xo[:, t % 2]).then_inc(x2_out[t % 2], 16)
                    for i in range(2):
                        sp.wait_ge(x2_out[i], 16 * NT // 2)

                @block.gpsimd
                def _(pool):
                    def bias(t):
                        pool.wait_ge(tile_in[t % 2], 32 * (t // 2 + 1))
                        pool.tensor_tensor(xin[:, t % 2], xin[:, t % 2], brow[:, 0], ALU.add).then_inc(xb_added, 1)

                    bias(0)
                    for t in range(NT):
                        if t + 1 < NT:
                            bias(t + 1)
                        pool.wait_ge(f_step, 5 * t + 4)
                        pool.tensor_tensor(rstd[:], rstd[:], mhalf[:, 0:1], ALU.pow).then_inc(powed, 1)

                @block.tensor
                def _(pe):
                    for t in range(NT + 3):
                        if t < NT:
                            pe.wait_ge(tile_in[t % 2], 32 * (t // 2 + 1))
                            if t >= 2:
                                pe.wait_ge(f_step, 5 * (t - 2) + 1)
                            for c in range(CT):
                                mm = pe.matmul(pm[:, t % 2, 0:C], oin[:, t % 2, c], wp0[:, c], start=(c == 0), stop=(c == CT - 1))
                            mm.then_inc(proj0, 1)
                        if 0 <= t - 2 < NT:
                            turn_xn(pe, t - 2)
                        if t >= 3:
                            values_in(pe, t - 3)
                    pe.wait_ge(v_added, NT)
                    j = 0
                    for a in range(2):
                        for hp in range(HEADS // 2):
                            for half in range(2):
                                if j >= 2:
                                    pe.wait_ge(qk_act, j - 1)
                                    pe.wait_ge(qk_dve, j - 1)
                                for c in range(CT):
                                    mm = pe.matmul(pqk[:, j % 2, :], wqk[:, c, a, 2 * hp:2 * hp + 2].rearrange("p h e -> p (h e)"),
                                                   xnt[:, c, half * 512:(half + 1) * 512], start=(c == 0), stop=(c == CT - 1))
                                mm.then_inc(qk_done, 1)
                                j += 1
                    pe.wait_ge(qk_act, 16)
                    pe.wait_ge(qk_dve, 16)
                    for u in range(U + 4):
                        t = (u - 4) // 2
                        last = u >= 4 and u % 2 == 1
                        if u < U:
                            scores(pe, u)
                        if last:
                            turn_y(pe, t)
                        if 0 <= u - 3 < U:
                            value_sums(pe, u - 3)
                        if 0 <= u - 2 < U:
                            turn_probs(pe, u - 2)
                        if last:
                            project(pe, t)

                @block.vector
                def _(dve):
                    def add_v(t):
                        dve.wait_ge(v_done, t + 1)
                        if t + 1 < NT:
                            dve.tensor_tensor(vp[WIN:P, t + 1], pqk[WIN:P, t % 2, 0:C], brow[WIN:P, 1], ALU.add)
                        dve.tensor_tensor(vv[:, t], pqk[:, t % 2, 0:C], brow[:, 1], ALU.add).then_inc(v_added, 1)

                    n = 0
                    for t in range(NT):
                        dve.wait_ge(proj0, t + 1)
                        dve.wait_ge(xb_added, t + 1)
                        dve.tensor_tensor(x1[:, t], pm[:, t % 2, 0:C], xin[:, t % 2], ALU.add).then_inc(f_step, 1)
                        dve.wait_ge(f_step, n + 1)
                        if t >= 2:
                            dve.wait_ge(xn_turned, t - 1)
                        layer_norm(dve, f_step, n + 1, powed, t, x1[:, t], bst[:], bmv[:], rstd[:], xn[:, t % 2])
                        n += 5
                        if t >= 3:
                            add_v(t - 3)
                    for t in range(NT - 3, NT):
                        add_v(t)
                    j = 0
                    for a in range(2):
                        for hp in range(HEADS // 2):
                            for half in range(2):
                                dve.wait_ge(qk_done, j + 1)
                                src = pqk[64:64 + HD, j % 2, :]
                                h = 2 * hp + 1
                                if a == 0:
                                    dve.tensor_scalar(qt[0:HD, h, half * 512:(half + 1) * 512], src, SCALE, bqk[:, 0, h:h + 1],
                                                      ALU.mult, ALU.add).then_inc(qk_dve, 1)
                                else:
                                    s4 = src.rearrange("d (t k) -> d t k", k=P)
                                    m = 4 if half == 0 else 3
                                    dve.tensor_scalar(kb[0:HD, half * 4 + 1:half * 4 + 1 + m, h, MEM:MEM + WIN], s4[:, 0:m, WIN:P],
                                                      bqk[:, 1, h:h + 1], None, ALU.add)
                                    dve.tensor_scalar(kb[0:HD, half * 4:half * 4 + 4, h, MEM + WIN:KEYS], s4,
                                                      bqk[:, 1, h:h + 1], None, ALU.add).then_inc(qk_dve, 1)
                                j += 1

                    def divide(t):
                        dve.wait_ge(exped, 8 * (t + 1))
                        dve.reciprocal(rinv[:, t % 2], rsum[:, t % 3]).then_inc(x2_step, 1)
                        dve.wait_ge(x2_step, t + 1)
                        dve.wait_ge(y_done, 4 * (t + 1))
                        if t >= 1:
                            dve.wait_ge(y_turned, t)
                        dve.tensor_tensor(yn[:].rearrange("p (h d) -> p h d", d=HD), pm[:, 0, 0:C].rearrange("p (h d) -> p h d", d=HD),
                                          rinv[:, t % 2].rearrange("p (h o) -> p h o", o=1).broadcast_to([P, HEADS, HD]),
                                          ALU.mult).then_inc(y_step, 1)

                    def residual(t):
                        dve.wait_ge(proj1, t + 1)
                        if t >= 2:
                            dve.wait_ge(x2_out[t % 2], 16 * (t // 2))
                        dve.tensor_tensor(xo[:, t % 2], pm[:, 1, 0:C], x1[:, t], ALU.add).then_inc(x2_half, 1)
                        dve.wait_ge(x2_half, t + 1)
                        dve.tensor_tensor(xo[:, t % 2], xo[:, t % 2], brow[:, 2], ALU.add).then_inc(x2_added, 1)

                    for u in range(U + 5):
                        if u < U:
                            t, q = divmod(u, 2)
                            for k in range(4):
                                dve.wait_ge(s_done, 2 * u + k // 2 + 1)
                                if u >= 2 and k % 2 == 0:
                                    dve.wait_ge(p_turned, 2 * (u - 2) + k // 2 + 1)
                                dve.tensor_tensor_reduce(pr[:, u % 2, k, :], psc[:, k // 2, k % 2, :], mask[:, 1 if t == 0 else 0],
                                                         -1.0, BIG, ALU.add, ALU.min, nmax[:, u % 2, k:k + 1]).then_inc(masked, 1)
                        if u >= 6 and u % 2 == 0:
                            residual((u - 6) // 2)
                        if 4 <= u < U + 4 and u % 2 == 0:
                            divide((u - 4) // 2)

                @block.scalar
                def _(act):
                    for t in range(NT):
                        act.wait_ge(xn_turned, t + 1)
                        act.activation(xnt[:, :, t * P:(t + 1) * P], ptr[:, t % 2, 0:CT, :], ACT.Copy).then_inc(xnt_copied, 1)
                    j = 0
                    for a in range(2):
                        for hp in range(HEADS // 2):
                            for half in range(2):
                                act.wait_ge(qk_done, j + 1)
                                src = pqk[0:HD, j % 2, :]
                                h = 2 * hp
                                if a == 0:
                                    act.activation(qt[0:HD, h, half * 512:(half + 1) * 512], src, ACT.Identity, scale=SCALE,
                                                   bias=bqk[:, 0, h:h + 1]).then_inc(qk_act, 1)
                                else:
                                    s4 = src.rearrange("d (t k) -> d t k", k=P)
                                    m = 4 if half == 0 else 3
                                    act.activation(kb[0:HD, half * 4 + 1:half * 4 + 1 + m, h, MEM:MEM + WIN], s4[:, 0:m, WIN:P],
                                                   ACT.Identity, bias=bqk[:, 1, h:h + 1])
                                    act.activation(kb[0:HD, half * 4:half * 4 + 4, h, MEM + WIN:KEYS], s4, ACT.Identity,
                                                   bias=bqk[:, 1, h:h + 1]).then_inc(qk_act, 1)
                                j += 1

                    for u in range(U + 4):
                        if u >= 4 and u % 2 == 1:
                            t = (u - 4) // 2
                            act.wait_ge(y_turned, t + 1)
                            act.activation(yt[:], pqk[:, 0, 0:C].rearrange("p (c n) -> p c n", c=CT), ACT.Copy).then_inc(y_copied, 1)
                        if 0 <= u - 2 < U:
                            for i in range(2):
                                act.wait_ge(p_turned, 2 * (u - 2) + i + 1)
                                if u >= 3:
                                    act.wait_ge(y_done, 2 * (u - 3) + i + 1)
                                act.activation(pt[:, i], ptr[:, i], ACT.Copy).then_inc(p_copied, 1)
                        if u < U:
                            t, q = divmod(u, 2)
                            for k in range(4):
                                act.wait_ge(masked, 4 * u + k + 1)
                                if t >= 3 and k == 0:
                                    act.wait_ge(x2_step, t - 2)
                                act.activation(pr[:, u % 2, k, :], pr[:, u % 2, k, :], ACT.Exp, bias=nmax[:, u % 2, k:k + 1],
                                               scale=-1.0, accum_out=rsum[:, t % 3, q * 4 + k:q * 4 + k + 1]).then_inc(exped, 1)
            s.clear()


def experts(nc, x2, gate_w, gate_b, w1, b1, w2, b2, ident, mhalf, xns, out):
    TB = 512
    TT = TB // P
    NB = T // TB
    NTT = T // P
    HI, LO = 0, 1
    PASSES = ((HI, HI), (HI, LO), (LO, HI))
    RING = 3
    LN_STEPS = 3 * TT + 1
    with Scope(nc) as s:
        acc = s.sb("acc", [P, NTT, C])
        xb = s.sb("xb", [P, 2, 2, CT, TB], F32R)
        wr = s.sb("wr", [P, 2, HT, 2 * CT, P], F32R)
        stage = s.sb("stage", [P, RING, 2 * CT, P])
        hs = s.sb("hs", [P, RING, TB])
        hr = s.sb("hr", [P, 2, RING, TB], F32R)
        xn = s.sb("xne", [P, 2, C])
        xs = s.sb("xs", [P, 2, CT, TB])
        gw = s.sb("gw", [P, CT, EXPERTS])
        gb = s.sb("gb", [P, EXPERTS])
        b1e = s.sb("b1e", [P, HT])
        b2e = s.sb("b2e", [P, C])
        tri = s.sb("tri", [P, EXPERTS, EXPERTS])
        bst = s.sb("bste", [P, TT, 6])
        bmv = s.sb("bmve", [P, TT, 2])
        rstd = s.sb("rstde", [P, TT])
        g = s.sb("g", [P, NTT, EXPERTS])
        ge = s.sb("ge", [P, NTT])
        red = s.sb("red", [P, NTT])
        lt = s.sb("lt", [P, NTT, EXPERTS, EXPERTS])
        eq = s.sb("eq", [P, NTT, EXPERTS, EXPERTS])
        pu = s.ps("pu", [P, RING, 512])
        pd = s.ps("pd", [P, TT, 512])
        pgt = s.ps("pgt", [P, 512])

        wl = s.sem("wle")
        tri_step = s.sem("tri_step")
        x_in = [s.sem(f"x_in_e{i}") for i in range(NB)]
        ln = s.sem("ln")
        powed = s.sem("powede")
        turned = s.sem("turned_e")
        copied = s.sem("copied_e")
        g_done = s.sem("g_done")
        g_step = s.sem("g_step")
        g_exp = s.sem("g_exp")
        xn_out = [s.sem(f"xn_out{i}") for i in range(2)]
        w_in = [s.sem(f"w_in_e{i}") for i in range(RING)]
        w_hi = s.sem("w_hi")
        w_lo = s.sem("w_lo")
        xs_in = [s.sem(f"xs_in{i}") for i in range(2)]
        x_hi = s.sem("x_hi")
        x_lo = s.sem("x_lo")
        b_in = s.sem("b_in")
        up = s.sem("up")
        gelu = s.sem("gelu")
        h_hi = s.sem("h_hi")
        h_lo = s.sem("h_lo")
        down = s.sem("down")
        ge_done = s.sem("ge_done")
        summed = s.sem("summed")
        o_out = s.sem("o_out_e")

        with nc.Block() as block:
            @block.sync
            def _(sp):
                for i in range(NB):
                    sp.dma_start(acc[:, i * TT:(i + 1) * TT], x2[i * TB:(i + 1) * TB, :].rearrange("(t p) c -> p t c", p=P)
                                 ).then_inc(x_in[i], 16)
                sp.dma_start(gw[:], gate_w.rearrange("(t p) n -> p t n", p=P)).then_inc(wl, 16)
                sp.dma_start(gb[:], gate_b.rearrange("(o n) -> o n", o=1).broadcast_to([P, EXPERTS])).then_inc(wl, 16)
                for i in range(NB):
                    sp.wait_ge(copied, TT * (i + 1))
                    sp.dma_start(xns[i], xs[:, i % 2].rearrange("p t n -> p (t n)")).then_inc(xn_out[i % 2], 16)
                for i in range(2):
                    sp.wait_ge(xn_out[i], 16 * NB // 2)

            @block.gpsimd
            def _(pool):
                pool.memset(tri[:].rearrange("p j e -> p (j e)"), 1.0).then_inc(tri_step, 1)
                pool.wait_ge(tri_step, 1)
                pool.affine_select(out=tri[:], in_=tri[:], compare_op=ALU.is_gt, fill=0.0, base=0,
                                   pattern=[[-1, EXPERTS], [1, EXPERTS]], channel_multiplier=0).then_inc(tri_step, 1)
                for i in range(NB):
                    pool.wait_ge(ln, LN_STEPS * i + 2 * TT + 1)
                    pool.tensor_tensor(rstd[:], rstd[:], mhalf[:, 0:TT], ALU.pow).then_inc(powed, 1)

            @block.tensor
            def _(pe):
                def gates(t):
                    pe.wait_ge(copied, t + 1)
                    for c in range(CT):
                        mm = pe.matmul(pgt[:, t * EXPERTS:(t + 1) * EXPERTS],
                                       xs[:, t // TT % 2, c, t % TT * P:(t % TT + 1) * P], gw[:, c],
                                       start=(c == 0), stop=(c == CT - 1), skip_group_check=True)
                    mm.then_inc(g_done, 1)

                pe.wait_ge(wl, 32)
                for t in range(NTT):
                    i, k = divmod(t, TT)
                    pe.wait_ge(ln, LN_STEPS * i + 2 * TT + 1 + k + 1)
                    if t >= 2:
                        pe.wait_ge(copied, t - 1)
                    for c in range(CT):
                        mm = pe.matmul(pd[:, t % 2, c * P:(c + 1) * P], xn[:, t % 2, c * P:(c + 1) * P], ident[:],
                                       start=True, stop=True, is_transpose=True)
                    mm.then_inc(turned, 1)
                    if t >= 1:
                        gates(t - 1)
                gates(NTT - 1)

            @block.scalar
            def _(act):
                for t in range(NTT):
                    i, k = divmod(t, TT)
                    src = pd[:, t % 2, 0:C].rearrange("p (c n) -> p c n", c=CT)
                    act.wait_ge(turned, t + 1)
                    if i >= 2 and k == 0:
                        act.wait_ge(xn_out[i % 2], 16 * (i // 2))
                        act.wait_ge(g_done, TT * (i - 1))
                    act.activation(xs[:, i % 2, :, k * P:(k + 1) * P], src, ACT.Copy).then_inc(copied, 1)
                act.wait_ge(g_step, 3)
                act.activation(g[:], g[:], ACT.Exp).then_inc(g_exp, 1)

            @block.vector
            def _(dve):
                for i in range(NB):
                    n = LN_STEPS * i
                    dve.wait_ge(x_in[i], 16)
                    for k in range(TT):
                        dve.bn_stats(bst[:, k], acc[:, i * TT + k]).then_inc(ln, 1)
                    for k in range(TT):
                        dve.wait_ge(ln, n + k + 1)
                        if k == 0 and i >= 1:
                            dve.wait_ge(ln, n)
                        dve.bn_aggr(bmv[:, k], bst[:, k]).then_inc(ln, 1)
                    dve.wait_ge(ln, n + 2 * TT)
                    dve.tensor_scalar(rstd[:], bmv[:, :, 1], 1e-5, None, ALU.add).then_inc(ln, 1)
                    dve.wait_ge(powed, i + 1)
                    for k in range(TT):
                        t = i * TT + k
                        if t >= 2:
                            dve.wait_ge(turned, t - 1)
                        dve.tensor_scalar(xn[:, t % 2], acc[:, t], bmv[:, k, 0:1], rstd[:, k:k + 1],
                                          ALU.subtract, ALU.mult).then_inc(ln, 1)
                n = [0]

                def step(ins):
                    ins.then_inc(g_step, 1)
                    n[0] += 1
                    dve.wait_ge(g_step, n[0])

                def over(a, e):
                    return a.rearrange("p (t o) -> p t o", o=1).broadcast_to([P, NTT, e])

                FULL = [P, NTT, EXPERTS, EXPERTS]
                dve.wait_ge(g_done, NTT)
                scores = pgt[:, 0:NTT * EXPERTS].rearrange("p (t e) -> p t e", e=EXPERTS)
                step(dve.tensor_tensor(g[:], scores, gb[:].rearrange("p (o e) -> p o e", o=1).broadcast_to([P, NTT, EXPERTS]),
                                       ALU.add))
                step(dve.tensor_reduce(red[:], g[:], AX_X, ALU.max))
                step(dve.tensor_tensor(g[:], g[:], over(red[:], EXPERTS), ALU.subtract))
                dve.wait_ge(g_exp, 1)
                step(dve.tensor_reduce(red[:], g[:], AX_X, ALU.add))
                step(dve.reciprocal(red[:], red[:]))
                step(dve.tensor_tensor(g[:], g[:], over(red[:], EXPERTS), ALU.mult))
                for_e = g[:].rearrange("p t (o e) -> p t o e", o=1).broadcast_to(FULL)
                for_j = g[:].rearrange("p t (j o) -> p t j o", o=1).broadcast_to(FULL)
                dve.wait_ge(tri_step, 2)
                dve.tensor_tensor(lt[:], for_e, for_j, ALU.is_lt)
                step(dve.tensor_tensor(eq[:], for_e, for_j, ALU.is_equal))
                step(dve.tensor_tensor(eq[:], eq[:], tri[:].rearrange("p (o j) e -> p o j e", o=1).broadcast_to(FULL), ALU.mult))
                step(dve.tensor_tensor(lt[:], lt[:], eq[:], ALU.add))
                step(dve.tensor_reduce(eq[:, :, 0, :], lt[:].rearrange("p t j e -> p t e j"), AX_X, ALU.add))
                step(dve.scalar_tensor_tensor(out=g[:], in0=eq[:, :, 0, :], scalar=1.5, in1=g[:], op0=ALU.is_lt, op1=ALU.mult))
                step(dve.tensor_reduce(red[:], g[:], AX_X, ALU.add))
                step(dve.tensor_scalar(red[:], red[:], 1e-9, None, ALU.add))
                step(dve.reciprocal(red[:], red[:]))
                step(dve.tensor_tensor(g[:], g[:], over(red[:], EXPERTS), ALU.mult))

        NJ = NB * HT
        LAG = 2

        def expert(e, last):
            with nc.Block() as block:
                @block.sync
                def _(sp):
                    one = bass.ds(e, 1)

                    def weights(m):
                        if m >= RING:
                            sp.wait_ge(w_lo, m - RING + 1)
                        sp.dma_start(stage[:, m % RING, 0:CT], w1[one].rearrange("e (t p) n -> p (e t) n", p=P)[
                            :, :, m * P:(m + 1) * P]).then_inc(w_in[m % RING], 16)
                        sp.dma_start(stage[:, m % RING, CT:2 * CT].rearrange("p t n -> p (t n)"),
                                     w2[one].rearrange("e k n -> (e k) n")[m * P:(m + 1) * P, :]).then_inc(w_in[m % RING], 16)

                    def tokens(i):
                        if i >= 2:
                            sp.wait_ge(x_hi, i - 1)
                            sp.wait_ge(x_lo, i - 1)
                        sp.dma_start(xs[:, i % 2].rearrange("p t n -> p (t n)"), xns[i]).then_inc(xs_in[i % 2], 16)

                    tokens(0)
                    weights(0)
                    weights(1)
                    tokens(1)
                    sp.dma_start(b1e[:], b1[:, one, :].rearrange("p e m -> p (e m)")).then_inc(b_in, 16)
                    sp.dma_start(b2e[:], b2[one, :].broadcast_to([P, C])).then_inc(b_in, 16)
                    for m in range(2, HT):
                        weights(m)
                    for i in range(2, NB):
                        tokens(i)
                    if last:
                        for i in range(NB):
                            sp.wait_ge(summed, 2 * TT * (i + 1))
                            sp.dma_start(out[i * TB:(i + 1) * TB, :].rearrange("(t p) c -> p t c", p=P),
                                         acc[:, i * TT:(i + 1) * TT]).then_inc(o_out, 16)
                        sp.wait_ge(o_out, 16 * NB)

                @block.gpsimd
                def _(pool):
                    def split_x(i):
                        pool.wait_ge(x_hi, i + 1)
                        pool.tensor_tensor(xb[:, i % 2, LO], xs[:, i % 2], xb[:, i % 2, HI].bitcast(F32),
                                           ALU.subtract).then_inc(x_lo, 1)

                    split_x(0)
                    for m in range(HT):
                        pool.wait_ge(w_hi, m + 1)
                        pool.tensor_tensor(wr[:, LO, m], stage[:, m % RING], wr[:, HI, m].bitcast(F32),
                                           ALU.subtract).then_inc(w_lo, 1)
                    for i in range(1, NB):
                        split_x(i)

                @block.tensor
                def _(pe):
                    def first(j):
                        i, m = divmod(j, HT)
                        if m == 0:
                            pe.wait_ge(x_lo, i + 1)
                        if i == 0:
                            pe.wait_ge(w_lo, m + 1)
                        if j >= RING:
                            pe.wait_ge(gelu, j - RING + 1)
                        n = 0
                        for a, b in PASSES:
                            for c in range(CT):
                                mm = pe.matmul(pu[:, j % RING, :], wr[:, a, m, c, :], xb[:, i % 2, b, c, :],
                                               start=(n == 0), stop=(n == 3 * CT - 1))
                                n += 1
                        mm.then_inc(up, 1)

                    def second(j):
                        i, m = divmod(j, HT)
                        pe.wait_ge(h_lo, j + 1)
                        for t in range(TT):
                            if m == 0 and i >= 1:
                                pe.wait_ge(summed, 2 * TT * (i - 1) + TT + t + 1)
                            for n, (a, b) in enumerate(PASSES):
                                mm = pe.matmul(pd[:, t, 0:C], hr[:, a, j % RING, t * P:(t + 1) * P],
                                               wr[:, b, m, CT:2 * CT, :],
                                               start=(m == 0 and n == 0), stop=(m == HT - 1 and n == 2))
                        mm.then_inc(down, 1)

                    for j in range(NJ + LAG):
                        if j < NJ:
                            first(j)
                        if j >= LAG:
                            second(j - LAG)

                @block.scalar
                def _(act):
                    act.wait_ge(b_in, 32)
                    for j in range(NJ):
                        act.wait_ge(up, j + 1)
                        if j >= RING:
                            act.wait_ge(h_lo, j - RING + 1)
                        act.activation(hs[:, j % RING], pu[:, j % RING, :], ACT.Gelu, bias=b1e[:, j % HT:j % HT + 1]
                                       ).then_inc(gelu, 1)

                @block.vector
                def _(dve):
                    def split_w(m):
                        dve.wait_ge(w_in[m % RING], 32 * (m // RING + 1))
                        dve.tensor_copy(wr[:, HI, m], stage[:, m % RING]).then_inc(w_hi, 1)

                    def split_x(i):
                        dve.wait_ge(xs_in[i % 2], 16 * (i // 2 + 1))
                        if i >= 2:
                            dve.wait_ge(up, HT * (i - 1))
                        dve.tensor_copy(xb[:, i % 2, HI], xs[:, i % 2]).then_inc(x_hi, 1)

                    def biases(i):
                        for t in range(i * TT, (i + 1) * TT):
                            dve.scalar_tensor_tensor(out=acc[:, t], in0=b2e[:], scalar=ge[:, t:t + 1], in1=acc[:, t],
                                                     op0=ALU.mult, op1=ALU.add).then_inc(summed, 1)

                    def sums(i):
                        dve.wait_ge(down, HT * (i + 1))
                        for t in range(TT):
                            dve.wait_ge(summed, 2 * TT * i + t + 1)
                            dve.scalar_tensor_tensor(out=acc[:, i * TT + t], in0=pd[:, t, 0:C],
                                                     scalar=ge[:, i * TT + t:i * TT + t + 1],
                                                     in1=acc[:, i * TT + t], op0=ALU.mult, op1=ALU.add).then_inc(summed, 1)

                    split_x(0)
                    for m in range(RING):
                        split_w(m)
                    dve.tensor_copy(ge[:], g[:, :, bass.ds(e, 1)].rearrange("p t e -> p (t e)")).then_inc(ge_done, 1)
                    dve.wait_ge(b_in, 32)
                    dve.wait_ge(ge_done, 1)
                    for j in range(NJ + LAG):
                        if j < NJ:
                            dve.wait_ge(gelu, j + 1)
                            if j >= RING:
                                dve.wait_ge(down, j - RING + 1)
                            dve.tensor_copy(hr[:, HI, j % RING], hs[:, j % RING]).then_inc(h_hi, 1)
                            dve.wait_ge(h_hi, j + 1)
                            dve.tensor_tensor(hr[:, LO, j % RING], hs[:, j % RING], hr[:, HI, j % RING].bitcast(F32),
                                              ALU.subtract).then_inc(h_lo, 1)
                            if j + RING < HT:
                                split_w(j + RING)
                            if j % HT == 2 and j // HT + 1 < NB:
                                split_x(j // HT + 1)
                            if j % HT == HT // 2:
                                biases(j // HT)
                        if j >= LAG and (j - LAG) % HT == HT - 1:
                            sums((j - LAG) // HT)
            s.clear()

        s.clear()
        with nc.Fori(0, EXPERTS - 1) as e:
            expert(e, False)
        expert(EXPERTS - 1, True)


def build(nc, a):
    def dram(name, shape):
        return nc.dram_tensor(name, shape, F32, kind="Internal").ap()

    qs, ks = dram("qs", (HEADS, HD, T)), dram("ks", (HEADS, HD, T))
    vs = dram("vs", (P, T // P, C))
    tve = dram("tve", (HEADS, SPAN, EXT, HD))
    us = dram("us", (HEADS, 8, P, NCH, 512))
    ws = dram("ws", (HEADS, B, WW, SPAN, N))
    os_ = dram("os_", (C, T))
    x2 = dram("x2", (T, C))
    xns = dram("xns", (T // 512, P, CT * 512))
    with Scope(nc) as s:
        ident = s.sb("ident", [P, P])
        mhalf = s.sb("mhalf", [P, B])
        ident_step = s.sem("ident_step")
        with nc.Block() as block:
            @block.gpsimd
            def _(pool):
                pool.memset(mhalf[:], -0.5)
                pool.memset(ident[:], 1.0).then_inc(ident_step, 1)
                pool.wait_ge(ident_step, 1)
                pool.affine_select(out=ident[:], in_=ident[:], compare_op=ALU.is_equal, fill=0.0, base=0,
                                   pattern=[[-1, P]], channel_multiplier=1)
        norm_qkv(nc, a["x"], a["w_qkv"], a["tv"], mhalf, qs, ks, vs, tve)
        bias_tables(nc, a["tkq"], qs, ks, us, ws)
        attention(nc, ident, qs, ks, vs, us, ws, tve, os_)
        window(nc, a["xt"], a["w_proj"], a["b_proj"], a["mem_t"], a["mem"], a["qkv_w"], a["qkv_b"], a["qkb"],
               a["proj_w"], a["proj_b"], ident, mhalf, os_, x2)
        experts(nc, x2, a["gate_w"], a["gate_b"], a["w1"], a["b1"], a["w2"], a["b2"], ident, mhalf, xns, a["out"])


def kernel(**inputs):
    import numpy as np
    import concourse.bacc as bacc
    from concourse.bass_utils import run_bass_kernel_spmd

    i = {k: np.asarray(v) for k, v in inputs.items()}
    x = i["x"].reshape(B, C, N)
    tk = i["L0_conv_table_k"].reshape(HEADS, SPAN, SPAN, HD)[:, ::-1, ::-1].transpose(0, 3, 1, 2)
    tq = i["L0_conv_table_q"].reshape(HEADS, SPAN, SPAN, HD)[:, :, ::-1].transpose(0, 3, 1, 2)
    arrays = {
        "x": x,
        "xt": x.transpose(0, 2, 1).reshape(T, C),
        "w_qkv": i["L0_conv_w_qkv"], "w_proj": i["L0_conv_w_proj"], "b_proj": i["L0_conv_b_proj"],
        "tkq": np.stack([tk, tq], axis=2),
        "tv": i["L0_conv_table_v"].reshape(HEADS, SPAN, SPAN, HD)[:, ::-1, ::-1],
        "mem": i["L1_attn_mem"],
        "mem_t": i["L1_attn_mem"].reshape(MEM, HEADS, HD).transpose(2, 1, 0),
        "qkv_w": i["L1_attn_qkv_w"], "qkv_b": i["L1_attn_qkv_b"],
        "qkb": i["L1_attn_qkv_b"][:2 * C].reshape(2, HEADS, HD).transpose(2, 0, 1),
        "proj_w": i["L1_attn_proj_w"], "proj_b": i["L1_attn_proj_b"],
        "gate_w": i["L1_ffn_gate_w"], "gate_b": i["L1_ffn_gate_b"],
        "w1": i["L1_ffn_w1"], "b1": i["L1_ffn_b1"].reshape(EXPERTS, HT, P).transpose(2, 0, 1),
        "w2": i["L1_ffn_w2"], "b2": i["L1_ffn_b2"],
    }
    nc = bacc.Bacc("TRN2", target_bir_lowering=False, num_devices=1)
    given, a = {}, {}
    for name, v in arrays.items():
        given[f"in_{name}"] = np.ascontiguousarray(v)
        a[name] = nc.dram_tensor(f"in_{name}", v.shape, F32, kind="ExternalInput").ap()
    a["out"] = nc.dram_tensor("out_tokens", (T, C), F32, kind="ExternalOutput").ap()
    build(nc, a)
    r = run_bass_kernel_spmd(nc, [given], core_ids=[0])
    y = r.results[0]["out_tokens"]
    return y.reshape(B, N, C).transpose(0, 2, 1).reshape(B, C, HH, WW)
```

```python
from contextlib import ExitStack

import concourse.bass as bass
from concourse import mybir

F32 = mybir.dt.float32
F32R = mybir.dt.float32r
ACT = mybir.ActivationFunctionType
ALU = mybir.AluOpType
AX_X = mybir.AxisListType.X

P = 128
B, C, HH, WW = 4, 384, 32, 32
N = HH * WW
T = B * N
CT = C // P
HEADS = 8
HD = C // HEADS
SPAN = 15
MAXD = 7
EXT = 2 * WW - 1
PIECE = 2 * HD
KP = P
SCALE = float(HD) ** -0.5
BIG = 3.0e38
CH_ROWS = [4, 4, 4, 3]
NCH = len(CH_ROWS)
GROUP = 12
MEM = 64
WIN = 64
EXPERTS = 4
HID = 4 * C
HT = HID // P
MASKED = -1.0e30


class Scope:

    def __init__(self, nc):
        self.nc, self.ctx, self.sems = nc, ExitStack(), []

    def __enter__(self):
        return self

    def __exit__(self, *a):
        self.ctx.close()

    def sb(self, name, shape, dt=F32):
        return self.ctx.enter_context(self.nc.sbuf_tensor(name, shape, dt))

    def ps(self, name, shape, dt=F32):
        return self.ctx.enter_context(self.nc.psum_tensor(name, shape, dt))

    def sem(self, name):
        s = self.ctx.enter_context(self.nc.semaphore(name))
        self.sems.append(s)
        return s

    def clear(self):
        for s in self.sems:
            self.nc.gpsimd.sem_clear(s)
        self.nc.all_engine_barrier()


def norm_qkv(nc, x, w_qkv, tv, mhalf, qs, ks, vs, tve):
    PASSES = [(p_w, p_x, t) for p_w, p_x in ((0, 0), (0, 1), (1, 0)) for t in range(CT)]
    with Scope(nc) as s:
        xc = s.sb("xc", [P, CT, B, N])
        xh = s.sb("xh", [P, CT, B, N], F32R)
        xl = s.sb("xl", [P, CT, B, N], F32R)
        wr = s.sb("w0r", [P, 2, CT, 3 * C], F32R)
        x_parts = (xh, xl)
        grp = s.sb("grp", [P, P])
        stats = s.sb("stats", [P, CT, B, 2, 6])
        mv = s.sb("mv", [P, CT, B, 2])
        mean = s.sb("mean", [P, B])
        dev = s.sb("dev", [P, CT, B])
        var = s.sb("var", [P, CT, B])
        rstd = s.sb("rstd", [P, B])
        st = s.sb("st", [PIECE, 2, T // 2])
        vst = s.sb("vst", [P, 3 * CT, C])
        w = vst[:].rearrange("p (t a) c -> p t (a c)", t=CT)
        pg = s.ps("pg", [P, 2, 512])
        pq = s.ps("pq", [P, 4, 512])
        x_in = [s.sem(f"x_in{b}") for b in range(B)]
        w_in = s.sem("w_in")
        grp_step = s.sem("grp_step")
        stat_step = s.sem("stat_step")
        sums = s.sem("sums")
        normed = s.sem("normed")
        split_hi = s.sem("split_hi")
        split_lo = s.sem("split_lo")
        w_hi = s.sem("w_hi0")
        w_lo = s.sem("w_lo0")
        prod = s.sem("prod")
        copied_act = s.sem("copied_act")
        copied_dve = s.sem("copied_dve")
        stored = [s.sem(f"stored{i}") for i in range(2)]
        vstored = [s.sem(f"vstored{i}") for i in range(2)]
        ext_out = s.sem("ext_out")
        powed = s.sem("powed0")
        NB = T // 512
        PIECES = [(part, m) for part in range(2) for m in range(4)]
        NQK = len(PIECES) * NB
        NV = T // P

        with nc.Block() as block:
            @block.sync
            def _(sp):
                sp.dma_start(w, w_qkv.rearrange("(p t) n -> p t n", t=CT)).then_inc(w_in, 16)
                for b in range(B):
                    sp.dma_start(xc[:, :, b, :], x[b].rearrange("(p t) n -> p t n", t=CT)).then_inc(x_in[b], 16)
                lo = WW - 1 - MAXD
                for h in range(HEADS):
                    sp.dma_start(tve[h, :, lo:lo + SPAN, :], tv[h]).then_inc(ext_out, 16)
                    sp.dma_start(tve[h, :, 0:lo, :], tv[h, :, 0:1, :].broadcast_to([SPAN, lo, HD])).then_inc(ext_out, 16)
                    sp.dma_start(tve[h, :, lo + SPAN:EXT, :],
                                 tv[h, :, SPAN - 1:SPAN, :].broadcast_to([SPAN, EXT - lo - SPAN, HD])).then_inc(ext_out, 16)
                for i, (part, m) in enumerate(PIECES):
                    dst = (qs if part == 0 else ks).rearrange("h d n -> (h d) n")
                    for half in range(2):
                        sp.wait_ge(copied_act, (2 * i + half + 1) * NB // 4)
                        sp.wait_ge(copied_dve, (2 * i + half + 1) * NB // 4)
                        sp.dma_start(dst[m * PIECE:(m + 1) * PIECE, half * T // 2:(half + 1) * T // 2], st[:, half, :]
                                     ).then_inc(stored[half], 16)
                for i in range(NV // 4):
                    sp.wait_ge(copied_act, NQK // 2 + (i + 1) * 2)
                    sp.wait_ge(copied_dve, NQK // 2 + (i + 1) * 2)
                    sp.dma_start(vs[:, i * 4:(i + 1) * 4, :], vst[:, i % 2 * 4:i % 2 * 4 + 4]).then_inc(vstored[i % 2], 16)
                for i in range(2):
                    sp.wait_ge(stored[i], 16 * len(PIECES))
                    sp.wait_ge(vstored[i], 16 * NV // 8)
                sp.wait_ge(ext_out, 16 * 3 * HEADS)

            @block.gpsimd
            def _(pool):
                pool.memset(grp[:], 1.0 / GROUP).then_inc(grp_step, 1)
                g3 = grp[:].rearrange("p (g r) -> p g r", r=4)
                pool.wait_ge(grp_step, 1)
                pool.affine_select(out=g3, in_=g3, compare_op=ALU.is_ge, fill=0.0, base=0,
                                   pattern=[[-4, 32], [0, 4]], channel_multiplier=1).then_inc(grp_step, 1)
                pool.wait_ge(grp_step, 2)
                pool.affine_select(out=g3, in_=g3, compare_op=ALU.is_ge, fill=0.0, base=3,
                                   pattern=[[4, 32], [0, 4]], channel_multiplier=-1).then_inc(grp_step, 1)
                pool.wait_ge(stat_step, 3 * CT * B + 5)
                pool.tensor_tensor(rstd[:], rstd[:], mhalf[:, 0:B], ALU.pow).then_inc(powed, 1)

            @block.vector
            def _(dve):
                dve.wait_ge(w_hi, 1)
                dve.tensor_tensor(wr[:, 1], w, wr[:, 0].bitcast(F32), ALU.subtract).then_inc(w_lo, 1)
                n = 0
                for b in range(B):
                    dve.wait_ge(x_in[b], 16)
                    for t in range(CT):
                        for k in range(2):
                            dve.bn_stats(stats[:, t, b, k, :], xc[:, t, b, k * 512:(k + 1) * 512]).then_inc(stat_step, 1)
                            n += 1
                for b in range(B):
                    for t in range(CT):
                        dve.wait_ge(stat_step, 2 * CT * B)
                        dve.bn_aggr(mv[:, t, b, :], stats[:, t, b].rearrange("p k s -> p (k s)")).then_inc(stat_step, 1)
                        n += 1
                dve.wait_ge(sums, 1)
                dve.tensor_copy(mean[:], pg[:, 0, 0:B]).then_inc(stat_step, 1)
                n += 1
                dve.wait_ge(stat_step, n)
                dve.tensor_tensor(dev[:], mv[:, :, :, 0], mean[:].rearrange("p (o b) -> p o b", o=1).broadcast_to([P, CT, B]),
                                  ALU.subtract).then_inc(stat_step, 1)
                n += 1
                dve.wait_ge(stat_step, n)
                dve.tensor_tensor(dev[:], dev[:], dev[:], ALU.mult).then_inc(stat_step, 1)
                n += 1
                dve.wait_ge(stat_step, n)
                dve.tensor_tensor(var[:], mv[:, :, :, 1], dev[:], ALU.add).then_inc(stat_step, 1)
                n += 1
                dve.wait_ge(sums, 2)
                dve.tensor_scalar(rstd[:], pg[:, 1, 0:B], 1e-5, None, ALU.add).then_inc(stat_step, 1)
                dve.wait_ge(powed, 1)

                def low(b):
                    for t in range(CT):
                        dve.wait_ge(split_hi, CT * b + t + 1)
                        dve.tensor_tensor(xl[:, t, b, :], xc[:, t, b, :], xh[:, t, b, :].bitcast(F32),
                                          ALU.subtract).then_inc(split_lo, 1)

                for b in range(B):
                    for t in range(CT):
                        dve.tensor_scalar(xc[:, t, b, :], xc[:, t, b, :], mean[:, b:b + 1], rstd[:, b:b + 1],
                                          ALU.subtract, ALU.mult).then_inc(normed, 1)
                    if b >= 1:
                        low(b - 1)
                low(B - 1)
                for i, (part, m) in enumerate(PIECES):
                    for nb in range(1, NB, 2):
                        j = i * NB + nb
                        dve.wait_ge(prod, j + 1)
                        if i >= 1:
                            dve.wait_ge(stored[nb * 2 // NB], 16 * i)
                        dve.tensor_scalar(st[:, nb * 2 // NB, nb * 512 % (T // 2):nb * 512 % (T // 2) + 512], pq[0:PIECE, j % 4, :],
                                          SCALE if part == 0 else 1.0, None, ALU.mult).then_inc(copied_dve, 1)
                for i in range(1, NV, 2):
                    dve.wait_ge(prod, NQK + i + 1)
                    if i >= 8:
                        dve.wait_ge(vstored[i // 4 % 2], 16 * (i // 8))
                    dve.tensor_copy(vst[:, i // 4 % 2 * 4 + i % 4, :], pq[:, (NQK + i) % 4, 0:C]).then_inc(copied_dve, 1)

            @block.scalar
            def _(act):
                act.wait_ge(w_in, 16)
                act.activation(wr[:, 0], w, ACT.Copy).then_inc(w_hi, 1)
                for b in range(B):
                    for t in range(CT):
                        act.wait_ge(normed, CT * b + t + 1)
                        act.activation(xh[:, t, b, :], xc[:, t, b, :], ACT.Copy).then_inc(split_hi, 1)
                for i, (part, m) in enumerate(PIECES):
                    for nb in range(0, NB, 2):
                        j = i * NB + nb
                        act.wait_ge(prod, j + 1)
                        if i >= 1:
                            act.wait_ge(stored[nb * 2 // NB], 16 * i)
                        act.activation(st[:, nb * 2 // NB, nb * 512 % (T // 2):nb * 512 % (T // 2) + 512], pq[0:PIECE, j % 4, :], ACT.Copy,
                                       scale=SCALE if part == 0 else 1.0).then_inc(copied_act, 1)
                for i in range(0, NV, 2):
                    act.wait_ge(prod, NQK + i + 1)
                    if i >= 8:
                        act.wait_ge(vstored[i // 4 % 2], 16 * (i // 8))
                    act.activation(vst[:, i // 4 % 2 * 4 + i % 4, :], pq[:, (NQK + i) % 4, 0:C], ACT.Copy).then_inc(copied_act, 1)

            @block.tensor
            def _(pe):
                pe.wait_ge(grp_step, 3)
                pe.wait_ge(stat_step, 3 * CT * B)
                for t in range(CT):
                    mm = pe.matmul(pg[:, 0, 0:B], grp[:], mv[:, t, :, 0], start=(t == 0), stop=(t == CT - 1))
                mm.then_inc(sums, 1)
                pe.wait_ge(stat_step, 3 * CT * B + 4)
                for t in range(CT):
                    mm = pe.matmul(pg[:, 1, 0:B], grp[:], var[:, t, :], start=(t == 0), stop=(t == CT - 1))
                mm.then_inc(sums, 1)
                pe.wait_ge(w_lo, 1)

                def free(j):
                    if j >= 4:
                        pe.wait_ge(copied_dve if j % 2 else copied_act, (j - 4) // 2 + 1)

                for i, (part, m) in enumerate(PIECES):
                    for nb in range(NB):
                        j = i * NB + nb
                        pe.wait_ge(split_lo, CT * (nb // 2 + 1))
                        free(j)
                        for step, (p_w, p_x, t) in enumerate(PASSES):
                            mm = pe.matmul(pq[0:PIECE, j % 4, :],
                                           wr[:, p_w, t, part * C + m * PIECE:part * C + (m + 1) * PIECE],
                                           x_parts[p_x][:, t, nb // 2, nb % 2 * 512:nb % 2 * 512 + 512],
                                           start=(step == 0), stop=(step == len(PASSES) - 1))
                        mm.then_inc(prod, 1)
                for i in range(NV):
                    free(NQK + i)
                    for step, (p_w, p_x, t) in enumerate(PASSES):
                        mm = pe.matmul(pq[:, (NQK + i) % 4, 0:C], x_parts[p_x][:, t, i // 8, i % 8 * P:(i % 8 + 1) * P],
                                       wr[:, p_w, t, 2 * C:3 * C], start=(step == 0), stop=(step == len(PASSES) - 1))
                    mm.then_inc(prod, 1)
        s.clear()


def bias_tables(nc, tkq, qs, ks, us, ws):
    PER = 4
    with Scope(nc) as s:
        qk = s.sb("qk", [KP, 2, 2, B, HH, WW])
        tab = s.sb("tab", [HD, 2, 2, SPAN, SPAN])
        ext = s.sb("ext", [HD, 2, 2, SPAN, EXT])
        win = s.sb("win", [KP, 2, WW, P])
        st = [s.sb(f"bst{i}", [P, B * HH, WW]) for i in range(4)]
        win_dve = s.sem("win_dve")
        win_act = s.sem("win_act")
        pb = s.ps("pb", [P, 4, 4, P])
        qk_in = [s.sem(f"qk_in{i}") for i in range(2)]
        tab_in = [s.sem(f"tab_in{i}") for i in range(2)]
        extended = s.sem("extended")
        prod = s.sem("bprod")
        copied_act = s.sem("bcopied_act")
        copied_dve = s.sem("bcopied_dve")
        out = [s.sem(f"bout{i}") for i in range(4)]

        with nc.Block() as block:
            @block.vector
            def _(dve):
                dve.memset(qk[:].rearrange("p s a b y x -> p (s a b y x)"), 0.0)
                dve.memset(win[:].rearrange("p a x e -> p (a x e)"), 0.0)

        lo = WW - 1 - MAXD
        HU = 2 * NCH
        UNITS = [(which, c) for _ in range(PER) for c in range(NCH) for which in range(2)]

        def stores(which, c):
            return CH_ROWS[c] if which else 1

        def stored_before(u):
            return sum(stores(*UNITS[v]) for v in range(u % 4, u, 4))

        def window_of(u):
            which, c = UNITS[u]
            rows = CH_ROWS[c]
            src = ext[:, u // HU % 2, which, c * 4:c * 4 + rows, 0:WW]
            src = bass.AP(tensor=src.tensor, offset=src.offset, ap=[list(src.ap[0]), [1, WW], [EXT, rows], [1, WW]])
            return win[0:HD, u % 2, :, 0:rows * WW].rearrange("d x (r e) -> d x r e", r=rows), src

        def windows(eng, u, part):
            if u % HU == 0:
                eng.wait_ge(extended, 6 * (u // HU + 1))
            if u >= 2:
                eng.wait_ge(prod, (u - 1) * 8)
            dst, src = window_of(u)
            if part == "dve":
                eng.tensor_copy(dst[:, 0:DVE_COLS], src[:, 0:DVE_COLS]).then_inc(win_dve, 1)
            else:
                eng.activation(dst[:, DVE_COLS:WW], src[:, DVE_COLS:WW], ACT.Copy).then_inc(win_act, 1)

        DVE_COLS = 20

        def evac(eng, odd):
            for u, (which, c) in enumerate(UNITS):
                if odd and u % HU == HU // 2 and u // HU + 1 < PER:
                    extend(eng, u // HU + 1)
                if u == 0:
                    windows(eng, 0, "dve" if odd else "act")
                if u + 1 < len(UNITS):
                    windows(eng, u + 1, "dve" if odd else "act")
                n = CH_ROWS[c] * 32
                for q in range(odd, 8, 2):
                    eng.wait_ge(prod, u * 8 + q + 1)
                    if u >= 4:
                        eng.wait_ge(out[u % 4], 16 * stored_before(u))
                    dst = st[u % 4][0:n, :, q * 4:(q + 1) * 4].rearrange("p t x -> p x t")
                    src = pb[0:n, (u * 8 + q) % 4]
                    if odd:
                        eng.tensor_copy(dst, src).then_inc(copied_dve, 1)
                    else:
                        eng.activation(dst, src, ACT.Copy).then_inc(copied_act, 1)

        def extend(dve, i):
            k = i % 2
            dve.wait_ge(tab_in[k], 16 * (i // 2 + 1))
            for a, fac in ((0, 1.0), (1, SCALE)):
                dve.tensor_scalar(ext[0:HD, k, a, :, lo:lo + SPAN], tab[:, k, a], fac, None, ALU.mult).then_inc(extended, 1)
                dve.tensor_scalar(ext[0:HD, k, a, :, 0:lo], tab[:, k, a, :, 0:1].broadcast_to([HD, SPAN, lo]),
                                  fac, None, ALU.mult).then_inc(extended, 1)
                dve.tensor_scalar(ext[0:HD, k, a, :, lo + SPAN:EXT],
                                  tab[:, k, a, :, SPAN - 1:SPAN].broadcast_to([HD, SPAN, EXT - lo - SPAN]),
                                  fac, None, ALU.mult).then_inc(extended, 1)

        with nc.Fori(0, HEADS // PER) as turn:
            with nc.Block() as block:
                @block.sync
                def _(sp):
                    def load(i):
                        h, k = turn * PER + i, i % 2
                        if i >= 2:
                            sp.wait_ge(extended, 6 * (i - 1))
                            sp.wait_ge(prod, (i - 1) * HU * 8)
                        sp.dma_start(tab[:, k], tkq[bass.ds(h, 1)].rearrange("h d a r e -> (h d) a r e")).then_inc(tab_in[k], 16)
                        for which, src in ((0, qs), (1, ks)):
                            sp.dma_start(qk[0:HD, k, which].rearrange("d b y x -> d (b y x)"),
                                         src[bass.ds(h, 1)].rearrange("h d n -> (h d) n")).then_inc(qk_in[k], 16)

                    load(0)
                    for u, (which, c) in enumerate(UNITS):
                        if u % HU == 0 and u // HU + 1 < PER:
                            load(u // HU + 1)
                        h = turn * PER + u // HU
                        rows = CH_ROWS[c]
                        sp.wait_ge(copied_act, 4 * (u + 1))
                        sp.wait_ge(copied_dve, 4 * (u + 1))
                        if which == 0:
                            sp.dma_start(us[bass.ds(h, 1), :, 0:rows * 32, c, :].rearrange("h g p f -> p (h g) f"),
                                         st[u % 4][0:rows * 32].rearrange("p (g f) x -> p g (f x)", g=8)).then_inc(out[u % 4], 16)
                        else:
                            for r in range(rows):
                                sp.dma_start(ws[bass.ds(h, 1), :, :, c * 4 + r, :].rearrange("h b x f -> x (h b) f"),
                                             st[u % 4][r * 32:(r + 1) * 32].rearrange("p (b y) x -> p b (y x)", b=B)).then_inc(out[u % 4], 16)
                    for i in range(4):
                        sp.wait_ge(out[i], 16 * stored_before(len(UNITS) + i))

                @block.vector
                def _(dve):
                    extend(dve, 0)
                    evac(dve, 1)

                @block.scalar
                def _(act):
                    evac(act, 0)

                @block.tensor
                def _(pe):
                    for u, (which, c) in enumerate(UNITS):
                        n = CH_ROWS[c] * 32
                        if u % HU == 0:
                            pe.wait_ge(qk_in[u // HU % 2], 32 * (u // HU // 2 + 1))
                        pe.wait_ge(win_dve, u + 1)
                        pe.wait_ge(win_act, u + 1)
                        for q in range(8):
                            j = u * 8 + q
                            if j >= 4:
                                pe.wait_ge(copied_dve if j % 2 else copied_act, (j - 4) // 2 + 1)
                            for i in range(4):
                                x = q * 4 + i
                                mov = qk[:, u // HU % 2, which, :, :, x]
                                if which == 0:
                                    mov = mov.rearrange("d b y -> d y b")
                                mm = pe.matmul(pb[0:n, j % 4, i, :], win[:, u % 2, WW - 1 - x, 0:n], mov, start=True, stop=True)
                            mm.then_inc(prod, 1)
            s.clear()


def attention(nc, ident, qs, ks, vs, us, ws, tve, os_):
    GR = 4
    NG = HH // GR
    HALF = HH // 2
    PADR = MAXD
    PRB = 3
    with Scope(nc) as s:
        kk = s.sb("kk", [KP, B, N])
        qg = s.sb("qg", [KP, 2, B, GR * WW])
        ug = s.sb("ug", [P, 2, NCH, GR * P])
        wt = s.sb("wt", [P, SPAN * HH, WW])
        vh = s.sb("vh", [P, T // P, HD])
        tvx = s.sb("tvx", [P, NCH, WW, HD])
        pr = s.sb("pr", [P, PRB * (HH + PADR) + PADR, WW])
        edge_lo = s.sb("edge_lo", [P, 2, 4, WW])
        edge_hi = s.sb("edge_hi", [P, 2, 3, WW])
        pt = s.sb("pt", [P, 8, GR, P])
        rt = s.sb("rt", [P, NCH, HALF, P])
        oh = s.sb("oh", [HD, B, HALF, WW])
        pick4 = s.sb("pick4", [P, 12, WW])
        pick3 = s.sb("pick3", [P, 12, WW])
        uf = s.sb("uf", [P, 2, GR, 2, WW])
        nmax = s.sb("nmax", [P, 2, 3])
        rsum = s.sb("rsum", [P, 2])
        rinv = s.sb("rinv", [P, 2])
        ps = s.ps("ps_s", [P, 2, 2, 512])
        ptp = s.ps("ptp", [P, 2, 4, P])
        rtp = s.ps("rtp", [P, 4, P])
        po = s.ps("po", [P, 512])

        zeroed = s.sem("zeroed")
        v_in, tv_in = s.sem("v_in"), s.sem("tv_in")
        EARLY = [((1, SPAN), (0, 8), 14), ((1, SPAN), (8, 16), 22), ((SPAN - 1, SPAN), (16, HH), 25)]
        LATE = [((0, 1), (0, HH), MAXD), ((1, SPAN - 1), (16, 24), 10), ((1, SPAN - 1), (24, HH), 18)]
        late_in = [s.sem(f"late_in{i}") for i in range(len(LATE))]
        next_in = s.sem("next_in")
        grp_in = [s.sem(f"grp_in{i}") for i in range(2)]
        scored = s.sem("scored")
        biased = s.sem("biased")
        far_added = s.sem("far_added")
        far_turned = s.sem("far_turned")
        bias_step = s.sem("bias_step")
        exped = s.sem("exped")
        norm_step = s.sem("norm_step")
        normed = s.sem("normed2")
        turned = s.sem("turned")
        turned_rel = s.sem("turned_rel")
        pt_copied = s.sem("pt_copied")
        rt_copied = s.sem("rt_copied")
        vprod = s.sem("vprod")
        o_step = s.sem("o_step")
        o_out = s.sem("o_out")

        def rows_of(y, a, b):
            r = y % PRB * (HH + PADR)
            return pr[:, r + a:r + b, :]

        def spans(y):
            out = [(max(0, y - MAXD), min(HH, y + MAXD + 1), False)]
            if y > MAXD:
                out.insert(0, (0, y - MAXD, True))
            if y + MAXD + 1 < HH:
                out.append((y + MAXD + 1, HH, True))
            return out

        def far_ready(g):
            return g + 1 + (2 if g - 1 > HALF // GR else 0)

        NSP = [len(spans(y)) for y in range(HH)]

        def load_table(sp, h, part, done):
            (a0, a1), (y0, y1), _ = part
            dst = wt[:].rearrange("p (a y) x -> p a (y x)", a=SPAN)[:, a0:a1, y0 * WW:y1 * WW]
            sp.dma_start(dst, ws[bass.ds(h, 1)].rearrange("h b x a f -> (h b x) a f")[:, a0:a1, y0 * WW:y1 * WW]
                         ).then_inc(done, 16)

        def load_keys(sp, h, done):
            sp.dma_start(kk[0:HD].rearrange("d b n -> d (b n)"),
                         ks[bass.ds(h, 1)].rearrange("h d n -> (h d) n")).then_inc(done, 16)

        def load_group(sp, h, g, done):
            sp.dma_start(qg[0:HD, g % 2], qs[bass.ds(h, 1)].rearrange("h d (b n) -> (h d) b n", b=B)[
                :, :, g * GR * WW:(g + 1) * GR * WW]).then_inc(done, 16)
            sp.dma_start(ug[:, g % 2, 0:3], us[bass.ds(h, 1), g, :, 0:3, :].rearrange("h p c f -> (h p) c f")).then_inc(done, 16)
            sp.dma_start(ug[0:96, g % 2, 3], us[bass.ds(h, 1), g, 0:96, 3, :].rearrange("h p f -> (h p) f")).then_inc(done, 16)

        NEXT_DMAS = len(EARLY) + 4
        with nc.Block() as block:
            @block.sync
            def _(sp):
                for part in EARLY:
                    load_table(sp, 0, part, next_in)
                sp.wait_ge(zeroed, 2)
                load_keys(sp, 0, next_in)
                load_group(sp, 0, 0, next_in)
                sp.wait_ge(next_in, 16 * NEXT_DMAS)

            @block.vector
            def _(dve):
                dve.memset(kk[:].rearrange("p b n -> p (b n)"), 0.0).then_inc(zeroed, 1)
                dve.memset(qg[:].rearrange("p a b n -> p (a b n)"), 0.0).then_inc(zeroed, 1)
                dve.memset(pr[:].rearrange("p y x -> p (y x)"), 0.0)
                dve.memset(ug[96:P, :, 3, :], 0.0)
                dve.memset(rt[96:P, 3].rearrange("p y n -> p (y n)"), 0.0)
                dve.memset(tvx[96:P, 3].rearrange("p x d -> p (x d)"), 0.0)
                for pick, rows in ((pick4, 4), (pick3, 3)):
                    dve.memset(pick[:, 0:4, :], 0.0)
                    dve.memset(pick[:, 4 + rows:12, :], 0.0)
                    dve.tensor_copy(pick[:, 4:4 + rows, :], ident[:, 0:rows * 32].rearrange("p (r x) -> p r x", x=WW))
        s.clear()

        def head(h, last):
            with nc.Block() as block:
                @block.sync
                def _(sp):
                    load_table(sp, h, LATE[0], late_in[0])
                    load_group(sp, h, 1, grp_in[1])
                    sp.dma_start(vh[:], vs[:, :, bass.ds(h * HD, HD)]).then_inc(v_in, 16)
                    load_table(sp, h, LATE[1], late_in[1])
                    load_table(sp, h, LATE[2], late_in[2])
                    for c in range(NCH):
                        for r in range(CH_ROWS[c]):
                            src = tve[bass.ds(h, 1), c * 4 + r].rearrange("h e d -> (h e) d")
                            sp.dma_start(tvx[r * 32:(r + 1) * 32, c], skewed(src)).then_inc(tv_in, 16)

                    def store(half):
                        sp.wait_ge(o_step, 2 + (half + 1) * (NG // 2 + 2))
                        sp.dma_start(os_[bass.ds(h * HD, HD)].rearrange("c (b n) -> c b n", b=B)[
                            :, :, half * HALF * WW:(half + 1) * HALF * WW],
                            oh[:].rearrange("d b y x -> d b (y x)")).then_inc(o_out, 16)

                    def early(i):
                        if not last:
                            sp.wait_ge(biased, EARLY[i][2] + 1)
                            load_table(sp, h + 1, EARLY[i], next_in)

                    for g in range(2, NG):
                        if g == 5:
                            early(0)
                        if g == HALF // GR + 2:
                            store(0)
                        if g == NG - 1:
                            early(1)
                        sp.wait_ge(scored, GR * (g - 1))
                        load_group(sp, h, g, grp_in[g % 2])
                    early(2)
                    if not last:
                        sp.wait_ge(scored, GR * (NG - 1))
                        load_group(sp, h + 1, 0, next_in)
                        sp.wait_ge(scored, HH)
                        load_keys(sp, h + 1, next_in)
                    store(1)
                    sp.wait_ge(o_out, 32)
                    if not last:
                        sp.wait_ge(next_in, 16 * NEXT_DMAS)

                @block.tensor
                def _(pe):
                    def scores(y):
                        g = y // GR
                        if y % GR == 0 and g >= 1:
                            pe.wait_ge(grp_in[g % 2], 48 * ((g + 1) // 2))
                        if y >= 2:
                            pe.wait_ge(biased, y - 1)
                        for half in range(2):
                            for b in range(B):
                                pe.matmul(ps[b * 32:(b + 1) * 32, y % 2, half, :],
                                          qg[:, g % 2, b, y % GR * WW:(y % GR + 1) * WW],
                                          kk[:, b, half * 512:(half + 1) * 512],
                                          start=True, stop=True, skip_group_check=True)
                        for c in range(NCH):
                            first = y - MAXD + 4 * c
                            pick = pick4 if CH_ROWS[c] == 4 else pick3
                            for half in range(2):
                                r0, r1 = max(first, half * HALF), min(first + CH_ROWS[c], (half + 1) * HALF)
                                if r0 >= r1:
                                    continue
                                base = min(max(first, half * HALF), (half + 1) * HALF - 4)
                                mm = pe.matmul(ps[:, y % 2, half, (base - half * HALF) * WW:(base - half * HALF + 4) * WW],
                                               ug[:, g % 2, c, y % GR * P:(y % GR + 1) * P],
                                               pick[:, 4 + base - first:8 + base - first, :],
                                               start=False, stop=True, skip_group_check=True)
                        mm.then_inc(scored, 1)

                    def turn(y):
                        pe.wait_ge(normed, y + 1)
                        for i in range(2):
                            if y >= 1:
                                pe.wait_ge(pt_copied, 2 * y - 1 + i)
                            for k in range(4):
                                r0 = PADR + (i * 4 + k) * 4
                                mm = pe.matmul(ptp[:, i, k, :], rows_of(y, r0, r0 + 4), ident[:], start=True,
                                               stop=True, is_transpose=True)
                            mm.then_inc(turned, 1)
                        if y >= 1:
                            pe.wait_ge(rt_copied, y)
                        for c, rows in enumerate((edge_lo[:, y % 2], rows_of(y, y + 4, y + 8),
                                                  rows_of(y, y + 8, y + 12), edge_hi[:, y % 2])):
                            n = CH_ROWS[c] * 32
                            mm = pe.matmul(rtp[0:n, c, :], rows, ident[:], start=True, stop=True, is_transpose=True)
                        mm.then_inc(turned_rel, 1)

                    def free(n):
                        pe.wait_ge(o_step, n)

                    def turn_far(g):
                        if g >= 1:
                            pe.wait_ge(grp_in[g % 2], 48 * ((g + 1) // 2))
                        for far, (p0, c) in enumerate(((0, 0), (64, 3))):
                            if far:
                                mm.then_inc(far_turned, 1)
                                pe.wait_ge(far_turned, g + 1)
                            for i in range(GR):
                                col = 256 + (i * 2 + far) * WW
                                mm = pe.matmul(po[:, col:col + WW], ug[p0:p0 + WW, g % 2, c, i * P:(i + 1) * P],
                                               ident[p0:p0 + WW, p0:p0 + WW], start=True, stop=True, is_transpose=True)
                        return mm

                    def values(g, n, far=False):
                        pe.wait_ge(pt_copied, 2 * GR * (g + 1))
                        if g == 0:
                            pe.wait_ge(v_in, 16)
                        free(n)
                        for pair in range(B // 2):
                            for k in range(8):
                                for odd in range(2):
                                    b = 2 * pair + odd
                                    mm = pe.matmul(po[odd * 64:odd * 64 + HD, pair * P:(pair + 1) * P], vh[:, b * 8 + k, :],
                                                   pt[:, k, :, b * 32:(b + 1) * 32], start=(k == 0), stop=(k == 7))
                        if far:
                            mm = turn_far(g + 2)
                        mm.then_inc(vprod, 1)

                    def table_values(half, n):
                        pe.wait_ge(rt_copied, HALF * (half + 1))
                        if half == 0:
                            pe.wait_ge(tv_in, 16 * SPAN)
                        for q in range(2):
                            free(n + q)
                            for i in range(8):
                                for c in range(NCH):
                                    for odd in range(2):
                                        x = q * 16 + 2 * i + odd
                                        mov = rt[:, c].rearrange("p y (b x) -> p y b x", b=B)[:, :, :, x]
                                        mm = pe.matmul(po[odd * 64:odd * 64 + HD, i * 64:(i + 1) * 64],
                                                       tvx[:, c, WW - 1 - x, :], mov,
                                                       start=(c == 0), stop=(c == NCH - 1))
                            mm.then_inc(vprod, 1)

                    turn_far(0).then_inc(vprod, 1)
                    n = 1
                    for y in range(HH + 2):
                        if y < HH:
                            scores(y)
                        t = y - 2
                        if t == 0:
                            free(n)
                            turn_far(1).then_inc(vprod, 1)
                            n += 1
                        elif t > 0 and t % GR == 0:
                            values(t // GR - 1, n, t // GR + 1 < NG)
                            n += 1
                        if t == HALF:
                            table_values(0, n)
                            n += 2
                        if t >= 0:
                            turn(t)
                    values(NG - 1, n)
                    table_values(1, n + 1)

                @block.gpsimd
                def _(pool):
                    for y in range(HH):
                        g = y // GR
                        if y % GR == 0:
                            pool.wait_ge(o_step, far_ready(g))
                        if y == LATE[0][2] + 1:
                            pool.wait_ge(late_in[0], 16)
                        if y >= PRB:
                            pool.wait_ge(turned_rel, y - PRB + 1)
                        far = [sp for sp in spans(y) if sp[2]]
                        for i, (a, b, _) in enumerate(far):
                            row = 0 if a == 0 and y > MAXD else SPAN - 1
                            ins = pool.tensor_tensor(
                                rows_of(y, PADR + a, PADR + b), wt[:, row * HH + a:row * HH + b, :],
                                uf[:, g % 2, y % GR, 1 if row else 0, :].rearrange("p (o x) -> p o x", o=1).broadcast_to([P, b - a, WW]),
                                ALU.add)
                        ins.then_inc(far_added, 1)

                @block.vector
                def _(dve):
                    def bias(y):
                        dve.wait_ge(scored, y + 1)
                        if y >= PRB:
                            dve.wait_ge(turned_rel, y - PRB + 1)
                        for i, (_, _, tile) in enumerate(LATE):
                            if y == tile:
                                dve.wait_ge(late_in[i], 16)
                        dve.wait_ge(far_added, y + 1)
                        for i, (a, b, far) in enumerate(spans(y)):
                            if far:
                                tabl = rows_of(y, PADR + a, PADR + b)
                            else:
                                r0 = (a - y + MAXD) * HH + a
                                tabl = wt[:, r0:r0 + (b - a - 1) * (HH + 1) + 1:HH + 1, :]
                            if i:
                                dve.wait_ge(bias_step, sum(k - 1 for k in NSP[:y]) + i)
                            ins = dve.tensor_tensor_reduce(
                                rows_of(y, PADR + a, PADR + b),
                                ps[:, y % 2].rearrange("p a f -> p (a f)")[:, a * 32:b * 32].rearrange("p (y x) -> p y x", x=WW),
                                tabl, -1.0, nmax[:, y % 2, i - 1:i] if i else BIG, ALU.add, ALU.min,
                                nmax[:, y % 2, i:i + 1])
                            ins.then_inc(biased if i == NSP[y] - 1 else bias_step, 1)

                    def normalise(y):
                        dve.wait_ge(exped, y + 1)
                        dve.reciprocal(rinv[:, y % 2:y % 2 + 1], rsum[:, y % 2:y % 2 + 1]).then_inc(norm_step, 1)
                        dve.wait_ge(norm_step, 2 * y + 1)
                        dve.tensor_scalar(rows_of(y, PADR, PADR + HH), rows_of(y, PADR, PADR + HH),
                                          rinv[:, y % 2:y % 2 + 1], None, ALU.mult).then_inc(norm_step, 1)
                        dve.wait_ge(norm_step, 2 * y + 2)
                        if y >= 2:
                            dve.wait_ge(turned_rel, y - 1)
                        dve.tensor_reduce(edge_lo[:, y % 2, 0, :], rows_of(y, min(y, PADR), y + 1).rearrange("p y x -> p x y"),
                                          AX_X, ALU.add)
                        dve.tensor_copy(edge_lo[:, y % 2, 1:4, :], rows_of(y, y + 1, y + 4))
                        dve.tensor_reduce(edge_hi[:, y % 2, 2, :],
                                          rows_of(y, y + 2 * PADR, max(y + 2 * PADR + 1, HH + PADR)).rearrange("p y x -> p x y"),
                                          AX_X, ALU.add)
                        dve.tensor_copy(edge_hi[:, y % 2, 0:2, :], rows_of(y, y + 12, y + 14)).then_inc(normed, 1)

                    def copy_far(g):
                        return dve.tensor_copy(uf[:, g % 2], po[:, 256:512].rearrange("p (i f x) -> p i f x", i=GR, f=2))

                    def out_values(g, n, far=False):
                        dve.wait_ge(vprod, n + 1)
                        if g == NG // 2:
                            dve.wait_ge(o_out, 16)
                        y0 = g * GR % HALF
                        for odd in range(2):
                            ins = dve.tensor_copy(oh[:, odd:B:2, y0:y0 + GR, :],
                                                  po[odd * 64:odd * 64 + HD, 0:2 * P].rearrange("d (b y x) -> d b y x", b=2, y=GR))
                        if far:
                            ins = copy_far(g + 2)
                        ins.then_inc(o_step, 1)

                    def out_table(n):
                        for q in range(2):
                            dve.wait_ge(vprod, n + q + 1)
                            dve.wait_ge(o_step, n + q)
                            for odd in range(2):
                                o = oh[:, :, :, q * 16 + odd:(q + 1) * 16:2].rearrange("d b y x -> d x y b")
                                ins = dve.tensor_tensor(o, po[odd * 64:odd * 64 + HD].rearrange("d (x y b) -> d x y b", x=8, b=B), o,
                                                        ALU.add)
                            ins.then_inc(o_step, 1)

                    dve.wait_ge(vprod, 1)
                    copy_far(0).then_inc(o_step, 1)
                    n = 1
                    for y in range(HH + 2):
                        t = y - 2
                        if t == 0:
                            dve.wait_ge(vprod, n + 1)
                            copy_far(1).then_inc(o_step, 1)
                            n += 1
                        elif t > 0 and t % GR == 0:
                            out_values(t // GR - 1, n, t // GR + 1 < NG)
                            n += 1
                        if t == HALF:
                            out_table(n)
                            n += 2
                        if y < HH:
                            bias(y)
                        if 1 <= y <= HH:
                            normalise(y - 1)
                    out_values(NG - 1, n)
                    out_table(n + 1)

                @block.scalar
                def _(act):
                    for y in range(HH + 1):
                        if y < HH:
                            act.wait_ge(biased, y + 1)
                            if y >= 2:
                                act.wait_ge(norm_step, 2 * (y - 2) + 1)
                            act.activation(rows_of(y, PADR, PADR + HH), rows_of(y, PADR, PADR + HH), ACT.Exp,
                                           bias=nmax[:, y % 2, NSP[y] - 1:NSP[y]], scale=-1.0,
                                           accum_out=rsum[:, y % 2:y % 2 + 1]).then_inc(exped, 1)
                        t = y - 1
                        if t < 0:
                            continue
                        for i in range(2):
                            act.wait_ge(turned, 2 * t + i + 1)
                            act.activation(pt[:, i * 4:(i + 1) * 4, t % GR, :], ptp[:, i], ACT.Copy).then_inc(pt_copied, 1)
                        act.wait_ge(turned_rel, t + 1)
                        act.activation(rt[:, 0:3, t % HALF, :], rtp[:, 0:3], ACT.Copy)
                        act.activation(rt[0:96, 3, t % HALF, :], rtp[0:96, 3], ACT.Copy).then_inc(rt_copied, 1)
            s.clear()

        with nc.Fori(0, HEADS - 1) as h:
            head(h, False)
        head(HEADS - 1, True)


def skewed(src):
    row = list(src.ap[-2])[0]
    return bass.AP(tensor=src.tensor, offset=src.offset, ap=[[row, WW], [row, WW], [1, HD]])


def layer_norm(dve, step, n, powed, m, x, bst, bmv, rstd, xn):
    dve.bn_stats(bst, x).then_inc(step, 1)
    dve.wait_ge(step, n + 1)
    dve.bn_aggr(bmv, bst).then_inc(step, 1)
    dve.wait_ge(step, n + 2)
    dve.tensor_scalar(rstd, bmv[:, 1:2], 1e-5, None, ALU.add).then_inc(step, 1)
    dve.wait_ge(powed, m + 1)
    dve.tensor_scalar(xn, x, bmv[:, 0:1], rstd, ALU.subtract, ALU.mult).then_inc(step, 1)


def window(nc, xt, w_proj0, b_proj0, mem_t, mem, qkv_w, qkv_b, qkb, proj_w, proj_b, ident, mhalf, os_, x2):
    NT = N // P
    KEYS = MEM + WIN + P
    LOADS = 21
    with Scope(nc) as s:
        wp0 = s.sb("wp0", [P, CT, C])
        wqk = s.sb("wqk", [P, CT, 2, HEADS, 64])
        wv = s.sb("wv", [P, CT, C])
        wp1 = s.sb("wp1", [P, HEADS // 2, C])
        yt = s.sb("yt", [P, HEADS // 2, P])
        brow = s.sb("brow", [P, 3, C])
        bqk = s.sb("bqk", [HD, 2, HEADS])
        mask = s.sb("mask", [P, 2, KEYS])
        oin = s.sb("oin", [P, 2, CT, P])
        xin = s.sb("xin", [P, 2, C])
        x1 = s.sb("x1", [P, NT, C])
        xn = s.sb("xn", [P, 2, C])
        xnt = s.sb("xnt", [P, CT, N])
        bst = s.sb("bst", [P, 6])
        rstd = s.sb("rstdw", [P, 1])
        powed = s.sem("powedw")
        bmv = s.sb("bmv", [P, 2])
        qt = s.sb("qt", [KP, HEADS, N])
        kb = s.sb("kb", [KP, NT, HEADS, KEYS])
        vv = s.sb("vv", [P, NT, C])
        vp = s.sb("vp", [P, NT, C])
        pr = s.sb("pw", [P, 3, 4, KEYS])
        nmax = s.sb("nmaxw", [P, 2, 4])
        rsum = s.sb("rsumw", [P, 2, 4])
        rinv = s.sb("rinvw", [P, 2, 4])
        pt = s.sb("ptw", [P, 2, 4, P])
        pm = s.ps("pm", [P, 2, 512])
        pqk = s.ps("pqk", [P, 2, 512])
        psc = s.ps("psc", [P, 2, 2, KEYS])
        ptr = s.ps("ptr", [P, 2, 4, P])

        wl = s.sem("wl")
        zer = s.sem("zer")
        kb_zer = s.sem("kb_zer")
        msk = s.sem("msk")
        tile_in = [s.sem(f"tile_in{i}") for i in range(2)]
        xb_added = s.sem("xb_added")
        proj0 = s.sem("proj0")
        v_done = s.sem("v_done")
        y_done = s.sem("y_done")
        proj1 = s.sem("proj1")
        f_step = s.sem("f_step")
        xn_turned = s.sem("xn_turned")
        xnt_copied = s.sem("xnt_copied")
        qk_done = s.sem("qk_done")
        qk_act = s.sem("qk_act")
        qk_dve = s.sem("qk_dve")
        v_added = s.sem("v_added")
        s_done = s.sem("s_done")
        masked = s.sem("masked")
        exped = s.sem("exped_w")
        p_turned = s.sem("p_turned")
        p_copied = s.sem("p_copied")
        inverted = s.sem("inverted")
        scaled = s.sem("scaled")
        y_copied = s.sem("y_copied")
        x2_added = s.sem("x2_added")
        x2_half = s.sem("x2_half")
        x2_out = s.sem("x2_out")

        with nc.Block() as block:
            @block.vector
            def _(dve):
                dve.memset(wqk[:].rearrange("p t a h e -> p (t a h e)"), 0.0).then_inc(zer, 1)
                dve.memset(wp1[:].rearrange("p t c -> p (t c)"), 0.0).then_inc(zer, 1)
                dve.memset(vp[:].rearrange("p t c -> p (t c)"), 0.0).then_inc(zer, 1)
                dve.memset(kb[:, NT // 2:NT].rearrange("p t h k -> p (t h k)"), 0.0).then_inc(zer, 1)
                dve.wait_ge(wl, 16 * LOADS)
                dve.tensor_scalar(bqk[:, 0], bqk[:, 0], SCALE, None, ALU.mult)

            @block.gpsimd
            def _(pool):
                pool.memset(kb[:, 0:NT // 2].rearrange("p t h k -> p (t h k)"), 0.0).then_inc(kb_zer, 1)
                pool.memset(qt[:].rearrange("p h n -> p (h n)"), 0.0)
                pool.memset(yt[:].rearrange("p h n -> p (h n)"), 0.0)
                pool.memset(mask[:].rearrange("p a k -> p (a k)"), 0.0).then_inc(msk, 1)
                pool.wait_ge(msk, 1)
                pool.affine_select(out=mask[:, 0, MEM:MEM + WIN], in_=mask[:, 0, MEM:MEM + WIN], compare_op=ALU.is_ge,
                                   fill=MASKED, base=0, pattern=[[1, WIN]], channel_multiplier=-1)
                pool.memset(mask[:, 1, MEM:MEM + WIN], MASKED)
                for a in range(2):
                    m = mask[:, a, MEM + WIN:KEYS]
                    pool.affine_select(out=m, in_=m, compare_op=ALU.is_ge, fill=MASKED, base=0,
                                       pattern=[[-1, P]], channel_multiplier=1).then_inc(msk, 1)
                    pool.wait_ge(msk, 2 + 2 * a)
                    pool.affine_select(out=m, in_=m, compare_op=ALU.is_ge, fill=MASKED, base=WIN,
                                       pattern=[[1, P]], channel_multiplier=-1).then_inc(msk, 1)

            @block.sync
            def _(sp):
                def load(dst, src):
                    sp.dma_start(dst, src).then_inc(wl, 16)

                load(wp0[:], w_proj0.rearrange("(t p) n -> p t n", p=P))
                load(wv[:], qkv_w[:, 2 * C:3 * C].rearrange("(t p) n -> p t n", p=P))
                load(brow[:, 0], b_proj0.rearrange("(o n) -> o n", o=1).broadcast_to([P, C]))
                load(brow[:, 1], qkv_b[2 * C:3 * C].rearrange("(o n) -> o n", o=1).broadcast_to([P, C]))
                load(brow[:, 2], proj_b.rearrange("(o n) -> o n", o=1).broadcast_to([P, C]))
                load(bqk[:], qkb)
                sp.wait_ge(zer, 1)
                for t in range(CT):
                    for a in range(2):
                        load(wqk[:, t, a, :, 0:HD], qkv_w[t * P:(t + 1) * P, a * C:(a + 1) * C].rearrange("p (h d) -> p h d", d=HD))
                sp.wait_ge(zer, 2)
                for odd in range(2):
                    load(wp1[odd * 64:odd * 64 + HD], proj_w.rearrange("(t s p) n -> s p t n", s=2, p=HD)[odd])
                sp.wait_ge(zer, 4)
                sp.wait_ge(kb_zer, 1)
                for t in range(4):
                    load(kb[0:HD, 2 * t:2 * t + 1, :, 0:MEM].rearrange("d o h k -> d (o h) k"), mem_t)
                for t in range(2):
                    load(vp[0:MEM, 4 * t], mem)
                load(vp[0:MEM, 2], mem)
                sp.wait_ge(wl, 16 * LOADS)

        with nc.Block() as block:
            @block.scalar
            def _(act):
                for t in range(4):
                    act.activation(kb[0:HD, 2 * t + 1, :, 0:MEM], kb[0:HD, 2 * t, :, 0:MEM], ACT.Copy)
                for t, u in ((1, 0), (3, 2), (5, 4)):
                    act.activation(vp[0:MEM, t], vp[0:MEM, u], ACT.Copy)

            @block.vector
            def _(dve):
                for t, u in ((6, 4), (7, 4)):
                    dve.tensor_copy(vp[0:MEM, t], vp[0:MEM, u])

        def turn_xn(pe, t):
            pe.wait_ge(f_step, 5 * (t + 1))
            if t >= 2:
                pe.wait_ge(xnt_copied, t - 1)
            for c in range(CT):
                mm = pe.matmul(ptr[:, t % 2, c, :], xn[:, t % 2, c * P:(c + 1) * P], ident[:], start=True, stop=True,
                               is_transpose=True)
            mm.then_inc(xn_turned, 1)

        QK = [(half, a, hp) for half in range(2) for a in range(2) for hp in range(HEADS // 2)]
        EARLY = len(QK) // 2

        def project_qk(pe, j):
            half, a, hp = QK[j]
            if j >= 2:
                pe.wait_ge(qk_act, j - 1)
                pe.wait_ge(qk_dve, j - 1)
            for c in range(CT):
                mm = pe.matmul(pqk[:, j % 2, :], wqk[:, c, a, 2 * hp:2 * hp + 2].rearrange("p h e -> p (h e)"),
                               xnt[:, c, half * 512:(half + 1) * 512], start=(c == 0), stop=(c == CT - 1))
            mm.then_inc(qk_done, 1)

        def values_in(pe, t):
            pe.wait_ge(xnt_copied, t + 1)
            if t >= 2:
                pe.wait_ge(v_added, t - 1)
            for c in range(CT):
                mm = pe.matmul(pqk[:, t % 2, 0:C], xnt[:, c, t * P:(t + 1) * P], wv[:, c], start=(c == 0), stop=(c == CT - 1))
            mm.then_inc(v_done, 1)

        U = 2 * NT

        def scores(pe, u):
            t, q = divmod(u, 2)
            for k in range(4):
                if u >= 1 and k % 2 == 0:
                    pe.wait_ge(masked, 4 * (u - 1) + k + 2)
                h = q * 4 + k
                mm = pe.matmul(psc[:, k // 2, k % 2, :], qt[:, h, t * P:(t + 1) * P], kb[:, t, h, :],
                               start=True, stop=True)
                if k % 2 == 1:
                    mm.then_inc(s_done, 1)

        def turn_probs(pe, u):
            pe.wait_ge(scaled, u + 1)
            for k in range(4):
                if k % 2 == 0 and u >= 1:
                    pe.wait_ge(p_copied, 2 * (u - 1) + k // 2 + 1)
                for c in range(2):
                    mm = pe.matmul(ptr[:, k // 2, k % 2 * 2 + c, :], pr[:, u % 3, k, c * P:(c + 1) * P], ident[:],
                                   start=True, stop=True, is_transpose=True)
                if k % 2 == 1:
                    mm.then_inc(p_turned, 1)

        def value_sums(pe, u):
            t, q = divmod(u, 2)
            if q == 0 and t >= 1:
                pe.wait_ge(y_copied, 2 * t)
            for i in range(2):
                pe.wait_ge(p_copied, 2 * u + i + 1)
                pair = q * 2 + i
                for c in range(2):
                    for odd in range(2):
                        h = 2 * pair + odd
                        mm = pe.matmul(pm[odd * 64:odd * 64 + HD, 0, pair * P:(pair + 1) * P],
                                       (vp if c == 0 else vv)[:, t, h * HD:(h + 1) * HD], pt[:, i, odd * 2 + c, :],
                                       start=(c == 0), stop=(c == 1))
                mm.then_inc(y_done, 1)

        def project(pe, t):
            pe.wait_ge(y_copied, 2 * (t + 1))
            if t >= 1:
                pe.wait_ge(x2_added, t)
            for c in range(HEADS // 2):
                mm = pe.matmul(pm[:, 1, 0:C], yt[:, c], wp1[:, c], start=(c == 0), stop=(c == HEADS // 2 - 1))
            mm.then_inc(proj1, 1)

        with nc.Fori(0, B) as b:
            with nc.Block() as block:
                @block.sync
                def _(sp):
                    for t in range(NT):
                        if t >= 2:
                            sp.wait_ge(proj0, t - 1)
                            sp.wait_ge(f_step, 5 * (t - 2) + 1)
                        tok = bass.ds(b * N + t * P, P)
                        sp.dma_start(oin[:, t % 2], os_.rearrange("(c p) n -> p c n", p=P)[:, :, tok]).then_inc(tile_in[t % 2], 16)
                        sp.dma_start(xin[:, t % 2], xt[tok, :]).then_inc(tile_in[t % 2], 16)
                    for t in range(NT):
                        sp.wait_ge(x2_added, t + 1)
                        sp.dma_start(x2[bass.ds(b * N + t * P, P), :], x1[:, t]).then_inc(x2_out, 16)
                    sp.wait_ge(x2_out, 16 * NT)

                @block.gpsimd
                def _(pool):
                    def bias(t):
                        pool.wait_ge(tile_in[t % 2], 32 * (t // 2 + 1))
                        pool.tensor_tensor(xin[:, t % 2], xin[:, t % 2], brow[:, 0], ALU.add).then_inc(xb_added, 1)

                    bias(0)
                    for t in range(NT):
                        if t + 1 < NT:
                            bias(t + 1)
                        pool.wait_ge(f_step, 5 * t + 4)
                        pool.tensor_tensor(rstd[:], rstd[:], mhalf[:, 0:1], ALU.pow).then_inc(powed, 1)

                @block.tensor
                def _(pe):
                    for t in range(NT + 3):
                        if t < NT:
                            pe.wait_ge(tile_in[t % 2], 32 * (t // 2 + 1))
                            if t >= 2:
                                pe.wait_ge(f_step, 5 * (t - 2) + 1)
                            for c in range(CT):
                                mm = pe.matmul(pm[:, t % 2, 0:C], oin[:, t % 2, c], wp0[:, c], start=(c == 0), stop=(c == CT - 1))
                            mm.then_inc(proj0, 1)
                        if 0 <= t - 2 < NT:
                            turn_xn(pe, t - 2)
                        if t >= 3:
                            values_in(pe, t - 3)
                    pe.wait_ge(v_added, NT)
                    for j in range(EARLY):
                        project_qk(pe, j)
                    for u in range(U + 4):
                        t = (u - 4) // 2
                        last = u >= 4 and u % 2 == 1
                        if u in (0, EARLY):
                            pe.wait_ge(qk_act, EARLY + u)
                            pe.wait_ge(qk_dve, EARLY + u)
                        if u < U:
                            scores(pe, u)
                        if u < EARLY:
                            project_qk(pe, EARLY + u)
                        if last:
                            project(pe, t)
                        if 0 <= u - 3 < U:
                            value_sums(pe, u - 3)
                        if 0 <= u - 2 < U:
                            turn_probs(pe, u - 2)

                @block.vector
                def _(dve):
                    def add_v(t):
                        dve.wait_ge(v_done, t + 1)
                        if t + 1 < NT:
                            dve.tensor_tensor(vp[WIN:P, t + 1], pqk[WIN:P, t % 2, 0:C], brow[WIN:P, 1], ALU.add)
                        dve.tensor_tensor(vv[:, t], pqk[:, t % 2, 0:C], brow[:, 1], ALU.add).then_inc(v_added, 1)

                    n = 0
                    for t in range(NT):
                        dve.wait_ge(proj0, t + 1)
                        dve.wait_ge(xb_added, t + 1)
                        dve.tensor_tensor(x1[:, t], pm[:, t % 2, 0:C], xin[:, t % 2], ALU.add).then_inc(f_step, 1)
                        dve.wait_ge(f_step, n + 1)
                        if t >= 2:
                            dve.wait_ge(xn_turned, t - 1)
                        layer_norm(dve, f_step, n + 1, powed, t, x1[:, t], bst[:], bmv[:], rstd[:], xn[:, t % 2])
                        n += 5
                        if t >= 3:
                            add_v(t - 3)
                    for t in range(NT - 3, NT):
                        add_v(t)
                    def copy_qk(j):
                        half, a, hp = QK[j]
                        dve.wait_ge(qk_done, j + 1)
                        src = pqk[64:64 + HD, j % 2, :]
                        h = 2 * hp + 1
                        if a == 0:
                            dve.tensor_scalar(qt[0:HD, h, half * 512:(half + 1) * 512], src, SCALE, bqk[:, 0, h:h + 1],
                                              ALU.mult, ALU.add).then_inc(qk_dve, 1)
                        else:
                            s4 = src.rearrange("d (t k) -> d t k", k=P)
                            m = 4 if half == 0 else 3
                            dve.tensor_scalar(kb[0:HD, half * 4 + 1:half * 4 + 1 + m, h, MEM:MEM + WIN], s4[:, 0:m, WIN:P],
                                              bqk[:, 1, h:h + 1], None, ALU.add)
                            dve.tensor_scalar(kb[0:HD, half * 4:half * 4 + 4, h, MEM + WIN:KEYS], s4,
                                              bqk[:, 1, h:h + 1], None, ALU.add).then_inc(qk_dve, 1)

                    for j in range(EARLY):
                        copy_qk(j)

                    def divide(u):
                        dve.wait_ge(exped, 4 * (u + 1))
                        dve.reciprocal(rinv[:, u % 2], rsum[:, u % 2]).then_inc(inverted, 1)
                        dve.wait_ge(inverted, u + 1)
                        dve.tensor_tensor(pr[:, u % 3], pr[:, u % 3],
                                          rinv[:, u % 2].rearrange("p (h o) -> p h o", o=1).broadcast_to([P, 4, KEYS]),
                                          ALU.mult).then_inc(scaled, 1)

                    def residual(t):
                        dve.wait_ge(proj1, t + 1)
                        dve.tensor_tensor(x1[:, t], pm[:, 1, 0:C], x1[:, t], ALU.add).then_inc(x2_half, 1)
                        dve.wait_ge(x2_half, t + 1)
                        dve.tensor_tensor(x1[:, t], x1[:, t], brow[:, 2], ALU.add).then_inc(x2_added, 1)

                    for u in range(U + 5):
                        if u < U:
                            t, q = divmod(u, 2)
                            for k in range(4):
                                dve.wait_ge(s_done, 2 * u + k // 2 + 1)
                                if u >= 3 and k % 2 == 0:
                                    dve.wait_ge(p_turned, 2 * (u - 3) + k // 2 + 1)
                                dve.tensor_tensor_reduce(pr[:, u % 3, k, :], psc[:, k // 2, k % 2, :], mask[:, 1 if t == 0 else 0],
                                                         -1.0, BIG, ALU.add, ALU.min, nmax[:, u % 2, k:k + 1]).then_inc(masked, 1)
                        if 1 <= u <= U:
                            divide(u - 1)
                        if u < EARLY:
                            copy_qk(EARLY + u)
                        if u >= 6 and u % 2 == 0:
                            residual((u - 6) // 2)

                @block.scalar
                def _(act):
                    for t in range(NT):
                        act.wait_ge(xn_turned, t + 1)
                        act.activation(xnt[:, :, t * P:(t + 1) * P], ptr[:, t % 2, 0:CT, :], ACT.Copy).then_inc(xnt_copied, 1)
                    def copy_qk(j):
                        half, a, hp = QK[j]
                        act.wait_ge(qk_done, j + 1)
                        src = pqk[0:HD, j % 2, :]
                        h = 2 * hp
                        if a == 0:
                            act.activation(qt[0:HD, h, half * 512:(half + 1) * 512], src, ACT.Identity, scale=SCALE,
                                           bias=bqk[:, 0, h:h + 1]).then_inc(qk_act, 1)
                        else:
                            s4 = src.rearrange("d (t k) -> d t k", k=P)
                            m = 4 if half == 0 else 3
                            act.activation(kb[0:HD, half * 4 + 1:half * 4 + 1 + m, h, MEM:MEM + WIN], s4[:, 0:m, WIN:P],
                                           ACT.Identity, bias=bqk[:, 1, h:h + 1])
                            act.activation(kb[0:HD, half * 4:half * 4 + 4, h, MEM + WIN:KEYS], s4, ACT.Identity,
                                           bias=bqk[:, 1, h:h + 1]).then_inc(qk_act, 1)

                    for j in range(EARLY):
                        copy_qk(j)
                    for u in range(U + 4):
                        if u < U:
                            if u >= 2:
                                act.wait_ge(inverted, u - 1)
                            for k in range(4):
                                act.wait_ge(masked, 4 * u + k + 1)
                                act.activation(pr[:, u % 3, k, :], pr[:, u % 3, k, :], ACT.Exp, bias=nmax[:, u % 2, k:k + 1],
                                               scale=-1.0, accum_out=rsum[:, u % 2, k:k + 1]).then_inc(exped, 1)
                        if u < EARLY:
                            copy_qk(EARLY + u)
                        if u >= 4 and u % 2 == 0:
                            t = (u - 4) // 2
                            act.wait_ge(y_done, 4 * (t + 1))
                            if t >= 1:
                                act.wait_ge(proj1, t)
                            for odd in range(2):
                                act.activation(yt[odd * 64:odd * 64 + HD], pm[odd * 64:odd * 64 + HD, 0, :].rearrange(
                                    "p (c n) -> p c n", n=P), ACT.Copy).then_inc(y_copied, 1)
                        if 0 <= u - 2 < U:
                            for i in range(2):
                                act.wait_ge(p_turned, 2 * (u - 2) + i + 1)
                                if u >= 3:
                                    act.wait_ge(y_done, 2 * (u - 3) + i + 1)
                                act.activation(pt[:, i], ptr[:, i], ACT.Copy).then_inc(p_copied, 1)
            s.clear()


def experts(nc, x2, gate_w, gate_b, w1, b1, w2, b2, ident, mhalf, xns, out):
    TB = 512
    TT = TB // P
    NB = T // TB
    NTT = T // P
    HI, LO = 0, 1
    PASSES = ((HI, HI), (HI, LO), (LO, HI))
    RING = 3
    LN_STEPS = 3 * TT + 1
    with Scope(nc) as s:
        acc = s.sb("acc", [P, NTT, C])
        xb = s.sb("xb", [P, 2, 2, CT, TB], F32R)
        wr = s.sb("wr", [P, 2, HT, 2 * CT, P], F32R)
        stage = s.sb("stage", [P, RING, 2 * CT, P])
        hs = s.sb("hs", [P, RING, TB])
        hr = s.sb("hr", [P, 2, RING, TB], F32R)
        xn = s.sb("xne", [P, 2, C])
        xs = s.sb("xs", [P, 2, CT, TB])
        gw = s.sb("gw", [P, CT, EXPERTS])
        gb = s.sb("gb", [P, EXPERTS])
        b1e = s.sb("b1e", [P, HT])
        b2e = s.sb("b2e", [P, C])
        tri = s.sb("tri", [P, EXPERTS, EXPERTS])
        bst = s.sb("bste", [P, TT, 6])
        bmv = s.sb("bmve", [P, TT, 2])
        rstd = s.sb("rstde", [P, TT])
        g = s.sb("g", [P, NTT, EXPERTS])
        ge = s.sb("ge", [P, NTT])
        red = s.sb("red", [P, NTT])
        lt = s.sb("lt", [P, NTT, EXPERTS, EXPERTS])
        eq = s.sb("eq", [P, NTT, EXPERTS, EXPERTS])
        pu = s.ps("pu", [P, RING, 512])
        pd = s.ps("pd", [P, TT, 512])
        pgt = s.ps("pgt", [P, 512])

        wl = s.sem("wle")
        tri_step = s.sem("tri_step")
        x_in = [s.sem(f"x_in_e{i}") for i in range(NB)]
        ln = s.sem("ln")
        powed = s.sem("powede")
        turned = s.sem("turned_e")
        copied = s.sem("copied_e")
        g_done = s.sem("g_done")
        g_step = s.sem("g_step")
        g_exp = s.sem("g_exp")
        xn_out = [s.sem(f"xn_out{i}") for i in range(2)]
        w_in = [s.sem(f"w_in_e{i}") for i in range(RING)]
        w_hi = s.sem("w_hi")
        w_lo = s.sem("w_lo")
        xs_in = [s.sem(f"xs_in{i}") for i in range(2)]
        x_hi = s.sem("x_hi")
        x_lo = s.sem("x_lo")
        first_lo = s.sem("first_lo")
        next_in = s.sem("next_in_e")
        b_in = s.sem("b_in")
        up = s.sem("up")
        gelu = s.sem("gelu")
        h_hi = s.sem("h_hi")
        h_lo = s.sem("h_lo")
        down = s.sem("down")
        ge_done = s.sem("ge_done")
        summed = s.sem("summed")
        o_out = s.sem("o_out_e")

        def load_weights(sp, e, m, done):
            one = bass.ds(e, 1)
            sp.dma_start(stage[:, m % RING, 0:CT], w1[one].rearrange("e (t p) n -> p (e t) n", p=P)[
                :, :, m * P:(m + 1) * P]).then_inc(done, 16)
            sp.dma_start(stage[:, m % RING, CT:2 * CT].rearrange("p t n -> p (t n)"),
                         w2[one].rearrange("e k n -> (e k) n")[m * P:(m + 1) * P, :]).then_inc(done, 16)

        def load_tokens(sp, i, done):
            sp.dma_start(xs[:, i % 2].rearrange("p t n -> p (t n)"), xns[i]).then_inc(done, 16)

        NEXT_DMAS = 2 * RING + 2

        with nc.Block() as block:
            @block.sync
            def _(sp):
                sp.dma_start(gw[:], gate_w.rearrange("(t p) n -> p t n", p=P)).then_inc(wl, 16)
                sp.dma_start(gb[:], gate_b.rearrange("(o n) -> o n", o=1).broadcast_to([P, EXPERTS])).then_inc(wl, 16)
                for i in range(NB):
                    sp.dma_start(acc[:, i * TT:(i + 1) * TT], x2[i * TB:(i + 1) * TB, :].rearrange("(t p) c -> p t c", p=P)
                                 ).then_inc(x_in[i], 16)
                for i in range(NB):
                    sp.wait_ge(copied, TT * (i + 1))
                    sp.dma_start(xns[i], xs[:, i % 2].rearrange("p t n -> p (t n)")).then_inc(xn_out[i % 2], 16)
                for m in range(RING):
                    load_weights(sp, 0, m, next_in)
                for i in range(2):
                    sp.wait_ge(xn_out[i], 16 * NB // 2)
                sp.wait_ge(g_done, NTT)
                for i in range(2):
                    load_tokens(sp, i, next_in)
                sp.wait_ge(next_in, 16 * NEXT_DMAS)

            @block.gpsimd
            def _(pool):
                pool.memset(tri[:].rearrange("p j e -> p (j e)"), 1.0).then_inc(tri_step, 1)
                pool.wait_ge(tri_step, 1)
                pool.affine_select(out=tri[:], in_=tri[:], compare_op=ALU.is_gt, fill=0.0, base=0,
                                   pattern=[[-1, EXPERTS], [1, EXPERTS]], channel_multiplier=0).then_inc(tri_step, 1)
                for i in range(NB):
                    pool.wait_ge(ln, LN_STEPS * i + 2 * TT + 1)
                    pool.tensor_tensor(rstd[:], rstd[:], mhalf[:, 0:TT], ALU.pow).then_inc(powed, 1)

            @block.tensor
            def _(pe):
                def gates(t):
                    pe.wait_ge(copied, t + 1)
                    for c in range(CT):
                        mm = pe.matmul(pgt[:, t * EXPERTS:(t + 1) * EXPERTS],
                                       xs[:, t // TT % 2, c, t % TT * P:(t % TT + 1) * P], gw[:, c],
                                       start=(c == 0), stop=(c == CT - 1), skip_group_check=True)
                    mm.then_inc(g_done, 1)

                pe.wait_ge(wl, 32)
                for t in range(NTT):
                    i, k = divmod(t, TT)
                    pe.wait_ge(ln, LN_STEPS * i + 2 * TT + 1 + k + 1)
                    if t >= 2:
                        pe.wait_ge(copied, t - 1)
                    for c in range(CT):
                        mm = pe.matmul(pd[:, t % 2, c * P:(c + 1) * P], xn[:, t % 2, c * P:(c + 1) * P], ident[:],
                                       start=True, stop=True, is_transpose=True)
                    mm.then_inc(turned, 1)
                    if t >= 1:
                        gates(t - 1)
                gates(NTT - 1)

            @block.scalar
            def _(act):
                for t in range(NTT):
                    i, k = divmod(t, TT)
                    src = pd[:, t % 2, 0:C].rearrange("p (c n) -> p c n", c=CT)
                    act.wait_ge(turned, t + 1)
                    if i >= 2 and k == 0:
                        act.wait_ge(xn_out[i % 2], 16 * (i // 2))
                        act.wait_ge(g_done, TT * (i - 1))
                    act.activation(xs[:, i % 2, :, k * P:(k + 1) * P], src, ACT.Copy).then_inc(copied, 1)
                act.wait_ge(g_step, 3)
                act.activation(g[:], g[:], ACT.Exp).then_inc(g_exp, 1)

            @block.vector
            def _(dve):
                for i in range(NB):
                    n = LN_STEPS * i
                    dve.wait_ge(x_in[i], 16)
                    for k in range(TT):
                        dve.bn_stats(bst[:, k], acc[:, i * TT + k]).then_inc(ln, 1)
                    for k in range(TT):
                        dve.wait_ge(ln, n + k + 1)
                        if k == 0 and i >= 1:
                            dve.wait_ge(ln, n)
                        dve.bn_aggr(bmv[:, k], bst[:, k]).then_inc(ln, 1)
                    dve.wait_ge(ln, n + 2 * TT)
                    dve.tensor_scalar(rstd[:], bmv[:, :, 1], 1e-5, None, ALU.add).then_inc(ln, 1)
                    dve.wait_ge(powed, i + 1)
                    for k in range(TT):
                        t = i * TT + k
                        if t >= 2:
                            dve.wait_ge(turned, t - 1)
                        dve.tensor_scalar(xn[:, t % 2], acc[:, t], bmv[:, k, 0:1], rstd[:, k:k + 1],
                                          ALU.subtract, ALU.mult).then_inc(ln, 1)
                n = [0]

                def step(ins):
                    ins.then_inc(g_step, 1)
                    n[0] += 1
                    dve.wait_ge(g_step, n[0])

                def over(a, e):
                    return a.rearrange("p (t o) -> p t o", o=1).broadcast_to([P, NTT, e])

                FULL = [P, NTT, EXPERTS, EXPERTS]
                dve.wait_ge(g_done, NTT)
                scores = pgt[:, 0:NTT * EXPERTS].rearrange("p (t e) -> p t e", e=EXPERTS)
                step(dve.tensor_tensor(g[:], scores, gb[:].rearrange("p (o e) -> p o e", o=1).broadcast_to([P, NTT, EXPERTS]),
                                       ALU.add))
                step(dve.tensor_reduce(red[:], g[:], AX_X, ALU.max))
                step(dve.tensor_tensor(g[:], g[:], over(red[:], EXPERTS), ALU.subtract))
                dve.wait_ge(g_exp, 1)
                step(dve.tensor_reduce(red[:], g[:], AX_X, ALU.add))
                step(dve.reciprocal(red[:], red[:]))
                step(dve.tensor_tensor(g[:], g[:], over(red[:], EXPERTS), ALU.mult))
                for_e = g[:].rearrange("p t (o e) -> p t o e", o=1).broadcast_to(FULL)
                for_j = g[:].rearrange("p t (j o) -> p t j o", o=1).broadcast_to(FULL)
                dve.wait_ge(tri_step, 2)
                dve.tensor_tensor(lt[:], for_e, for_j, ALU.is_lt)
                step(dve.tensor_tensor(eq[:], for_e, for_j, ALU.is_equal))
                step(dve.tensor_tensor(eq[:], eq[:], tri[:].rearrange("p (o j) e -> p o j e", o=1).broadcast_to(FULL), ALU.mult))
                step(dve.tensor_tensor(lt[:], lt[:], eq[:], ALU.add))
                step(dve.tensor_reduce(eq[:, :, 0, :], lt[:].rearrange("p t j e -> p t e j"), AX_X, ALU.add))
                step(dve.scalar_tensor_tensor(out=g[:], in0=eq[:, :, 0, :], scalar=1.5, in1=g[:], op0=ALU.is_lt, op1=ALU.mult))
                step(dve.tensor_reduce(red[:], g[:], AX_X, ALU.add))
                step(dve.tensor_scalar(red[:], red[:], 1e-9, None, ALU.add))
                step(dve.reciprocal(red[:], red[:]))
                step(dve.tensor_tensor(g[:], g[:], over(red[:], EXPERTS), ALU.mult))

        NJ = NB * HT
        LAG = 2

        def expert(e, last):
            with nc.Block() as block:
                @block.sync
                def _(sp):
                    one = bass.ds(e, 1)
                    sp.dma_start(b1e[:], b1[:, one, :].rearrange("p e m -> p (e m)")).then_inc(b_in, 16)
                    sp.dma_start(b2e[:], b2[one, :].broadcast_to([P, C])).then_inc(b_in, 16)
                    for m in range(RING, HT):
                        sp.wait_ge(w_lo, m - RING + 1)
                        load_weights(sp, e, m, w_in[m % RING])
                    for i in range(2, NB):
                        sp.wait_ge(x_hi, i - 1)
                        if i == 2:
                            sp.wait_ge(first_lo, 1)
                        else:
                            sp.wait_ge(x_lo, i - 2)
                        load_tokens(sp, i, xs_in[i % 2])
                    if not last:
                        sp.wait_ge(w_lo, HT)
                        for m in range(RING):
                            load_weights(sp, e + 1, m, next_in)
                        sp.wait_ge(x_hi, NB)
                        sp.wait_ge(x_lo, NB - 1)
                        for i in range(2):
                            load_tokens(sp, i, next_in)
                        sp.wait_ge(next_in, 16 * NEXT_DMAS)
                    if last:
                        for i in range(NB):
                            sp.wait_ge(summed, 2 * TT * (i + 1))
                            sp.dma_start(out[i * TB:(i + 1) * TB, :].rearrange("(t p) c -> p t c", p=P),
                                         acc[:, i * TT:(i + 1) * TT]).then_inc(o_out, 16)
                        sp.wait_ge(o_out, 16 * NB)

                @block.gpsimd
                def _(pool):
                    def split_x(i):
                        pool.wait_ge(x_hi, i + 1)
                        pool.tensor_tensor(xb[:, i % 2, LO], xs[:, i % 2], xb[:, i % 2, HI].bitcast(F32),
                                           ALU.subtract).then_inc(x_lo, 1)

                    for m in range(HT):
                        pool.wait_ge(w_hi, m + 1)
                        pool.tensor_tensor(wr[:, LO, m], stage[:, m % RING], wr[:, HI, m].bitcast(F32),
                                           ALU.subtract).then_inc(w_lo, 1)
                    for i in range(1, NB):
                        split_x(i)

                @block.tensor
                def _(pe):
                    def first(j):
                        i, m = divmod(j, HT)
                        if m == 0:
                            pe.wait_ge(x_lo if i else first_lo, max(i, 1))
                        if i == 0:
                            pe.wait_ge(w_lo, m + 1)
                        if j >= RING:
                            pe.wait_ge(gelu, j - RING + 1)
                        n = 0
                        for a, b in PASSES:
                            for c in range(CT):
                                mm = pe.matmul(pu[:, j % RING, :], wr[:, a, m, c, :], xb[:, i % 2, b, c, :],
                                               start=(n == 0), stop=(n == 3 * CT - 1))
                                n += 1
                        mm.then_inc(up, 1)

                    def second(j):
                        i, m = divmod(j, HT)
                        pe.wait_ge(h_lo, j + 1)
                        for t in range(TT):
                            if m == 0 and i >= 1:
                                pe.wait_ge(summed, 2 * TT * (i - 1) + TT + t + 1)
                            for n, (a, b) in enumerate(PASSES):
                                mm = pe.matmul(pd[:, t, 0:C], hr[:, a, j % RING, t * P:(t + 1) * P],
                                               wr[:, b, m, CT:2 * CT, :],
                                               start=(m == 0 and n == 0), stop=(m == HT - 1 and n == 2))
                        mm.then_inc(down, 1)

                    for j in range(NJ + LAG):
                        if j < NJ:
                            first(j)
                        if j >= LAG:
                            second(j - LAG)

                @block.scalar
                def _(act):
                    act.wait_ge(b_in, 32)
                    for j in range(NJ):
                        act.wait_ge(up, j + 1)
                        if j >= RING:
                            act.wait_ge(h_lo, j - RING + 1)
                        act.activation(hs[:, j % RING], pu[:, j % RING, :], ACT.Gelu, bias=b1e[:, j % HT:j % HT + 1]
                                       ).then_inc(gelu, 1)

                @block.vector
                def _(dve):
                    def split_w(m):
                        if m >= RING:
                            dve.wait_ge(w_in[m % RING], 32 * (m // RING))
                        dve.tensor_copy(wr[:, HI, m], stage[:, m % RING]).then_inc(w_hi, 1)

                    def split_x(i):
                        if i >= 2:
                            dve.wait_ge(xs_in[i % 2], 16 * (i // 2))
                        if i >= 2:
                            dve.wait_ge(up, HT * (i - 1))
                        dve.tensor_copy(xb[:, i % 2, HI], xs[:, i % 2]).then_inc(x_hi, 1)

                    def biases(i):
                        for t in range(i * TT, (i + 1) * TT):
                            dve.scalar_tensor_tensor(out=acc[:, t], in0=b2e[:], scalar=ge[:, t:t + 1], in1=acc[:, t],
                                                     op0=ALU.mult, op1=ALU.add).then_inc(summed, 1)

                    def sums(i):
                        dve.wait_ge(down, HT * (i + 1))
                        for t in range(TT):
                            dve.wait_ge(summed, 2 * TT * i + t + 1)
                            dve.scalar_tensor_tensor(out=acc[:, i * TT + t], in0=pd[:, t, 0:C],
                                                     scalar=ge[:, i * TT + t:i * TT + t + 1],
                                                     in1=acc[:, i * TT + t], op0=ALU.mult, op1=ALU.add).then_inc(summed, 1)

                    split_w(0)
                    split_x(0)
                    dve.wait_ge(x_hi, 1)
                    dve.tensor_tensor(xb[:, 0, LO], xs[:, 0], xb[:, 0, HI].bitcast(F32), ALU.subtract).then_inc(first_lo, 1)
                    for m in range(1, RING):
                        split_w(m)
                    dve.tensor_copy(ge[:], g[:, :, bass.ds(e, 1)].rearrange("p t e -> p (t e)")).then_inc(ge_done, 1)
                    dve.wait_ge(b_in, 32)
                    dve.wait_ge(ge_done, 1)
                    for j in range(NJ + LAG):
                        if j < NJ:
                            dve.wait_ge(gelu, j + 1)
                            if j >= RING:
                                dve.wait_ge(down, j - RING + 1)
                            dve.tensor_copy(hr[:, HI, j % RING], hs[:, j % RING]).then_inc(h_hi, 1)
                            dve.wait_ge(h_hi, j + 1)
                            dve.tensor_tensor(hr[:, LO, j % RING], hs[:, j % RING], hr[:, HI, j % RING].bitcast(F32),
                                              ALU.subtract).then_inc(h_lo, 1)
                            if j + RING < HT:
                                split_w(j + RING)
                            if j % HT == 2 and j // HT + 1 < NB:
                                split_x(j // HT + 1)
                            if j % HT == HT // 2:
                                biases(j // HT)
                        if j >= LAG and (j - LAG) % HT == HT - 1:
                            sums((j - LAG) // HT)
            s.clear()

        s.clear()
        with nc.Fori(0, EXPERTS - 1) as e:
            expert(e, False)
        expert(EXPERTS - 1, True)


def build(nc, a):
    def dram(name, shape):
        return nc.dram_tensor(name, shape, F32, kind="Internal").ap()

    qs, ks = dram("qs", (HEADS, HD, T)), dram("ks", (HEADS, HD, T))
    vs = dram("vs", (P, T // P, C))
    tve = dram("tve", (HEADS, SPAN, EXT, HD))
    us = dram("us", (HEADS, 8, P, NCH, 512))
    ws = dram("ws", (HEADS, B, WW, SPAN, N))
    os_ = dram("os_", (C, T))
    x2 = dram("x2", (T, C))
    xns = dram("xns", (T // 512, P, CT * 512))
    with Scope(nc) as s:
        ident = s.sb("ident", [P, P])
        mhalf = s.sb("mhalf", [P, B])
        ident_step = s.sem("ident_step")
        with nc.Block() as block:
            @block.gpsimd
            def _(pool):
                pool.memset(mhalf[:], -0.5)
                pool.memset(ident[:], 1.0).then_inc(ident_step, 1)
                pool.wait_ge(ident_step, 1)
                pool.affine_select(out=ident[:], in_=ident[:], compare_op=ALU.is_equal, fill=0.0, base=0,
                                   pattern=[[-1, P]], channel_multiplier=1)
        norm_qkv(nc, a["x"], a["w_qkv"], a["tv"], mhalf, qs, ks, vs, tve)
        bias_tables(nc, a["tkq"], qs, ks, us, ws)
        attention(nc, ident, qs, ks, vs, us, ws, tve, os_)
        window(nc, a["xt"], a["w_proj"], a["b_proj"], a["mem_t"], a["mem"], a["qkv_w"], a["qkv_b"], a["qkb"],
               a["proj_w"], a["proj_b"], ident, mhalf, os_, x2)
        experts(nc, x2, a["gate_w"], a["gate_b"], a["w1"], a["b1"], a["w2"], a["b2"], ident, mhalf, xns, a["out"])


def kernel(**inputs):
    import numpy as np
    import concourse.bacc as bacc
    from concourse.bass_utils import run_bass_kernel_spmd

    i = {k: np.asarray(v) for k, v in inputs.items()}
    x = i["x"].reshape(B, C, N)
    tk = i["L0_conv_table_k"].reshape(HEADS, SPAN, SPAN, HD)[:, ::-1, ::-1].transpose(0, 3, 1, 2)
    tq = i["L0_conv_table_q"].reshape(HEADS, SPAN, SPAN, HD)[:, :, ::-1].transpose(0, 3, 1, 2)
    arrays = {
        "x": x,
        "xt": x.transpose(0, 2, 1).reshape(T, C),
        "w_qkv": i["L0_conv_w_qkv"], "w_proj": i["L0_conv_w_proj"], "b_proj": i["L0_conv_b_proj"],
        "tkq": np.stack([tk, tq], axis=2),
        "tv": i["L0_conv_table_v"].reshape(HEADS, SPAN, SPAN, HD)[:, ::-1, ::-1],
        "mem": i["L1_attn_mem"],
        "mem_t": i["L1_attn_mem"].reshape(MEM, HEADS, HD).transpose(2, 1, 0),
        "qkv_w": i["L1_attn_qkv_w"], "qkv_b": i["L1_attn_qkv_b"],
        "qkb": i["L1_attn_qkv_b"][:2 * C].reshape(2, HEADS, HD).transpose(2, 0, 1),
        "proj_w": i["L1_attn_proj_w"], "proj_b": i["L1_attn_proj_b"],
        "gate_w": i["L1_ffn_gate_w"], "gate_b": i["L1_ffn_gate_b"],
        "w1": i["L1_ffn_w1"], "b1": i["L1_ffn_b1"].reshape(EXPERTS, HT, P).transpose(2, 0, 1),
        "w2": i["L1_ffn_w2"], "b2": i["L1_ffn_b2"],
    }
    nc = bacc.Bacc("TRN2", target_bir_lowering=False, num_devices=1)
    given, a = {}, {}
    for name, v in arrays.items():
        given[f"in_{name}"] = np.ascontiguousarray(v)
        a[name] = nc.dram_tensor(f"in_{name}", v.shape, F32, kind="ExternalInput").ap()
    a["out"] = nc.dram_tensor("out_tokens", (T, C), F32, kind="ExternalOutput").ap()
    build(nc, a)
    r = run_bass_kernel_spmd(nc, [given], core_ids=[0])
    y = r.results[0]["out_tokens"]
    return y.reshape(B, N, C).transpose(0, 2, 1).reshape(B, C, HH, WW)
```
